# Optimizing a Trainium2 kernel written in Bass

```python
import numpy as np
import jax
import jax.numpy as jnp

def _softmax(x, axis=-1):
    return jax.nn.softmax(x, axis=axis)

def _gelu(x):
    return jax.nn.gelu(x, approximate=True)

def _silu(x):
    return jax.nn.silu(x)

def _sigmoid(x):
    return jax.nn.sigmoid(x)

def _layernorm(x, axis=-1, eps=1e-05):
    m = jnp.mean(x, axis=axis, keepdims=True)
    v = jnp.var(x, axis=axis, keepdims=True)
    return (x - m) / jnp.sqrt(v + eps)

def _scatter_add(tgt, idx, src, axis=0):
    return tgt.at[idx].add(src)

def _segment_sum(src, seg, n):
    return jax.ops.segment_sum(src, seg, n)
kernel_name = 'mk_perceiver_d1_seqx_r8_d99876'

def setup_inputs(seed: int=0):
    np.random.seed(seed)
    _w = jnp.asarray

    def _rec_inputs():
        import jax
        import jax.numpy as jnp
        _rk = jax.random.key(seed)
        x = -0.0003929 + 0.9999 * jax.random.normal(jax.random.fold_in(_rk, 1), (32, 64, 256), jnp.float32)
        _lenS = 64 - jax.random.randint(jax.random.fold_in(_rk, 7), (32,), 0, max(1, 64 // 4) + 1, jnp.int32)
        _lenS2 = 1601 - jax.random.randint(jax.random.fold_in(_rk, 8), (32,), 0, max(1, 1601 // 4) + 1, jnp.int32)
        _ctx_2048P = jax.random.normal(jax.random.fold_in(_rk, 11), (32, 16, 256), jnp.float32)
        _ctx_2048c = jax.random.dirichlet(jax.random.fold_in(_rk, 511), 0.3 * jnp.ones((16,), jnp.float32), (32, 1601))
        _ctx_2048t = jnp.einsum('bsk,bkd->bsd', _ctx_2048c, _ctx_2048P)
        _ctx_2048t = _ctx_2048t * jax.lax.rsqrt(jnp.mean(jnp.square(_ctx_2048t)) + 1e-12) * 0.953939
        ctx_2048 = -1.39393e-06 + 0.999914 * (_ctx_2048t + 0.3 * jax.random.normal(jax.random.fold_in(_rk, 611), (32, 1601, 256), jnp.float32))
        itok_BxS_0_1023 = jax.random.randint(jax.random.fold_in(_rk, 12), (32, 64), 0, 128, jnp.int32)
        return (x, ctx_2048, itok_BxS_0_1023)
    x, ctx_2048, itok_BxS_0_1023 = _rec_inputs()

    def _L0_xattn_setup():
        import jax, jax.numpy as jnp
        import numpy as np
        B, Lq, Lk = (2, 512, 128)
        Q_DIM, KV_DIM = (256, 256)
        H, HD = (16, 128)
        KVC, QC, R = (64, 96, 64)
        LOOKBACK = 8
        NEG = -1e+30

        def _rope(x, L):
            half = x.shape[-1] // 2
            inv_freq = 1.0 / 10000.0 ** (jnp.arange(half, dtype=jnp.float32) / half)
            ang = jnp.arange(L, dtype=jnp.float32)[:, None] * inv_freq
            cos, sin = (jnp.cos(ang), jnp.sin(ang))
            x1, x2 = (x[..., :half], x[..., half:])
            return jnp.concatenate([x1 * cos - x2 * sin, x1 * sin + x2 * cos], axis=-1)
        key = jax.random.key(seed)
        ks = jax.random.split(key, 11)

        def w(k, shape, fan_in):
            return jax.random.normal(k, shape, jnp.float32) / np.sqrt(fan_in).astype(np.float32)
        return {'q': jax.random.normal(ks[0], (B, Lq, Q_DIM), jnp.float32), 'kv': jax.random.normal(ks[1], (B, Lk, KV_DIM), jnp.float32), 'seg_id': jnp.sort(jax.random.randint(ks[2], (B, Lq), 0, Lk), axis=-1), 'W_kvc': w(ks[3], (KV_DIM, KVC), KV_DIM), 'W_dq': w(ks[4], (Q_DIM, QC), Q_DIM), 'W_uq': w(ks[5], (QC, H * HD), QC), 'W_qr': w(ks[6], (QC, H * R), QC), 'W_uk': w(ks[7], (KVC, H * HD), KVC), 'W_kr': w(ks[8], (KVC, R), KVC), 'W_uv': w(ks[9], (KVC, H * HD), KVC), 'W_o': w(ks[10], (H * HD, Q_DIM), H * HD)}
    _L0_xattn_all = _L0_xattn_setup()
    _L0_xattn_in = {k: v for k, v in _L0_xattn_all.items() if k in ('W_kvc', 'W_dq', 'W_uq', 'W_qr', 'W_uk', 'W_kr', 'W_uv', 'W_o')}
    del _L0_xattn_all

    def _L0_attn_setup():
        import jax, jax.numpy as jnp
        import numpy as np
        D_MODEL = 256
        EXPAND = 2
        HEADDIM = 64
        D_STATE = 64
        D_CONV = 4
        D_INNER = EXPAND * D_MODEL
        NHEADS = D_INNER // HEADDIM
        NGROUPS = 1
        CONV_DIM = D_INNER + 2 * NGROUPS * D_STATE
        D_IN_PROJ = 2 * D_INNER + 2 * NGROUPS * D_STATE + NHEADS
        BATCH = 1
        SEQLEN = 128
        RMS_EPS = 1e-05
        key = jax.random.key(seed)
        ks = jax.random.split(key, 8)
        x = jax.random.normal(ks[0], (BATCH, SEQLEN, D_MODEL), jnp.float32)
        W_in = jax.random.normal(ks[1], (D_IN_PROJ, D_MODEL), jnp.float32) * 0.02
        conv_w = jax.random.normal(ks[2], (CONV_DIM, D_CONV), jnp.float32) * 0.2
        conv_b = jnp.zeros((CONV_DIM,), jnp.float32)
        dt_bias = jax.random.uniform(ks[3], (NHEADS,), jnp.float32, -6.0, -3.0)
        A_log = jnp.log(1.0 + 15.0 * jax.random.uniform(ks[4], (NHEADS,), jnp.float32))
        D = jnp.ones((NHEADS,), jnp.float32)
        norm_w = jnp.ones((D_INNER,), jnp.float32)
        W_out = jax.random.normal(ks[5], (D_MODEL, D_INNER), jnp.float32) * 0.02
        return {'x': x, 'W_in': W_in, 'conv_w': conv_w, 'conv_b': conv_b, 'dt_bias': dt_bias, 'A_log': A_log, 'D': D, 'norm_w': norm_w, 'W_out': W_out}
    _L0_attn_all = _L0_attn_setup()
    _L0_attn_in = {k: v for k, v in _L0_attn_all.items() if k in ('W_in', 'conv_w', 'conv_b', 'dt_bias', 'A_log', 'D', 'norm_w', 'W_out')}
    del _L0_attn_all

    def _L0_ffn_setup():
        import jax, jax.numpy as jnp
        import numpy as np
        E = 32
        K = 8
        H = 256
        F = 96
        B, S = (1, 128)

        def _moe(x, wg, w1, v1, w2):
            T = x.shape[0]
            logits = x @ wg.T
            scores = jax.nn.softmax(logits, axis=-1)
            weights, idx = jax.lax.top_k(scores, K)
            weights = weights / jnp.sum(weights, axis=-1, keepdims=True)
            flat_e = idx.reshape(-1)
            flat_t = jnp.repeat(jnp.arange(T), K)
            flat_w = weights.reshape(-1)
            order = jnp.argsort(flat_e)
            e_s = flat_e[order]
            t_s = flat_t[order]
            w_s = flat_w[order]
            group_sizes = jnp.bincount(e_s, length=E).astype(jnp.int32)
            xs = x[t_s]
            g = jax.lax.ragged_dot(xs, w1, group_sizes)
            u = jax.lax.ragged_dot(xs, v1, group_sizes)
            h = jax.nn.silu(g) * u
            ys = jax.lax.ragged_dot(h, w2, group_sizes)
            out = jnp.zeros((T, x.shape[1]), x.dtype).at[t_s].add(ys * w_s[:, None])
            return out
        key = jax.random.key(seed)
        k0, k1, k2, k3, k4 = jax.random.split(key, 5)
        scale = 0.02
        return {'hidden_states': jax.random.normal(k0, (B, S, H), jnp.float32), 'wg': jax.random.normal(k1, (E, H), jnp.float32) * scale, 'w1': jax.random.normal(k2, (E, H, F), jnp.float32) * scale, 'v1': jax.random.normal(k3, (E, H, F), jnp.float32) * scale, 'w2': jax.random.normal(k4, (E, F, H), jnp.float32) * scale}
    _L0_ffn_all = _L0_ffn_setup()
    _L0_ffn_in = {k: v for k, v in _L0_ffn_all.items() if k in ('wg', 'w1', 'v1', 'w2')}
    del _L0_ffn_all
    return {'x': x, 'ctx_2048': ctx_2048, 'itok_BxS_0_1023': itok_BxS_0_1023, 'L0_xattn_W_kvc': _L0_xattn_in['W_kvc'], 'L0_xattn_W_dq': _L0_xattn_in['W_dq'], 'L0_xattn_W_uq': _L0_xattn_in['W_uq'], 'L0_xattn_W_qr': _L0_xattn_in['W_qr'], 'L0_xattn_W_uk': _L0_xattn_in['W_uk'], 'L0_xattn_W_kr': _L0_xattn_in['W_kr'], 'L0_xattn_W_uv': _L0_xattn_in['W_uv'], 'L0_xattn_W_o': _L0_xattn_in['W_o'], 'L0_attn_W_in': _L0_attn_in['W_in'], 'L0_attn_conv_w': _L0_attn_in['conv_w'], 'L0_attn_conv_b': _L0_attn_in['conv_b'], 'L0_attn_dt_bias': _L0_attn_in['dt_bias'], 'L0_attn_A_log': _L0_attn_in['A_log'], 'L0_attn_D': _L0_attn_in['D'], 'L0_attn_norm_w': _L0_attn_in['norm_w'], 'L0_attn_W_out': _L0_attn_in['W_out'], 'L0_ffn_wg': _L0_ffn_in['wg'], 'L0_ffn_w1': _L0_ffn_in['w1'], 'L0_ffn_v1': _L0_ffn_in['v1'], 'L0_ffn_w2': _L0_ffn_in['w2']}

def reference(x, ctx_2048, itok_BxS_0_1023, L0_xattn_W_kvc, L0_xattn_W_dq, L0_xattn_W_uq, L0_xattn_W_qr, L0_xattn_W_uk, L0_xattn_W_kr, L0_xattn_W_uv, L0_xattn_W_o, L0_attn_W_in, L0_attn_conv_w, L0_attn_conv_b, L0_attn_dt_bias, L0_attn_A_log, L0_attn_D, L0_attn_norm_w, L0_attn_W_out, L0_ffn_wg, L0_ffn_w1, L0_ffn_v1, L0_ffn_w2):
    import jax
    import jax.numpy as jnp

    def _L0_xattn_ref(q, kv, seg_id, W_kvc, W_dq, W_uq, W_qr, W_uk, W_kr, W_uv, W_o):
        import jax, jax.numpy as jnp
        import numpy as np
        B, Lq, Lk = (2, 512, 128)
        Q_DIM, KV_DIM = (256, 256)
        H, HD = (16, 128)
        KVC, QC, R = (64, 96, 64)
        LOOKBACK = 8
        NEG = -1e+30

        def _rope(x, L):
            half = x.shape[-1] // 2
            inv_freq = 1.0 / 10000.0 ** (jnp.arange(half, dtype=jnp.float32) / half)
            ang = jnp.arange(L, dtype=jnp.float32)[:, None] * inv_freq
            cos, sin = (jnp.cos(ang), jnp.sin(ang))
            x1, x2 = (x[..., :half], x[..., half:])
            return jnp.concatenate([x1 * cos - x2 * sin, x1 * sin + x2 * cos], axis=-1)
        b, lq, _ = q.shape
        lk = kv.shape[1]
        kv_c = kv @ W_kvc
        q_c = q @ W_dq
        q_nope = (q_c @ W_uq).reshape(b, lq, H, HD).transpose(0, 2, 1, 3)
        q_rope = (q_c @ W_qr).reshape(b, lq, H, R).transpose(0, 2, 1, 3)
        k_nope = (kv_c @ W_uk).reshape(b, lk, H, HD)
        v = (kv_c @ W_uv).reshape(b, lk, H, HD)
        k_rope = kv_c @ W_kr
        q_rope = _rope(q_rope, lq)
        k_rope = _rope(k_rope, lk)
        scale = 1.0 / np.sqrt(HD + R).astype(np.float32)
        scores = (jnp.einsum('bhqd,bkhd->bhqk', q_nope, k_nope) + jnp.einsum('bhqr,bkr->bhqk', q_rope, k_rope)) * scale
        k_ids = jnp.arange(lk)[None, None, :]
        qs = seg_id[:, :, None]
        good = (k_ids <= qs) & (k_ids >= qs - LOOKBACK)
        scores = jnp.where(good[:, None, :, :], scores, NEG)
        attn = jax.nn.softmax(scores, axis=-1)
        out = jnp.einsum('bhqk,bkhd->bqhd', attn, v).reshape(b, lq, H * HD)
        return out @ W_o

    def _L0_attn_ref(x, W_in, conv_w, conv_b, dt_bias, A_log, D, norm_w, W_out):
        import jax, jax.numpy as jnp
        import numpy as np
        D_MODEL = 256
        EXPAND = 2
        HEADDIM = 64
        D_STATE = 64
        D_CONV = 4
        D_INNER = EXPAND * D_MODEL
        NHEADS = D_INNER // HEADDIM
        NGROUPS = 1
        CONV_DIM = D_INNER + 2 * NGROUPS * D_STATE
        D_IN_PROJ = 2 * D_INNER + 2 * NGROUPS * D_STATE + NHEADS
        BATCH = 1
        SEQLEN = 128
        RMS_EPS = 1e-05
        B, T, _ = x.shape
        zxbcdt = jnp.einsum('btd,pd->btp', x, W_in)
        z = zxbcdt[..., :D_INNER]
        xBC = zxbcdt[..., D_INNER:D_INNER + CONV_DIM]
        dt = jax.nn.softplus(zxbcdt[..., D_INNER + CONV_DIM:] + dt_bias)
        xp = jnp.pad(xBC, ((0, 0), (D_CONV - 1, 0), (0, 0)))
        conv = conv_b + sum((xp[:, k:k + T, :] * conv_w[:, k] for k in range(D_CONV)))
        xBC = jax.nn.silu(conv)
        xh = xBC[..., :D_INNER].reshape(B, T, NHEADS, HEADDIM)
        Bm = xBC[..., D_INNER:D_INNER + D_STATE]
        Cm = xBC[..., D_INNER + D_STATE:]
        A = -jnp.exp(A_log)
        dA = jnp.exp(dt * A)

        def step(h, inp):
            dA_t, dt_t, B_t, x_t, C_t = inp
            h = h * dA_t[:, :, None, None] + jnp.einsum('bh,bn,bhp->bhpn', dt_t, B_t, x_t)
            y_t = jnp.einsum('bhpn,bn->bhp', h, C_t)
            return (h, y_t)
        h0 = jnp.zeros((B, NHEADS, HEADDIM, D_STATE), x.dtype)
        xs = (dA.transpose(1, 0, 2), dt.transpose(1, 0, 2), Bm.transpose(1, 0, 2), xh.transpose(1, 0, 2, 3), Cm.transpose(1, 0, 2))
        _, ys = jax.lax.scan(step, h0, xs)
        y = ys.transpose(1, 0, 2, 3) + D[None, None, :, None] * xh
        y = y.reshape(B, T, D_INNER)
        y = y * jax.nn.silu(z)
        y = y * jax.lax.rsqrt(jnp.mean(y * y, axis=-1, keepdims=True) + RMS_EPS) * norm_w
        return jnp.einsum('bti,di->btd', y, W_out)

    def _L0_ffn_ref(hidden_states, wg, w1, v1, w2):
        import jax, jax.numpy as jnp
        import numpy as np
        E = 32
        K = 8
        H = 256
        F = 96
        B, S = (1, 128)

        def _moe(x, wg, w1, v1, w2):
            T = x.shape[0]
            logits = x @ wg.T
            scores = jax.nn.softmax(logits, axis=-1)
            weights, idx = jax.lax.top_k(scores, K)
            weights = weights / jnp.sum(weights, axis=-1, keepdims=True)
            flat_e = idx.reshape(-1)
            flat_t = jnp.repeat(jnp.arange(T), K)
            flat_w = weights.reshape(-1)
            order = jnp.argsort(flat_e)
            e_s = flat_e[order]
            t_s = flat_t[order]
            w_s = flat_w[order]
            group_sizes = jnp.bincount(e_s, length=E).astype(jnp.int32)
            xs = x[t_s]
            g = jax.lax.ragged_dot(xs, w1, group_sizes)
            u = jax.lax.ragged_dot(xs, v1, group_sizes)
            h = jax.nn.silu(g) * u
            ys = jax.lax.ragged_dot(h, w2, group_sizes)
            out = jnp.zeros((T, x.shape[1]), x.dtype).at[t_s].add(ys * w_s[:, None])
            return out
        Bb, Ss, Hh = hidden_states.shape
        x = hidden_states.reshape(Bb * Ss, Hh)
        out = _moe(x, wg, w1, v1, w2)
        return out.reshape(Bb, Ss, Hh)
    x = x + _L0_xattn_ref(_layernorm(x, axis=-1), ctx_2048, itok_BxS_0_1023, L0_xattn_W_kvc, L0_xattn_W_dq, L0_xattn_W_uq, L0_xattn_W_qr, L0_xattn_W_uk, L0_xattn_W_kr, L0_xattn_W_uv, L0_xattn_W_o)
    x = x + _L0_attn_ref(_layernorm(x, axis=-1), L0_attn_W_in, L0_attn_conv_w, L0_attn_conv_b, L0_attn_dt_bias, L0_attn_A_log, L0_attn_D, L0_attn_norm_w, L0_attn_W_out)
    x = x + _L0_ffn_ref(_layernorm(x, axis=-1), L0_ffn_wg, L0_ffn_w1, L0_ffn_v1, L0_ffn_w2)
    return x

_drawn_inputs = setup_inputs


def setup_inputs(seed=0):
    import zlib

    import numpy as np

    out = dict(_drawn_inputs(seed))
    spreads = {'L0_attn_conv_b': (0.0, 0.1), 'L0_attn_D': (1.0, 0.2), 'L0_attn_norm_w': (1.0, 0.2)}
    factors = {'L0_attn_dt_bias': 8.0,
     'L0_attn_A_log': 8.0,
     'L0_ffn_wg': 8.0,
     'L0_ffn_w1': 8.0,
     'L0_ffn_v1': 8.0,
     'L0_ffn_w2': 8.0}
    for name, (base, spread) in spreads.items():
        noise = np.random.default_rng([zlib.crc32(name.encode()), seed]).standard_normal(out[name].shape)
        drawn = base * np.exp(spread * noise) if base else spread * noise
        out[name] = jnp.asarray(drawn.astype(out[name].dtype))
    for name, factor in factors.items():
        out[name] = (out[name] * factor).astype(out[name].dtype)
    return out
```

```python
from contextlib import ExitStack

import numpy as np

import concourse.bass as bass
from concourse import mybir

ALU = mybir.AluOpType
ACT = mybir.ActivationFunctionType
F32 = mybir.dt.float32
BF16 = mybir.dt.bfloat16
I32 = mybir.dt.int32
AX_X = mybir.AxisListType.X

P = 128
B, L, D = 32, 64, 256
NB = P // L
T = B * L // P
DC = D // P
KEYS = 128
LOOKBACK = 8
H, HD = 16, 128
KVC, QC, R = 64, 96, 64
NP_ = H // 2
DI, NH, PH, NS, TAPS = 512, 8, 64, 64, 4
XC = DI // P
CH = XC + 2
E, K8, F = 32, 8, 96
EG = 4
GW = EG * F
G = E // EG
GC = GW // P
NEG = -1e30
SCALE = float(1.0 / np.sqrt(np.float32(HD + R)))
LN_EPS = 1e-5

CONSTS = [("ident", P), ("same_l", P), ("later", P), ("upto", L), ("upto4", L), ("key_no", KEYS),
          ("cos_q", R), ("sin_q", R), ("cos_k", R), ("sin_k", R), ("half", 1)]
PARAMS = [("dt_bias", NH), ("a_log", NH), ("d_skip", DI), ("norm_w", XC), ("conv_w", CH * TAPS), ("conv_b", CH)]


def columns(fields):
    at, out = 0, {}
    for name, width in fields:
        out[name] = (at, at + width)
        at += width
    return out, at


def constants():
    c, width = columns(CONSTS)
    out = np.zeros((P, width), np.float32)
    p = np.arange(P)

    def put(name, values):
        out[:, c[name][0]:c[name][1]] = values

    def rope(pos):
        half = R // 2
        inv = (1.0 / np.float32(10000.0) ** (np.arange(half, dtype=np.float32) / half)).astype(np.float32)
        ang = pos.astype(np.float32)[:, None] * inv
        cos, sin = np.cos(ang), np.sin(ang)
        return np.concatenate([cos, cos], 1), np.concatenate([-sin, sin], 1)

    put("ident", np.eye(P))
    put("same_l", (p[:, None] % L) == (p[None, :] % L))
    put("later", (p[:, None] > p[None, :]) & (p[:, None] // L == p[None, :] // L))
    put("upto", (p[:, None] % L) <= np.arange(L)[None, :])
    put("upto4", 0.25 * ((p[:, None] % L) <= np.arange(L)[None, :]))
    put("key_no", np.arange(KEYS)[None, :] + 4.0)
    cq, sq = rope(p % L)
    ck, sk = rope(p)
    put("cos_q", cq)
    put("sin_q", sq)
    put("cos_k", ck)
    put("sin_k", sk)
    put("half", -0.5)
    return out


ORDER = ["kv", "ln1", "ln2", "ln3", "qc", "gate", "gu0", "kt", "qup", "gu1", "ex0", "qt", "score", "gu2", "ex1",
         "gu3", "ex2", "pt", "gu4", "ex3", "pv", "gu5", "ex4", "attn_out", "proj", "gu6", "ex5", "decay", "gu7",
         "ex6", "conv", "ex7", "scan", "scan_out", "moe_out"]


def build(nc, xt, ctxT, seg, consts, params, w_dq, w_qr, w_uqT, w_ukT, w_kvc, w_kvcT, w_kr, w_uvT, w_o,
          w_in, w_out, wg, w1, v1, w2, out):
    cc, cwidth = columns(CONSTS)
    pc, pwidth = columns(PARAMS)
    with ExitStack() as ctx:
        def sb(name, shape, dt=F32):
            return ctx.enter_context(nc.sbuf_tensor(name, shape, dt))

        def sem(name):
            return ctx.enter_context(nc.semaphore(name))

        w1_sb = sb("w1_sb", [P, DC, E * F])
        v1_sb = sb("v1_sb", [P, DC, E * F])
        w2_sb = sb("w2_sb", [P, E * F // P, D])
        wg_sb = sb("wg_sb", [P, DC, E])
        wdq_sb = sb("wdq_sb", [P, DC, QC])
        wq_sb = sb("wq_sb", [QC, H, KVC + R])
        wk_sb = sb("wk_sb", [P, DC, KVC + R])
        wvo_sb = sb("wvo_sb", [P, NP_, D])
        win_sb = sb("win_sb", [P, DC, 2 * DI + 2 * NS + NH])
        wout_sb = sb("wout_sb", [P, XC, D])
        wkr_sb = sb("wkr_sb", [KVC, R])
        c_sb = sb("c_sb", [P, cwidth])
        p_sb = sb("p_sb", [P, pwidth])
        same_l = sb("same_l", [P, P], BF16)
        a_neg = sb("a_neg", [P, NH])
        seg_i = sb("seg_i", [P, T], I32)
        seg_f = sb("seg_f", [P, T])

        def const(name):
            return c_sb[:, cc[name][0]:cc[name][1]]

        def param(name):
            return p_sb[:, pc[name][0]:pc[name][1]]

        ident = const("ident")

        x_in = sb("x_in", [P, D])
        ctx_sb = sb("ctx_sb", [P, NB, DC, KEYS])
        x_res = sb("x_res", [P, D])
        x1 = sb("x1", [P, D])
        x1_res = sb("x1_res", [P, D])
        x2 = sb("x2", [P, D])
        x2_res = sb("x2_res", [P, D])
        x3 = sb("x3", [P, D])
        stats = sb("stats", [P, 3, 6])
        mean_var = sb("mean_var", [P, 3, 2])
        var_eps = sb("var_eps", [P, 4])
        rstd = sb("rstd", [P, 4])
        xn = sb("xn", [P, 3, D])
        xnT = sb("xnT", [P, 3, DC, P])
        qcT = sb("qcT", [QC, P])
        k_sb = sb("k_sb", [KEYS, NB, KVC + R])
        k_cos = sb("k_cos", [KEYS, NB, R])
        k_sin = sb("k_sin", [KEYS, NB, R])
        kT = sb("kT", [KVC + R, NB, KEYS])
        q_sb = sb("q_sb", [P, H, KVC + R])
        q_cos = sb("q_cos", [P, 2, EG, R])
        q_sin = sb("q_sin", [P, 2, EG, R])
        qT = sb("qT", [KVC + R, NB, H, L])
        mask_d = sb("mask_d", [P, KEYS])
        mask = sb("mask", [P, KEYS], BF16)
        neg_max = sb("neg_max", [P, NB, NP_])
        row_sum = sb("row_sum", [P, NB, NP_])
        row_inv = sb("row_inv", [P, NB, NP_])
        probs = sb("probs", [P, NB, NP_, KEYS])
        pT = sb("pT", [KEYS, NB, 2, NP_, L])
        oT = sb("oT", [P, NP_, NB, L])
        z_th = sb("z_th", [P, DI])
        xpad = sb("xpad", [P, CH, NB, TAPS - 1 + L])
        conv = sb("conv", [P, CH, NB, L])
        conv_th = sb("conv_th", [P, CH, NB, L])
        xbc = conv_th[:].rearrange("p c b l -> p c (b l)")
        dt8 = sb("dt8", [P, 10, NH])
        decay_in = sb("decay_in", [P, NH, L])
        decay = sb("decay", [P, NH, L])
        gram = sb("gram", [P, L])
        scan_w = decay
        xh = sb("xh", [P, DI])
        xh_dt = sb("xh_dt", [P, NH, PH])
        xh_d = sb("xh_d", [P, DI])
        y_sb = sb("y_sb", [P, DI])
        y_gated = y_sb
        y_ms = sb("y_ms", [P, 1])
        yT = sb("yT", [P, XC, P])
        logits = sb("logits", [P, E])
        top8 = sb("top8", [P, 8])
        struck = sb("struck", [P, E])
        chosen = sb("chosen", [P, E])
        neg_top = sb("neg_top", [P, 1])
        e_exp = sb("e_exp", [P, E])
        e_sum = sb("e_sum", [P, 2])
        e_w = sb("e_w", [P, E])
        g_th = sb("g_th", [P, 2, GW])
        gu = sb("gu", [P, 2, GW])
        h = sb("h", [P, 2, GW])
        hT = sb("hT", [P, 2, GC, P])

        wkvcT_sb = oT[:].rearrange("p j b l -> p (j b l)")[0:KVC, 0:D]
        wuqT_st = q_sb[:].rearrange("p h c -> p (h c)")[:, 0:H * QC].rearrange("p (h c) -> p h c", h=H)
        wukT_st = qT[:].rearrange("p b h l -> p (b h l)")[:, 0:H * KVC].rearrange("p (h c) -> p h c", h=H)
        wuvT_st = qT[:].rearrange("p b h l -> p (b h l)")[:, H * KVC:2 * H * KVC].rearrange("p (h c) -> p h c", h=H)
        wo_lo = probs[:].rearrange("p b j k -> p (b j k)").rearrange("p (h n) -> p h n", n=D)
        wo_hi = pT[:].rearrange("p b e j l -> p (b e j l)").rearrange("p (h n) -> p h n", n=D)

        ps = ctx.enter_context(nc.psum_tensor("ps", [P, 4, 512], F32))
        ps_g = ctx.enter_context(nc.psum_tensor("ps_g", [P, 512], F32))
        ps_u = ctx.enter_context(nc.psum_tensor("ps_u", [P, 512], F32))
        ps_t = ctx.enter_context(nc.psum_tensor("ps_t", [P, 512], F32))
        ps_y = ctx.enter_context(nc.psum_tensor("ps_y", [P, 512], F32))

        (s_const, s_wsetup, s_wmoe, s_x, s_ctx, s_xres, s_store) = [sem(n) for n in (
            "consts_loaded", "weights_loaded", "expert_weights_loaded", "x_loaded", "ctx_loaded",
            "x_res_loaded", "out_stored")]
        s_setup = sem("setup_products")
        s_setup_ev = sem("setup_copied")
        s_setup_misc = sem("setup_misc")
        s_aexp = sem("a_exp_done")
        s_pad = sem("pads_zeroed")
        ln_stat = [sem(f"ln{k}_stats") for k in range(3)]
        ln_mv = [sem(f"ln{k}_mean_var") for k in range(3)]
        ln_ve = [sem(f"ln{k}_var_eps") for k in range(3)]
        ln_rstd = [sem(f"ln{k}_rstd") for k in range(3)]
        ln_out = [sem(f"ln{k}_normed") for k in range(3)]
        ln_tr = [sem(f"ln{k}_transposed") for k in range(3)]
        ln_T = [sem(f"ln{k}_T_copied") for k in range(3)]
        kv_done = sem("kv_done")
        k_lat = sem("k_latent_copied")
        k_rot_parts = sem("k_rot_parts")
        k_rot = sem("k_rotated")
        kt_done = sem("kT_done")
        kt_copied = sem("kT_copied")
        qc_done = sem("qc_done")
        qc_copied = sem("qc_copied")
        qup_done = sem("q_up_done")
        q_lat = sem("q_latent_copied")
        q_parts = sem("q_rot_parts")
        q_rot = sem("q_rotated")
        qt_done = sem("qT_done")
        qt_copied = sem("qT_copied")
        mask_step = sem("mask_distance")
        mask_done = sem("mask_done")
        score_done = sem("scores_done")
        max_done = sem("max_done")
        exp_done = sem("exp_done")
        inv_done = sem("row_inv_done")
        prob_done = sem("probs_done")
        pt_done = sem("pT_done")
        pt_copied = sem("pT_copied")
        pv_done = sem("pv_done")
        o_copied = sem("oT_copied")
        ao_done = sem("attn_out_done")
        x1_ready = sem("x1_ready")
        x1_kept = sem("x1_kept")
        z_done = sem("z_done")
        zth_done = sem("z_tanh_done")
        zsilu_done = sem("z_silu_done")
        xpart_done = sem("x_part_done")
        bc_done = sem("dt_bc_done")
        pad_copied = sem("pad_copied")
        dt_raw = sem("dt_biased")
        dt_step = sem("softplus_steps")
        dt_abs = sem("dt_abs_done")
        soft_end = sem("softplus_end")
        dt_exp = sem("dt_exp_done")
        dt_done = sem("dt_done")
        a_done = sem("dt_a_done")
        decay_in_done = sem("decay_in_done")
        decay_sum = sem("decay_sums_done")
        decay_exp = sem("decay_exp_done")
        conv_step = sem("conv_steps")
        cth_done = sem("conv_tanh_done")
        xbc_done = sem("xbc_done")
        xh_tr = sem("xh_transposed")
        xh_copied = sem("xh_copied")
        xhdt_done = sem("xh_dt_done")
        xhd_done = sem("xh_d_done")
        gram_done = sem("gram_done")
        gram_masked = sem("gram_masked")
        scanw_done = sem("scan_w_done")
        y_done = sem("y_done")
        y_skip = sem("y_with_skip")
        yg_done = sem("y_gated_done")
        ysq_done = sem("y_mean_square")
        yve_done = sem("y_var_eps")
        yr_done = sem("y_rstd")
        yt_done = sem("yT_done")
        yt_copied = sem("yT_copied")
        so_done = sem("scan_out_done")
        x2_ready = sem("x2_ready")
        x2_kept = sem("x2_kept")
        lg_done = sem("logits_done")
        lg_copied = sem("logits_copied")
        gate_step = sem("gate_steps")
        e_neg = sem("neg_top_done")
        e_exp_done = sem("gate_exp_done")
        ew_done = sem("expert_weights_done")
        gu_done = sem("gate_up_done")
        gth_done = sem("gate_tanh_done")
        gsilu_done = sem("gate_silu_done")
        gu_prod = sem("gate_up_product")
        h_done = sem("h_done")
        ht_done = sem("hT_done")
        ht_copied = sem("hT_copied")
        down_done = sem("down_done")
        x3_ready = sem("x3_ready")
        passed = sem("waits_passed")
        SOFT, GATE = 12, 7

        def reuse(eng, s, value):
            if not (isinstance(value, int) and value <= 0):
                eng.wait_ge(s, value)

        def stand_alone(eng):
            eng.sem_inc(passed, 1)

        class Steps:
            def __init__(self, eng, s, tile, per):
                self.eng, self.s, self.base, self.per, self.k = eng, s, tile * per, per, 0

            def link(self, ins):
                self.k += 1
                assert self.k <= self.per
                ins.then_inc(self.s, 1)
                self.eng.wait_ge(self.s, self.base + self.k)

        def turns(eng, run):
            run(0, True, False, False)
            run(1, True, True, False)
            run(2, True, True, True)
            with eng.Fori(3, T) as n:
                run(n, True, True, True)
            run(T, False, True, True)
            run(T + 1, False, False, True)

        def run_order(steps, n, attn, scan, moe):
            for name in ORDER:
                chain, fn = steps.get(name, (None, None))
                if fn is None:
                    continue
                if chain == "a" and attn:
                    fn(n)
                if chain == "s" and scan:
                    fn(n - 1)
                if chain == "m" and moe:
                    fn(n - 2)

        block = ctx.enter_context(nc.Block())

        @block.sync
        def _(sp):
            sp.dma_start(c_sb[:], consts).then_inc(s_const, 16)
            sp.dma_start(p_sb[:], params).then_inc(s_const, 16)
            sp.dma_start(seg_i[:], seg).then_inc(s_const, 16)
            n_setup = 0
            for dst, src in ((wuqT_st, w_uqT), (wukT_st, w_ukT), (wq_sb[:, :, KVC:KVC + R], w_qr),
                             (wkvcT_sb, w_kvcT), (wkr_sb[:], w_kr), (wk_sb[:, :, 0:KVC], w_kvc),
                             (wuvT_st, w_uvT), (wo_lo, w_o[:, 0:NP_, :]), (wo_hi, w_o[:, NP_:H, :]),
                             (wdq_sb[:], w_dq), (win_sb[:], w_in), (wout_sb[:], w_out), (wg_sb[:], wg)):
                sp.dma_start(dst, src).then_inc(s_wsetup, 16)
                n_setup += 16

            def load(t):
                reuse(sp, ln_out[0], t)
                sp.dma_start(x_in[:], xt[bass.ts(t, P), :]).then_inc(s_x, 16)
                reuse(sp, kv_done, t)
                sp.dma_start(ctx_sb[:].rearrange("p b c k -> p (b c k)"), ctxT[bass.ts(t, P), :]).then_inc(s_ctx, 16)
                reuse(sp, x1_ready, t)
                sp.dma_start(x_res[:], xt[bass.ts(t, P), :]).then_inc(s_xres, 16)

            def store(t):
                sp.wait_ge(x3_ready, t + 1)
                sp.dma_start(out[bass.ts(t, P), :], x3[:]).then_inc(s_store, 16)

            load(0)
            for dst, src in ((w1_sb, w1), (v1_sb, v1), (w2_sb, w2)):
                sp.dma_start(dst[:].rearrange("p c n -> p (c n)"), src).then_inc(s_wmoe, 16)
            load(1)
            with sp.Fori(2, T) as n:
                load(n)
                store(n - 2)
            store(T - 2)
            store(T - 1)
            sp.wait_ge(s_store, 16 * T)

        @block.tensor
        def _(pe):
            mm = nc.tensor.matmul
            pe.wait_ge(s_const, 48)
            pe.wait_ge(s_wsetup, 16 * 13)
            for hh in range(H):
                ins = mm(ps[0:QC, hh // 8, (hh % 8) * KVC:(hh % 8 + 1) * KVC], wuqT_st[:, hh, :], wukT_st[:, hh, :],
                         start=True, stop=True)
                if hh % 8 == 7:
                    ins.then_inc(s_setup, 1)
            for c in range(DC):
                ins = mm(ps[:, 2, c * R:(c + 1) * R], wkvcT_sb[:, c * P:(c + 1) * P], wkr_sb[:], start=True, stop=True)
            ins.then_inc(s_setup, 1)
            for j in range(NP_):
                if j >= 2:
                    pe.wait_ge(s_setup_ev, 3 + j - 1)
                for e in range(2):
                    hh = 2 * j + e
                    wo = wo_lo if hh < NP_ else wo_hi
                    ins = mm((ps_g if j % 2 else ps_u)[e * KVC:(e + 1) * KVC, 0:D],
                             wuvT_st[:, hh, :], wo[:, hh % NP_, :], start=True, stop=True)
                ins.then_inc(s_setup, 1)
            pe.wait_ge(s_setup_ev, 3 + NP_)
            pe.wait_ge(s_setup_misc, 3)

            def transpose_in(k, t, bank):
                pe.wait_ge(ln_out[k], t + 1)
                for c in range(DC):
                    ins = nc.tensor.transpose(bank[:, c * P:(c + 1) * P], xn[:, k, c * P:(c + 1) * P], ident)
                ins.then_inc(ln_tr[k], 1)

            def kv(t):
                pe.wait_ge(s_ctx, (t + 1) * 16)
                reuse(pe, x2_ready, t - 1)
                for b in range(NB):
                    for c in range(DC):
                        ins = mm(ps[:, 0, b * P:(b + 1) * P], ctx_sb[:, b, c, :], wk_sb[:, c, :],
                                 start=(c == 0), stop=(c == DC - 1))
                ins.then_inc(kv_done, 1)

            def ln1(t):
                reuse(pe, gram_masked, t - 1)
                transpose_in(0, t, ps[:, 1, :])

            def qc(t):
                pe.wait_ge(ln_T[0], t + 1)
                reuse(pe, y_skip, t - 1)
                for c in range(DC):
                    ins = mm(ps[0:QC, 2, 0:P], wdq_sb[:, c, :], xnT[:, 0, c, :], start=(c == 0), stop=(c == DC - 1))
                ins.then_inc(qc_done, 1)

            def kt(t):
                reuse(pe, yt_copied, t - 1)
                pe.wait_ge(k_lat, t + 1)
                pe.wait_ge(k_rot, t + 1)
                for b in range(NB):
                    ins = nc.tensor.transpose(ps[:, 3, b * P:(b + 1) * P], k_sb[:, b, :], ident)
                ins.then_inc(kt_done, 1)

            def qup(t):
                pe.wait_ge(qc_copied, t + 1)
                for n in range(4):
                    if n == 3:
                        pe.wait_ge(kt_copied, t + 1)
                    mm(ps[:, n, :], qcT[:], wq_sb[:, EG * n:EG * n + EG, :], start=True, stop=True).then_inc(qup_done, 1)

            def qt(t):
                for n in range(4):
                    pe.wait_ge(q_lat, t * 4 + n + 1)
                    pe.wait_ge(q_rot, t * 4 + n + 1)
                    for hh in range(4):
                        ins = nc.tensor.transpose(ps[:, n, hh * P:(hh + 1) * P], q_sb[:, 4 * n + hh, :], ident)
                    ins.then_inc(qt_done, 1)

            def score(t):
                pe.wait_ge(mask_done, t + 1)
                pe.wait_ge(qt_copied, t * 4 + 4)
                for b in range(NB):
                    own = slice(b * L, (b + 1) * L)
                    for half in range(2):
                        bank = ps[:, 2 * b + half, :]
                        mm(bank, same_l[own, :], mask[own, :].unsqueeze(1).to_broadcast([L, 4, KEYS]),
                           start=True, stop=False)
                        for j in range(4):
                            jj = 4 * half + j
                            ins = mm(bank[:, j * KEYS:(j + 1) * KEYS], qT[:, b, 2 * jj:2 * jj + 2, :], kT[:, b, :],
                                     start=False, stop=(j == 3))
                    ins.then_inc(score_done, 1)

            def pt(t):
                for b in range(NB):
                    pe.wait_ge(prob_done, t * NB + b + 1)
                    for half in range(2):
                        for j in range(4):
                            ins = nc.tensor.transpose(ps[:, 2 * b + half, j * P:(j + 1) * P],
                                                      probs[:, b, 4 * half + j, :], ident)
                        ins.then_inc(pt_done, 1)

            def pv(t):
                for b in range(NB):
                    pe.wait_ge(pt_copied, t * 4 + 2 * b + 2)
                    for e in range(2):
                        ins = mm(ps[e * KVC:(e + 1) * KVC, b, :], k_sb[:, b, 0:KVC], pT[:, b, e, :, :],
                                 start=True, stop=True)
                    ins.then_inc(pv_done, 1)

            def attn_out(t):
                pe.wait_ge(o_copied, t * NB + NB)
                for j in range(NP_):
                    ins = mm(ps[:, 2, 0:D], oT[:, j, :, :], wvo_sb[:, j, :], start=(j == 0), stop=(j == NP_ - 1))
                ins.then_inc(ao_done, 1)

            def proj(t, attn):
                if not attn:
                    pe.wait_ge(x2_ready, t)
                transpose_in(1, t, ps[:, 3, :])
                pe.wait_ge(ln_T[1], t + 1)
                for c in range(DC):
                    ins = mm(ps[:, 0, :], xnT[:, 1, c, :], win_sb[:, c, 0:DI], start=(c == 0), stop=(c == DC - 1))
                ins.then_inc(z_done, 1)
                for m in range(XC):
                    for c in range(DC):
                        ins = mm(ps[:, 1, m * P:(m + 1) * P], win_sb[:, c, DI + m * P:DI + (m + 1) * P],
                                 xnT[:, 1, c, :], start=(c == 0), stop=(c == DC - 1))
                ins.then_inc(xpart_done, 1)
                if attn:
                    pe.wait_ge(x1_ready, t + 2)
                for c in range(DC):
                    mm(ps[:, 2, 0:NH], xnT[:, 1, c, :], win_sb[:, c, 2 * DI + 2 * NS:2 * DI + 2 * NS + NH],
                       start=(c == 0), stop=(c == DC - 1))
                for m in range(2):
                    at = 2 * DI + m * NS
                    for c in range(DC):
                        ins = mm(ps[0:NS, 2, (m + 1) * P:(m + 2) * P], win_sb[:, c, at:at + NS], xnT[:, 1, c, :],
                                 start=(c == 0), stop=(c == DC - 1))
                ins.then_inc(bc_done, 1)

            def decay_(t):
                pe.wait_ge(decay_in_done, t + 1)
                mm(ps[:, 3, :], const("later"), decay_in[:], start=True, stop=True).then_inc(decay_sum, 1)

            def conv_(t):
                pe.wait_ge(xbc_done, t * 2 + 2)
                pe.wait_ge(zth_done, t + 1)
                pe.wait_ge(zsilu_done, t + 1)
                for c in range(XC):
                    ins = nc.tensor.transpose(ps[:, 0, c * P:(c + 1) * P], xbc[:, c, :], ident)
                ins.then_inc(xh_tr, 1)
                for b in range(NB):
                    own = slice(b * L, (b + 1) * L)
                    ins = mm(ps[own, 1, 0:L], xbc[0:NS, XC, own], xbc[0:NS, XC + 1, own], start=True, stop=True)
                ins.then_inc(gram_done, 1)

            def scan_(t):
                pe.wait_ge(scanw_done, t + 1)
                pe.wait_ge(xhdt_done, t + 1)
                stand_alone(pe)
                for b in range(NB):
                    own = slice(b * L, (b + 1) * L)
                    for hh in range(NH):
                        ins = mm(ps[own, 2, hh * PH:(hh + 1) * PH], scan_w[own, hh, :], xh_dt[own, hh, :],
                                 start=True, stop=True)
                ins.then_inc(y_done, 1)

            def scan_out(t):
                pe.wait_ge(yg_done, t + 1)
                for c in range(XC):
                    ins = nc.tensor.transpose(ps[:, 3, c * P:(c + 1) * P], y_gated[:, c * P:(c + 1) * P], ident)
                ins.then_inc(yt_done, 1)
                pe.wait_ge(yt_copied, t + 1)
                pe.wait_ge(xh_copied, t + 1)
                for c in range(XC):
                    ins = mm(ps[:, 0, 0:D], yT[:, c, :], wout_sb[:, c, :], start=(c == 0), stop=(c == XC - 1))
                ins.then_inc(so_done, 1)

            def gate(t):
                if isinstance(t, int) and t == 0:
                    pe.wait_ge(s_wmoe, 48)
                reuse(pe, ht_copied, t * G)
                transpose_in(2, t, ps_t)
                pe.wait_ge(ln_T[2], t + 1)
                reuse(pe, gu_prod, t * G)
                for c in range(DC):
                    ins = mm(ps_g[:, 0:E], xnT[:, 2, c, :], wg_sb[:, c, :], start=(c == 0), stop=(c == DC - 1))
                ins.then_inc(lg_done, 1)

            def gate_up(g):
                def run(t):
                    if g == 0:
                        pe.wait_ge(lg_copied, t + 1)
                    else:
                        pe.wait_ge(gu_prod, t * G + g)
                    for w, bank in ((w1_sb, ps_g), (v1_sb, ps_u)):
                        for c in range(DC):
                            ins = mm(bank[:, 0:GW], xnT[:, 2, c, :], w[:, c, g * GW:(g + 1) * GW],
                                     start=(c == 0), stop=(c == DC - 1))
                    ins.then_inc(gu_done, 1)
                return run

            def down(g):
                def run(t):
                    pe.wait_ge(h_done, t * G + g + 1)
                    if g == 0:
                        pe.wait_ge(ln_T[2], t + 1)
                    else:
                        pe.wait_ge(ht_copied, t * G + g)
                    for c in range(GC):
                        ins = nc.tensor.transpose(ps_t[:, c * P:(c + 1) * P], h[:, g % 2, c * P:(c + 1) * P], ident)
                    ins.then_inc(ht_done, 1)
                    if g == 0:
                        reuse(pe, x3_ready, t)
                    pe.wait_ge(ht_copied, t * G + g + 1)
                    for c in range(GC):
                        ins = mm(ps_y[:, 0:D], hT[:, g % 2, c, :], w2_sb[:, g * GC + c, :],
                                 start=(g == 0 and c == 0), stop=(g == G - 1 and c == GC - 1))
                    ins.then_inc(down_done, 1)
                return run

            def run(n, attn, scan, moe):
                steps = {"kv": ("a", kv), "ln1": ("a", ln1), "qc": ("a", qc), "kt": ("a", kt), "qup": ("a", qup),
                         "qt": ("a", qt), "score": ("a", score), "pt": ("a", pt), "pv": ("a", pv),
                         "attn_out": ("a", attn_out), "proj": ("s", lambda t: proj(t, attn)), "decay": ("s", decay_),
                         "conv": ("s", conv_), "scan": ("s", scan_), "scan_out": ("s", scan_out), "gate": ("m", gate)}
                for g in range(G):
                    steps[f"gu{g}"] = ("m", gate_up(g))
                    steps[f"ex{g}"] = ("m", down(g))
                run_order(steps, n, attn, scan, moe)

            turns(pe, run)

        @block.scalar
        def _(act):
            fn = nc.scalar.activation
            act.wait_ge(s_const, 48)
            fn(a_neg[:], param("a_log"), ACT.Exp).then_inc(s_aexp, 1)

            def copy_T(k, t, bank):
                act.wait_ge(ln_tr[k], t + 1)
                fn(xnT[:, k, :, :], bank[:, 0:D], ACT.Copy).then_inc(ln_T[k], 1)

            def kv(t):
                act.wait_ge(kv_done, t + 1)
                fn(k_sb[:, :, 0:KVC], ps[:, 0, 0:NB * P].rearrange("p (b c) -> p b c", b=NB)[:, :, 0:KVC],
                   ACT.Copy).then_inc(k_lat, 1)

            def ln1(t):
                copy_T(0, t, ps[:, 1, :])

            def qc(t):
                act.wait_ge(qc_done, t + 1)
                fn(qcT[:], ps[0:QC, 2, 0:P], ACT.Copy).then_inc(qc_copied, 1)

            def kt(t):
                act.wait_ge(kt_done, t + 1)
                fn(kT[:], ps[:, 3, 0:NB * P].rearrange("p (b k) -> p b k", b=NB), ACT.Copy).then_inc(kt_copied, 1)

            def qup(t):
                for n in range(4):
                    act.wait_ge(qup_done, t * 4 + n + 1)
                    fn(q_sb[:, EG * n:EG * n + EG, 0:KVC],
                       ps[:, n, :].rearrange("p (h c) -> p h c", h=EG)[:, :, 0:KVC], ACT.Copy).then_inc(q_lat, 1)

            def qt(t):
                for n in range(4):
                    act.wait_ge(qt_done, t * 4 + n + 1)
                    fn(qT[:, :, 4 * n:4 * n + 4, :].rearrange("p b h l -> p h b l"),
                       ps[:, n, :].rearrange("p (h b l) -> p h b l", h=4, b=NB), ACT.Copy, scale=SCALE)\
                        .then_inc(qt_copied, 1)

            def score(t):
                for b in range(NB):
                    act.wait_ge(max_done, t * NB + b + 1)
                    for j in range(NP_):
                        fn(probs[:, b, j, :], ps[:, 2 * b + j // 4, (j % 4) * KEYS:(j % 4 + 1) * KEYS], ACT.Exp,
                           bias=neg_max[:, b, j:j + 1], accum_out=row_sum[:, b, j:j + 1]).then_inc(exp_done, 1)

            def pt(t):
                for b in range(NB):
                    for half in range(2):
                        act.wait_ge(pt_done, t * 4 + 2 * b + half + 1)
                        fn(pT[:, b, :, 4 * half:4 * half + 4, :].rearrange("p e j l -> p j e l"),
                           ps[:, 2 * b + half, :].rearrange("p (j e l) -> p j e l", j=4, e=2), ACT.Copy)\
                            .then_inc(pt_copied, 1)

            def proj(t):
                copy_T(1, t, ps[:, 3, :])
                act.wait_ge(z_done, t + 1)
                reuse(act, yg_done, t)
                fn(z_th[:], ps[:, 0, :], ACT.Tanh, scale=0.5).then_inc(zth_done, 1)
                act.wait_ge(xpart_done, t + 1)
                reuse(act, conv_step, t * TAPS * CH)
                fn(xpad[:, 0:XC, :, TAPS - 1:], ps[:, 1, :].rearrange("p (c b l) -> p c b l", c=XC, b=NB),
                   ACT.Copy).then_inc(pad_copied, 1)
                act.wait_ge(bc_done, t + 1)
                fn(xpad[0:NS, XC:CH, :, TAPS - 1:],
                   ps[0:NS, 2, P:3 * P].rearrange("p (c b l) -> p c b l", c=2, b=NB), ACT.Copy).then_inc(pad_copied, 1)
                act.wait_ge(dt_abs, t + 1)
                fn(dt8[:, 2, :], dt8[:, 1, :], ACT.Exp, scale=-1.0).then_inc(dt_exp, 1)

            def decay_(t):
                act.wait_ge(decay_sum, t + 1)
                reuse(act, y_done, t)
                fn(decay[:].rearrange("p h l -> p (h l)"), ps[:, 3, :], ACT.Exp).then_inc(decay_exp, 1)

            def conv_(t):
                act.wait_ge(conv_step, t * TAPS * CH + TAPS * CH)
                reuse(act, xh_tr, t)
                reuse(act, gram_done, t)
                fn(conv_th[:, 0:XC], conv[:, 0:XC], ACT.Tanh, scale=0.5).then_inc(cth_done, 1)
                fn(conv_th[0:NS, XC:CH], conv[0:NS, XC:CH], ACT.Tanh, scale=0.5).then_inc(cth_done, 1)
                act.wait_ge(xh_tr, t + 1)
                reuse(act, xhd_done, t)
                fn(xh[:], ps[:, 0, :], ACT.Copy).then_inc(xh_copied, 1)

            def scan_out(t):
                act.wait_ge(yg_done, t + 1)
                reuse(act, yve_done, t)
                fn(xh_d[:], y_gated[:], ACT.Square, scale=0.5, accum_out=y_ms[:]).then_inc(ysq_done, 1)
                act.wait_ge(yt_done, t + 1)
                fn(yT[:].rearrange("p c t -> p (c t)"), ps[:, 3, :], ACT.Copy).then_inc(yt_copied, 1)

            def gate(t):
                copy_T(2, t, ps_t)
                act.wait_ge(e_neg, t + 1)
                fn(e_exp[:], logits[:], ACT.Exp, bias=neg_top[:]).then_inc(e_exp_done, 1)

            def gate_up(g):
                def run(t):
                    act.wait_ge(gu_done, t * G + g + 1)
                    reuse(act, gsilu_done, t * G + g - 1)
                    fn(g_th[:, g % 2, :], ps_g[:, 0:GW], ACT.Tanh, scale=0.5).then_inc(gth_done, 1)
                return run

            def down(g):
                def run(t):
                    act.wait_ge(ht_done, t * G + g + 1)
                    reuse(act, down_done, t * G + g - 1)
                    fn(hT[:, g % 2, :, :], ps_t[:, 0:GW], ACT.Copy).then_inc(ht_copied, 1)
                return run

            steps = {"kv": ("a", kv), "ln1": ("a", ln1), "qc": ("a", qc), "kt": ("a", kt), "qup": ("a", qup),
                     "qt": ("a", qt), "score": ("a", score), "pt": ("a", pt), "proj": ("s", proj),
                     "decay": ("s", decay_), "conv": ("s", conv_), "scan_out": ("s", scan_out), "gate": ("m", gate)}
            for g in range(G):
                steps[f"gu{g}"] = ("m", gate_up(g))
                steps[f"ex{g}"] = ("m", down(g))
            turns(act, lambda n, a, s, m: run_order(steps, n, a, s, m))

        @block.gpsimd
        def _(pool):
            gp = nc.gpsimd
            gp.memset(xpad[:], 0.0).then_inc(s_pad, 1)
            pool.wait_ge(s_const, 48)

            def rsqrt(k, t, ready, done):
                pool.wait_ge(ready, t + 1)
                gp.tensor_tensor(rstd[:, k:k + 1], var_eps[:, k:k + 1], const("half"), ALU.pow).then_inc(done, 1)

            def ln1(t):
                rsqrt(0, t, ln_ve[0], ln_rstd[0])

            def ln2(t):
                rsqrt(1, t, ln_ve[1], ln_rstd[1])
                pool.wait_ge(x1_ready, t + 1)
                reuse(pool, x2_ready, t)
                stand_alone(pool)
                gp.tensor_copy(x1_res[:], x1[:]).then_inc(x1_kept, 1)

            def ln3(t):
                rsqrt(2, t, ln_ve[2], ln_rstd[2])
                pool.wait_ge(x2_ready, t + 1)
                reuse(pool, x3_ready, t)
                stand_alone(pool)
                gp.tensor_copy(x2_res[:], x2[:]).then_inc(x2_kept, 1)

            def qup(t):
                for n in range(4):
                    pool.wait_ge(q_parts, t * 12 + 3 * n + 3)
                    gp.tensor_tensor(q_sb[:, EG * n:EG * n + EG, KVC:KVC + R], q_cos[:, n % 2], q_sin[:, n % 2],
                                     ALU.add).then_inc(q_rot, 1)

            def score(t):
                for b in range(NB):
                    pool.wait_ge(inv_done, t * NB + b + 1)
                    gp.tensor_tensor(probs[:, b], probs[:, b],
                                     row_inv[:, b, :].unsqueeze(2).to_broadcast([P, NP_, KEYS]), ALU.mult)\
                        .then_inc(prob_done, 1)

            def decay_(t):
                pool.wait_ge(a_done, t + 1)
                reuse(pool, decay_sum, t)
                gp.tensor_tensor(decay_in[:], dt8[:, 9, :].unsqueeze(2).to_broadcast([P, NH, L]),
                                 const("upto").unsqueeze(1).to_broadcast([P, NH, L]), ALU.mult)\
                    .then_inc(decay_in_done, 1)

            def conv_(t):
                pool.wait_ge(xh_copied, t + 1)
                reuse(pool, ysq_done, t)
                gp.tensor_tensor(xh_d[:], xh[:], param("d_skip"), ALU.mult).then_inc(xhd_done, 1)

            def scan_out(t):
                rsqrt(3, t, yve_done, yr_done)

            def weigh(g):
                def run(t):
                    if g == 0:
                        pool.wait_ge(ew_done, t + 1)
                    pool.wait_ge(gu_prod, t * G + g + 1)
                    reuse(pool, ht_done, t * G + g - 1)
                    gp.tensor_tensor(h[:, g % 2, :].rearrange("p (e f) -> p e f", e=EG),
                                     gu[:, g % 2, :].rearrange("p (e f) -> p e f", e=EG),
                                     e_w[:, g * EG:(g + 1) * EG].unsqueeze(2).to_broadcast([P, EG, F]), ALU.mult)\
                        .then_inc(h_done, 1)
                return run

            steps = {"ln1": ("a", ln1), "ln2": ("s", ln2), "ln3": ("m", ln3), "qup": ("a", qup),
                     "score": ("a", score), "decay": ("s", decay_), "conv": ("s", conv_), "scan_out": ("s", scan_out)}
            for g in range(G):
                steps[f"gu{g}"] = ("m", weigh(g))
            turns(pool, lambda n, a, s, m: run_order(steps, n, a, s, m))

        @block.vector
        def _(dve):
            v = nc.vector
            dve.wait_ge(s_const, 48)
            v.tensor_copy(same_l[:], const("same_l")).then_inc(s_setup_misc, 1)
            v.tensor_copy(seg_f[:], seg_i[:]).then_inc(s_setup_misc, 1)
            v.tensor_scalar(param("d_skip"), param("d_skip"), 0.5, None, ALU.mult).then_inc(s_setup_misc, 1)
            dve.wait_ge(s_aexp, 1)
            v.tensor_scalar(a_neg[:], a_neg[:], 1e30, -1.0, ALU.min, ALU.mult).then_inc(s_setup_misc, 1)
            dve.wait_ge(s_wsetup, 16 * 13)
            for c in range(XC):
                v.tensor_scalar(wout_sb[:, c, :], wout_sb[:, c, :], param("norm_w")[:, c:c + 1], 0.5,
                                ALU.mult, ALU.mult).then_inc(s_setup_misc, 1)
            for n in range(2):
                dve.wait_ge(s_setup, n + 1)
                v.tensor_copy(wq_sb[:, 8 * n:8 * n + 8, 0:KVC],
                              ps[0:QC, n, :].rearrange("p (h c) -> p h c", h=8)).then_inc(s_setup_ev, 1)
            dve.wait_ge(s_setup, 3)
            v.tensor_copy(wk_sb[:, :, KVC:KVC + R], ps[:, 2, 0:DC * R].rearrange("p (c r) -> p c r", c=DC))\
                .then_inc(s_setup_ev, 1)
            for j in range(NP_):
                dve.wait_ge(s_setup, 4 + j)
                v.tensor_copy(wvo_sb[:, j, :], (ps_g if j % 2 else ps_u)[:, 0:D]).then_inc(s_setup_ev, 1)
            dve.wait_ge(s_setup_ev, 3 + NP_)
            dve.wait_ge(s_setup_misc, 4 + XC)
            dve.wait_ge(s_pad, 1)

            def norm(k, src, t):
                v.bn_stats(stats[:, k, :], src[:]).then_inc(ln_stat[k], 1)
                dve.wait_ge(ln_stat[k], t + 1)
                stand_alone(dve)
                v.bn_aggr(mean_var[:, k, :], stats[:, k, :]).then_inc(ln_mv[k], 1)
                dve.wait_ge(ln_mv[k], t + 1)
                v.tensor_scalar(var_eps[:, k:k + 1], mean_var[:, k, 1:2], LN_EPS, None, ALU.add).then_inc(ln_ve[k], 1)
                dve.wait_ge(ln_rstd[k], t + 1)
                reuse(dve, ln_tr[k], t)
                v.tensor_scalar(xn[:, k, :], src[:], mean_var[:, k, 0:1], rstd[:, k:k + 1], ALU.subtract, ALU.mult)\
                    .then_inc(ln_out[k], 1)

            def kv(t):
                v.tensor_scalar(mask_d[:], const("key_no"), seg_f[:, bass.ds(t, 1)], None, ALU.subtract)\
                    .then_inc(mask_step, 1)
                dve.wait_ge(mask_step, t * 2 + 1)
                v.scalar_tensor_tensor(mask_d[:], mask_d[:], -1.0, mask_d[:], ALU.mult, ALU.max)\
                    .then_inc(mask_step, 1)
                dve.wait_ge(mask_step, t * 2 + 2)
                reuse(dve, score_done, t * NB)
                v.tensor_scalar(mask[:], mask_d[:], LOOKBACK / 2.0, NEG, ALU.is_gt, ALU.mult).then_inc(mask_done, 1)

            def rotate_keys(t):
                dve.wait_ge(k_lat, t + 1)
                src = ps[:, 0, 0:NB * P].rearrange("p (b c) -> p b c", b=NB)
                half = R // 2
                v.tensor_tensor(k_cos[:], src[:, :, KVC:KVC + R], const("cos_k").unsqueeze(1).to_broadcast([P, NB, R]),
                                ALU.mult).then_inc(k_rot_parts, 1)
                for i, j in ((0, 1), (1, 0)):
                    v.tensor_tensor(k_sin[:, :, i * half:(i + 1) * half],
                                    src[:, :, KVC + j * half:KVC + (j + 1) * half],
                                    const("sin_k")[:, i * half:(i + 1) * half].unsqueeze(1)
                                    .to_broadcast([P, NB, half]), ALU.mult).then_inc(k_rot_parts, 1)
                dve.wait_ge(k_rot_parts, t * 3 + 3)
                v.tensor_tensor(k_sb[:, :, KVC:KVC + R], k_cos[:], k_sin[:], ALU.add).then_inc(k_rot, 1)

            def ln1(t):
                dve.wait_ge(s_x, (t + 1) * 16)
                norm(0, x_in, t)
                rotate_keys(t)

            def ln2(t):
                dve.wait_ge(x1_ready, t + 1)
                norm(1, x1, t)

            def ln3(t):
                dve.wait_ge(x2_ready, t + 1)
                norm(2, x2, t)

            def qup(t):
                half = R // 2
                for n in range(4):
                    dve.wait_ge(q_lat, t * 4 + n + 1)
                    reuse(dve, q_rot, t * 4 + n - 1)
                    src = ps[:, n, :].rearrange("p (h c) -> p h c", h=EG)
                    v.tensor_tensor(q_cos[:, n % 2], src[:, :, KVC:KVC + R],
                                    const("cos_q").unsqueeze(1).to_broadcast([P, EG, R]), ALU.mult)\
                        .then_inc(q_parts, 1)
                    for i, j in ((0, 1), (1, 0)):
                        v.tensor_tensor(q_sin[:, n % 2, :, i * half:(i + 1) * half],
                                        src[:, :, KVC + j * half:KVC + (j + 1) * half],
                                        const("sin_q")[:, i * half:(i + 1) * half].unsqueeze(1)
                                        .to_broadcast([P, EG, half]), ALU.mult).then_inc(q_parts, 1)

            def score(t):
                for b in range(NB):
                    dve.wait_ge(score_done, t * NB + b + 1)
                    v.tensor_reduce(neg_max[:, b, :], ps[:, 2 * b:2 * b + 2, :].rearrange("p n (j k) -> p (n j) k", j=4),
                                    AX_X, ALU.max, negate=True).then_inc(max_done, 1)
                for b in range(NB):
                    dve.wait_ge(exp_done, t * 16 + 8 * b + 8)
                    reuse(dve, prob_done, t * NB + b - 1)
                    v.reciprocal(row_inv[:, b, :], row_sum[:, b, :]).then_inc(inv_done, 1)

            def pv(t):
                for b in range(NB):
                    dve.wait_ge(pv_done, t * NB + b + 1)
                    v.tensor_copy(oT[:, :, b, :], ps[:, b, :].rearrange("p (j l) -> p j l", j=NP_)).then_inc(o_copied, 1)

            def attn_out(t):
                dve.wait_ge(ao_done, t + 1)
                dve.wait_ge(s_xres, (t + 1) * 16)
                reuse(dve, ln_out[1], t)
                reuse(dve, x1_kept, t)
                v.tensor_tensor(x1[:], ps[:, 2, 0:D], x_res[:], ALU.add).then_inc(x1_ready, 1)

            def softplus(t):
                raw, absv, u, den, s, q, poly, pos, dt, a = [dt8[:, i, :] for i in range(10)]
                dve.wait_ge(pad_copied, t * 2 + 2)
                reuse(dve, a_done, t)
                v.tensor_tensor(raw, ps[:, 2, 0:NH], param("dt_bias"), ALU.add).then_inc(dt_raw, 1)
                dve.wait_ge(dt_raw, t + 1)
                v.scalar_tensor_tensor(absv, raw, -1.0, raw, ALU.mult, ALU.max).then_inc(dt_abs, 1)
                chain = Steps(dve, dt_step, t, SOFT)
                chain.link(v.tensor_scalar(pos, raw, 0.0, None, ALU.max))
                dve.wait_ge(dt_exp, t + 1)
                chain.link(v.tensor_scalar(den, u, 2.0, None, ALU.add))
                chain.link(v.reciprocal(den, den))
                chain.link(v.tensor_tensor(s, u, den, ALU.mult))
                chain.link(v.tensor_tensor(q, s, s, ALU.mult))
                chain.link(v.tensor_scalar(poly, q, 1.0 / 15, None, ALU.mult))
                for k in (13, 11, 9, 7, 5):
                    chain.link(v.scalar_tensor_tensor(poly, poly, 1.0 / k, q, ALU.add, ALU.mult))
                chain.link(v.scalar_tensor_tensor(poly, poly, 1.0 / 3, q, ALU.add, ALU.mult))
                assert chain.k == SOFT

            def softplus_end(t):
                raw, absv, u, den, s, q, poly, pos, dt, a = [dt8[:, i, :] for i in range(10)]
                chain = Steps(dve, soft_end, t, 2)
                chain.link(v.scalar_tensor_tensor(poly, poly, 1.0, s, ALU.add, ALU.mult))
                chain.link(v.scalar_tensor_tensor(poly, poly, 2.0, pos, ALU.mult, ALU.add))
                reuse(dve, decay_in_done, t)
                v.tensor_tensor(a, poly, a_neg[:], ALU.mult).then_inc(a_done, 1)
                v.tensor_scalar(dt, poly, 0.5, None, ALU.mult).then_inc(dt_done, 1)

            def proj(t):
                softplus(t)
                softplus_end(t)
                dve.wait_ge(zth_done, t + 1)
                v.scalar_tensor_tensor(z_th[:], z_th[:], 1.0, ps[:, 0, :], ALU.add, ALU.mult).then_inc(zsilu_done, 1)

            def decay_(t):
                reuse(dve, xbc_done, t * 2)
                cw = param("conv_w").rearrange("p (c k) -> p c k", c=CH)
                for k in range(TAPS):
                    for c in range(CH):
                        if k == 0 and c in (0, XC):
                            dve.wait_ge(pad_copied, t * 2 + (1 if c == 0 else 2))
                        rows = slice(0, P if c < XC else NS)
                        src = xpad[rows, c, :, k:k + L]
                        if k == 0:
                            ins = v.tensor_scalar(conv[rows, c], src, cw[rows, c, 0:1],
                                                  param("conv_b")[rows, c:c + 1], ALU.mult, ALU.add)
                        else:
                            dve.wait_ge(conv_step, t * TAPS * CH + (k - 1) * CH + c + 1)
                            ins = v.scalar_tensor_tensor(conv[rows, c], src, cw[rows, c, k:k + 1], conv[rows, c],
                                                         ALU.mult, ALU.add)
                        ins.then_inc(conv_step, 1)

            def conv_(t):
                for i, (rows, cs) in enumerate(((slice(0, P), slice(0, XC)), (slice(0, NS), slice(XC, CH)))):
                    dve.wait_ge(cth_done, t * 2 + i + 1)
                    dve.wait_ge(conv_step, t * TAPS * CH + TAPS * CH)
                    v.scalar_tensor_tensor(xbc[rows, cs, :].rearrange("p c t -> p (c t)"),
                                           conv_th[rows, cs].rearrange("p c b l -> p (c b l)"), 1.0,
                                           conv[rows, cs].rearrange("p c b l -> p (c b l)"), ALU.add, ALU.mult)\
                        .then_inc(xbc_done, 1)
                dve.wait_ge(xh_copied, t + 1)
                dve.wait_ge(dt_done, t + 1)
                reuse(dve, y_done, t)
                v.tensor_tensor(xh_dt[:], ps[:, 0, :].rearrange("p (h c) -> p h c", h=NH),
                                dt8[:, 8, :].unsqueeze(2).to_broadcast([P, NH, PH]), ALU.mult).then_inc(xhdt_done, 1)
                dve.wait_ge(gram_done, t + 1)
                v.tensor_tensor(gram[:], ps[:, 1, 0:L], const("upto4"), ALU.mult).then_inc(gram_masked, 1)
                dve.wait_ge(gram_masked, t + 1)
                dve.wait_ge(decay_exp, t + 1)
                v.tensor_tensor(scan_w[:], decay[:], gram[:].unsqueeze(1).to_broadcast([P, NH, L]), ALU.mult)\
                    .then_inc(scanw_done, 1)

            def scan_(t):
                dve.wait_ge(y_done, t + 1)
                dve.wait_ge(xhd_done, t + 1)
                reuse(dve, yt_done, t)
                reuse(dve, ysq_done, t)
                v.tensor_tensor(y_sb[:], ps[:, 2, :], xh_d[:], ALU.add).then_inc(y_skip, 1)
                dve.wait_ge(y_skip, t + 1)
                dve.wait_ge(zsilu_done, t + 1)
                v.tensor_tensor(y_gated[:], y_sb[:], z_th[:], ALU.mult).then_inc(yg_done, 1)

            def scan_out(t):
                dve.wait_ge(ysq_done, t + 1)
                v.tensor_scalar(var_eps[:, 3:4], y_ms[:], 1.0 / DI, LN_EPS, ALU.mult, ALU.add).then_inc(yve_done, 1)
                dve.wait_ge(yr_done, t + 1)
                dve.wait_ge(so_done, t + 1)
                dve.wait_ge(x1_kept, t + 1)
                reuse(dve, ln_out[2], t)
                reuse(dve, x2_kept, t)
                v.scalar_tensor_tensor(x2[:], ps[:, 0, 0:D], rstd[:, 3:4], x1_res[:], ALU.mult, ALU.add)\
                    .then_inc(x2_ready, 1)

            def gate(t):
                dve.wait_ge(lg_done, t + 1)
                v.tensor_copy(logits[:], ps_g[:, 0:E]).then_inc(lg_copied, 1)
                dve.wait_ge(lg_copied, t + 1)
                chain = Steps(dve, gate_step, t, GATE)
                stand_alone(dve)
                chain.link(v.max(top8[:], logits[:]))
                v.tensor_scalar(neg_top[:], top8[:, 0:1], -1.0, None, ALU.mult).then_inc(e_neg, 1)
                chain.link(v.match_replace(struck[:], top8[:], logits[:], -3e38))
                chain.link(v.tensor_tensor(chosen[:], struck[:], logits[:], ALU.not_equal))
                dve.wait_ge(e_exp_done, t + 1)
                chain.link(v.tensor_tensor(e_exp[:], e_exp[:], chosen[:], ALU.mult))
                chain.link(v.tensor_reduce(e_sum[:, 0:1], e_exp[:], AX_X, ALU.add))
                chain.link(v.reciprocal(e_sum[:, 1:2], e_sum[:, 0:1]))
                reuse(dve, h_done, t * G)
                chain.link(v.tensor_scalar(e_w[:], e_exp[:], e_sum[:, 1:2], 0.5, ALU.mult, ALU.mult))
                assert chain.k == GATE
                v.tensor_copy(e_w[:, 0:1], e_w[:, 0:1]).then_inc(ew_done, 1)

            def gate_up(g):
                def run(t):
                    dve.wait_ge(gth_done, t * G + g + 1)
                    reuse(dve, h_done, t * G + g - 1)
                    v.scalar_tensor_tensor(gu[:, g % 2, :], g_th[:, g % 2, :], 1.0, ps_g[:, 0:GW], ALU.add, ALU.mult)\
                        .then_inc(gsilu_done, 1)
                    dve.wait_ge(gsilu_done, t * G + g + 1)
                    v.tensor_tensor(gu[:, g % 2, :], gu[:, g % 2, :], ps_u[:, 0:GW], ALU.mult).then_inc(gu_prod, 1)
                return run

            def moe_out(t):
                dve.wait_ge(down_done, t * G + G)
                dve.wait_ge(x2_kept, t + 1)
                reuse(dve, s_store, t * 16)
                v.tensor_tensor(x3[:], ps_y[:, 0:D], x2_res[:], ALU.add).then_inc(x3_ready, 1)

            steps = {"kv": ("a", kv), "ln1": ("a", ln1), "ln2": ("s", ln2), "ln3": ("m", ln3), "qup": ("a", qup),
                     "score": ("a", score), "pv": ("a", pv), "attn_out": ("a", attn_out), "proj": ("s", proj),
                     "decay": ("s", decay_), "conv": ("s", conv_), "scan": ("s", scan_), "scan_out": ("s", scan_out),
                     "gate": ("m", gate), "moe_out": ("m", moe_out)}
            for g in range(G):
                steps[f"gu{g}"] = ("m", gate_up(g))
            turns(dve, lambda n, a, s, m: run_order(steps, n, a, s, m))


def kernel(x, ctx_2048, itok_BxS_0_1023, L0_xattn_W_kvc, L0_xattn_W_dq, L0_xattn_W_uq, L0_xattn_W_qr, L0_xattn_W_uk,
           L0_xattn_W_kr, L0_xattn_W_uv, L0_xattn_W_o, L0_attn_W_in, L0_attn_conv_w, L0_attn_conv_b, L0_attn_dt_bias,
           L0_attn_A_log, L0_attn_D, L0_attn_norm_w, L0_attn_W_out, L0_ffn_wg, L0_ffn_w1, L0_ffn_v1, L0_ffn_w2):
    import concourse.bacc as bacc
    from concourse.bass_utils import run_bass_kernel_spmd

    def a(v):
        return np.asarray(v)

    def chunks(w):
        w = a(w)
        return w.reshape(-1, P, w.shape[1]).transpose(1, 0, 2)

    pc, pwidth = columns(PARAMS)
    par = np.zeros((P, pwidth), np.float32)
    par[:, slice(*pc["dt_bias"])] = a(L0_attn_dt_bias)[None]
    par[:, slice(*pc["a_log"])] = a(L0_attn_A_log)[None]
    par[:, slice(*pc["d_skip"])] = np.repeat(a(L0_attn_D), PH)[None]
    par[:, slice(*pc["norm_w"])] = a(L0_attn_norm_w).reshape(XC, P).T
    cw = np.zeros((P, CH, TAPS), np.float32)
    cb = np.zeros((P, CH), np.float32)
    for c in range(CH):
        lo, n = (c * P, P) if c < XC else (DI + (c - XC) * NS, NS)
        cw[:n, c] = a(L0_attn_conv_w)[lo:lo + n]
        cb[:n, c] = a(L0_attn_conv_b)[lo:lo + n]
    par[:, slice(*pc["conv_w"])] = cw.reshape(P, -1)
    par[:, slice(*pc["conv_b"])] = cb
    ctxT = a(ctx_2048)[:, :KEYS].reshape(T, NB, KEYS, DC, P).transpose(0, 4, 1, 3, 2).reshape(T * P, NB * DC * KEYS)
    arrays = {
        "xt": a(x).reshape(B * L, D), "ctxT": ctxT, "seg": a(itok_BxS_0_1023).reshape(T, P).T,
        "consts": constants(), "params": par, "w_dq": chunks(L0_xattn_W_dq),
        "w_qr": a(L0_xattn_W_qr).reshape(QC, H, R), "w_uqT": a(L0_xattn_W_uq).reshape(QC, H, HD).transpose(2, 1, 0),
        "w_ukT": a(L0_xattn_W_uk).reshape(KVC, H, HD).transpose(2, 1, 0), "w_kvc": chunks(L0_xattn_W_kvc),
        "w_kvcT": a(L0_xattn_W_kvc).T, "w_kr": a(L0_xattn_W_kr),
        "w_uvT": a(L0_xattn_W_uv).reshape(KVC, H, HD).transpose(2, 1, 0),
        "w_o": a(L0_xattn_W_o).reshape(H, HD, D).transpose(1, 0, 2), "w_in": chunks(a(L0_attn_W_in).T),
        "w_out": chunks(a(L0_attn_W_out).T), "wg": chunks(a(L0_ffn_wg).T),
        "w1": chunks(a(L0_ffn_w1).transpose(1, 0, 2).reshape(D, E * F)).reshape(P, -1),
        "v1": chunks(a(L0_ffn_v1).transpose(1, 0, 2).reshape(D, E * F)).reshape(P, -1),
        "w2": chunks(a(L0_ffn_w2).reshape(E * F, D)).reshape(P, -1),
    }
    arrays = {k: np.ascontiguousarray(w) for k, w in arrays.items()}
    nc = bacc.Bacc("TRN2", target_bir_lowering=False, num_devices=1)
    args = {k: nc.dram_tensor(k, w.shape, mybir.dt.from_np(w.dtype), kind="ExternalInput").ap()
            for k, w in arrays.items()}
    out = nc.dram_tensor("out", (B * L, D), F32, kind="ExternalOutput").ap()
    build(nc, out=out, **args)
    r = run_bass_kernel_spmd(nc, [arrays], core_ids=[0])
    return np.asarray(r.results[0]["out"]).reshape(B, L, D)
```

```python
from contextlib import ExitStack

import numpy as np

import concourse.bass as bass
from concourse import mybir

ALU = mybir.AluOpType
ACT = mybir.ActivationFunctionType
F32 = mybir.dt.float32
BF16 = mybir.dt.bfloat16
I32 = mybir.dt.int32
AX_X = mybir.AxisListType.X

P = 128
B, L, D = 32, 64, 256
NB = P // L
T = B * L // P
DC = D // P
KEYS = 128
LOOKBACK = 8
H, HD = 16, 128
KVC, QC, R = 64, 96, 64
NP_ = H // 2
DI, NH, PH, NS, TAPS = 512, 8, 64, 64, 4
XC = DI // P
CH = XC + 2
E, K8, F = 32, 8, 96
EG = 4
GW = EG * F
G = E // EG
GC = GW // P
NEG = -1e30
SCALE = float(1.0 / np.sqrt(np.float32(HD + R)))
LN_EPS = 1e-5

CONSTS = [("ident", P), ("same_l", P), ("later", P), ("upto", L), ("upto4", L), ("key_no", KEYS),
          ("cos_q", R), ("sin_q", R), ("cos_k", R), ("sin_k", R), ("half", 1)]
PARAMS = [("dt_bias", NH), ("a_log", NH), ("d_skip", DI), ("norm_w", XC), ("conv_w", CH * TAPS), ("conv_b", CH)]


def columns(fields):
    at, out = 0, {}
    for name, width in fields:
        out[name] = (at, at + width)
        at += width
    return out, at


def constants():
    c, width = columns(CONSTS)
    out = np.zeros((P, width), np.float32)
    p = np.arange(P)

    def put(name, values):
        out[:, c[name][0]:c[name][1]] = values

    def rope(pos):
        half = R // 2
        inv = (1.0 / np.float32(10000.0) ** (np.arange(half, dtype=np.float32) / half)).astype(np.float32)
        ang = pos.astype(np.float32)[:, None] * inv
        cos, sin = np.cos(ang), np.sin(ang)
        return np.concatenate([cos, cos], 1), np.concatenate([-sin, sin], 1)

    put("ident", np.eye(P))
    put("same_l", (p[:, None] % L) == (p[None, :] % L))
    put("later", (p[:, None] > p[None, :]) & (p[:, None] // L == p[None, :] // L))
    put("upto", (p[:, None] % L) <= np.arange(L)[None, :])
    put("upto4", 0.25 * ((p[:, None] % L) <= np.arange(L)[None, :]))
    put("key_no", np.arange(KEYS)[None, :] + 4.0)
    cq, sq = rope(p % L)
    ck, sk = rope(p)
    put("cos_q", cq)
    put("sin_q", sq)
    put("cos_k", ck)
    put("sin_k", sk)
    put("half", -0.5)
    return out


ORDER = ["kv", "trb", "trm", "bc", "qc", "xp", "lg", "kt", "gu0", "qup0", "conv0", "z", "qup1", "conv1", "gu1",
         "tr0", "qt0", "conv2", "dn0", "qt1", "conv3", "decay", "gu2", "tr1", "sc0", "cth", "dn1", "xh", "gu3",
         "tr2", "rc0", "sc1", "scan", "dn2", "gu4", "tr3", "scanT", "rc1", "pt0", "dn3", "so", "gu5", "tr4",
         "pt1", "dn4", "pv", "gu6", "tr5", "ao", "dn5", "ln1", "gu7", "tr6", "ln2", "dn6", "ln3", "tr7", "dn7",
         "moe_out"]


def build(nc, xt, ctxT, seg, consts, params, w_dq, w_qr, w_uqT, w_ukT, w_kvc, w_kvcT, w_kr, w_uvT, w_o,
          w_in, w_out, wg, w1, v1, w2, out):
    cc, cwidth = columns(CONSTS)
    pc, pwidth = columns(PARAMS)
    with ExitStack() as ctx:
        def sb(name, shape, dt=F32):
            return ctx.enter_context(nc.sbuf_tensor(name, shape, dt))

        def sem(name):
            return ctx.enter_context(nc.semaphore(name))

        w1_sb = sb("w1_sb", [P, DC, E * F])
        v1_sb = sb("v1_sb", [P, DC, E * F])
        w2_sb = sb("w2_sb", [P, E * F // P, D])
        wg_sb = sb("wg_sb", [P, DC, E])
        wdq_sb = sb("wdq_sb", [P, DC, QC])
        wq_sb = sb("wq_sb", [QC, H, KVC + R])
        wk_sb = sb("wk_sb", [P, DC, KVC + R])
        wvo_sb = sb("wvo_sb", [P, NP_, D])
        win_sb = sb("win_sb", [P, DC, 2 * DI + 2 * NS + NH])
        wout_sb = sb("wout_sb", [P, XC, D])
        wkr_sb = sb("wkr_sb", [KVC, R])
        c_sb = sb("c_sb", [P, cwidth])
        p_sb = sb("p_sb", [P, pwidth])
        same_l = sb("same_l", [P, P], BF16)
        a_neg = sb("a_neg", [P, NH])
        seg_i = sb("seg_i", [P, T], I32)
        seg_f = sb("seg_f", [P, T])

        def const(name):
            return c_sb[:, cc[name][0]:cc[name][1]]

        def param(name):
            return p_sb[:, pc[name][0]:pc[name][1]]

        ident = const("ident")

        x_in = sb("x_in", [P, D])
        ctx_sb = sb("ctx_sb", [P, NB, DC, KEYS])
        x_res = sb("x_res", [P, D])
        x1 = sb("x1", [P, D])
        x2 = sb("x2", [P, D])
        x2_res = sb("x2_res", [P, D])
        x3 = sb("x3", [P, D])
        stats = sb("stats", [P, 3, 6])
        mean_var = sb("mean_var", [P, 3, 2])
        var_eps = sb("var_eps", [P, 4])
        rstd = sb("rstd", [P, 4])
        xn = sb("xn", [P, 3, D])
        xnT = sb("xnT", [P, 3, DC, P])
        qcT = sb("qcT", [QC, P])
        k_sb = sb("k_sb", [KEYS, NB, KVC + R])
        k_cos = sb("k_cos", [KEYS, NB, R])
        k_sin = sb("k_sin", [KEYS, NB, R])
        kT = sb("kT", [KVC + R, NB, KEYS])
        q_sb = sb("q_sb", [P, H, KVC + R])
        q_cos = sb("q_cos", [P, 2, EG, R])
        q_sin = sb("q_sin", [P, 2, EG, R])
        qT = sb("qT", [KVC + R, NB, H, L])
        mask_d = sb("mask_d", [P, KEYS])
        mask = sb("mask", [P, KEYS], BF16)
        neg_max = sb("neg_max", [P, NB, NP_])
        row_sum = sb("row_sum", [P, NB, NP_])
        row_inv = sb("row_inv", [P, NB, NP_])
        probs = sb("probs", [P, NB, NP_, KEYS])
        pT = sb("pT", [KEYS, NB, 2, NP_, L])
        oT = sb("oT", [P, NP_, NB, L])
        z_th = sb("z_th", [P, DI])
        xpad = sb("xpad", [P, CH, NB, TAPS - 1 + L])
        conv = sb("conv", [P, CH, NB, L])
        conv_th = sb("conv_th", [P, CH, NB, L])
        xbc = conv_th[:].rearrange("p c b l -> p c (b l)")
        dt8 = sb("dt8", [P, 10, NH])
        decay_in = sb("decay_in", [P, NH, L])
        decay = sb("decay", [P, NH, L])
        gram = sb("gram", [P, L])
        scan_w = decay
        xh = sb("xh", [P, DI])
        xh_dt = sb("xh_dt", [P, NH, PH])
        xh_d = sb("xh_d", [P, DI])
        y_sb = sb("y_sb", [P, DI])
        y_gated = y_sb
        y_ms = sb("y_ms", [P, 1])
        yT = sb("yT", [P, XC, P])
        logits = sb("logits", [P, E])
        top8 = sb("top8", [P, 8])
        struck = sb("struck", [P, E])
        chosen = sb("chosen", [P, E])
        neg_top = sb("neg_top", [P, 1])
        e_exp = sb("e_exp", [P, E])
        e_sum = sb("e_sum", [P, 2])
        e_w = sb("e_w", [P, E])
        g_th = sb("g_th", [P, 2, GW])
        gu = sb("gu", [P, 2, GW])
        h = sb("h", [P, 2, GW])
        hT = sb("hT", [P, 2, GC, P])

        wkvcT_sb = oT[:].rearrange("p j b l -> p (j b l)")[0:KVC, 0:D]
        wuqT_st = q_sb[:].rearrange("p h c -> p (h c)")[:, 0:H * QC].rearrange("p (h c) -> p h c", h=H)
        wukT_st = qT[:].rearrange("p b h l -> p (b h l)")[:, 0:H * KVC].rearrange("p (h c) -> p h c", h=H)
        wuvT_st = qT[:].rearrange("p b h l -> p (b h l)")[:, H * KVC:2 * H * KVC].rearrange("p (h c) -> p h c", h=H)
        wo_lo = probs[:].rearrange("p b j k -> p (b j k)").rearrange("p (h n) -> p h n", n=D)
        wo_hi = pT[:].rearrange("p b e j l -> p (b e j l)").rearrange("p (h n) -> p h n", n=D)

        ps = ctx.enter_context(nc.psum_tensor("ps", [P, 4, 512], F32))
        ps_g = ctx.enter_context(nc.psum_tensor("ps_g", [P, 512], F32))
        ps_u = ctx.enter_context(nc.psum_tensor("ps_u", [P, 512], F32))
        ps_t = ctx.enter_context(nc.psum_tensor("ps_t", [P, 512], F32))
        ps_y = ctx.enter_context(nc.psum_tensor("ps_y", [P, 512], F32))

        (s_const, s_wsetup, s_wmoe, s_x, s_ctx, s_xres, s_store) = [sem(n) for n in (
            "consts_loaded", "weights_loaded", "expert_weights_loaded", "x_loaded", "ctx_loaded",
            "x_res_loaded", "out_stored")]
        s_setup = sem("setup_products")
        s_setup_ev = sem("setup_copied")
        s_setup_misc = sem("setup_misc")
        s_aexp = sem("a_exp_done")
        s_pad = sem("pads_zeroed")
        ln_stat = [sem(f"ln{k}_stats") for k in range(3)]
        ln_mv = [sem(f"ln{k}_mean_var") for k in range(3)]
        ln_ve = [sem(f"ln{k}_var_eps") for k in range(3)]
        ln_rstd = [sem(f"ln{k}_rstd") for k in range(3)]
        ln_out = [sem(f"ln{k}_normed") for k in range(3)]
        ln_tr = [sem(f"ln{k}_transposed") for k in range(3)]
        ln_T = [sem(f"ln{k}_T_copied") for k in range(3)]
        kv_done = sem("kv_done")
        k_lat = sem("k_latent_copied")
        k_rot_parts = sem("k_rot_parts")
        k_rot = sem("k_rotated")
        kt_done = sem("kT_done")
        kt_copied = sem("kT_copied")
        qc_done = sem("qc_done")
        qc_copied = sem("qc_copied")
        qup_done = sem("q_up_done")
        q_lat = sem("q_latent_copied")
        q_parts = sem("q_rot_parts")
        q_rot = sem("q_rotated")
        qt_done = sem("qT_done")
        qt_copied = sem("qT_copied")
        mask_step = sem("mask_distance")
        mask_done = sem("mask_done")
        score_done = sem("scores_done")
        max_done = sem("max_done")
        exp_done = sem("exp_done")
        inv_done = sem("row_inv_done")
        prob_done = sem("probs_done")
        pt_done = sem("pT_done")
        pt_copied = sem("pT_copied")
        pv_done = sem("pv_done")
        o_copied = sem("oT_copied")
        ao_done = sem("attn_out_done")
        x1_ready = sem("x1_ready")
        z_done = sem("z_done")
        zth_done = sem("z_tanh_done")
        zsilu_done = sem("z_silu_done")
        xpart_done = sem("x_part_done")
        bc_done = sem("dt_bc_done")
        pad_copied = sem("pad_copied")
        dt_raw = sem("dt_biased")
        dt_step = sem("softplus_steps")
        dt_abs = sem("dt_abs_done")
        soft_end = sem("softplus_end")
        dt_exp = sem("dt_exp_done")
        dt_done = sem("dt_done")
        a_done = sem("dt_a_done")
        decay_in_done = sem("decay_in_done")
        decay_sum = sem("decay_sums_done")
        decay_exp = sem("decay_exp_done")
        conv_step = sem("conv_steps")
        cth_done = sem("conv_tanh_done")
        xbc_done = sem("xbc_done")
        xh_tr = sem("xh_transposed")
        xh_copied = sem("xh_copied")
        xhdt_done = sem("xh_dt_done")
        xhd_done = sem("xh_d_done")
        gram_done = sem("gram_done")
        gram_masked = sem("gram_masked")
        scanw_done = sem("scan_w_done")
        y_done = sem("y_done")
        y_skip = sem("y_with_skip")
        yg_done = sem("y_gated_done")
        ysq_done = sem("y_mean_square")
        yve_done = sem("y_var_eps")
        yr_done = sem("y_rstd")
        yt_done = sem("yT_done")
        yt_copied = sem("yT_copied")
        so_done = sem("scan_out_done")
        x2_ready = sem("x2_ready")
        x2_kept = sem("x2_kept")
        lg_done = sem("logits_done")
        lg_copied = sem("logits_copied")
        gate_step = sem("gate_steps")
        e_neg = sem("neg_top_done")
        e_exp_done = sem("gate_exp_done")
        ew_done = sem("expert_weights_done")
        gu_done = sem("gate_up_done")
        gth_done = sem("gate_tanh_done")
        gsilu_done = sem("gate_silu_done")
        gu_prod = sem("gate_up_product")
        h_done = sem("h_done")
        ht_done = sem("hT_done")
        ht_copied = sem("hT_copied")
        down_done = sem("down_done")
        x3_ready = sem("x3_ready")
        passed = sem("waits_passed")
        SOFT, GATE = 12, 7

        def reuse(eng, s, value):
            if not (isinstance(value, int) and value <= 0):
                eng.wait_ge(s, value)

        def stand_alone(eng):
            eng.sem_inc(passed, 1)

        class Steps:
            def __init__(self, eng, s, tile, per):
                self.eng, self.s, self.base, self.per, self.k = eng, s, tile * per, per, 0

            def link(self, ins):
                self.k += 1
                assert self.k <= self.per
                ins.then_inc(self.s, 1)
                self.eng.wait_ge(self.s, self.base + self.k)

        def turns(eng, run):
            run(0, True, False, False)
            run(1, True, True, False)
            run(2, True, True, True)
            with eng.Fori(3, T - 1) as n:
                run(n, True, True, True)
            run(T - 1, True, True, True)
            run(T, False, True, True)
            run(T + 1, False, False, True)

        def run_order(steps, n, attn, scan, moe):
            for name in ORDER:
                chain, fn = steps.get(name, (None, None))
                if fn is None:
                    continue
                if chain == "a" and attn:
                    fn(n)
                if chain == "s" and scan:
                    fn(n - 1)
                if chain == "m" and moe:
                    fn(n - 2)
                if chain == "next" and not (isinstance(n, int) and n + 1 >= T):
                    fn(n + 1)

        block = ctx.enter_context(nc.Block())

        @block.sync
        def _(sp):
            sp.dma_start(c_sb[:], consts).then_inc(s_const, 16)
            sp.dma_start(p_sb[:], params).then_inc(s_const, 16)
            sp.dma_start(seg_i[:], seg).then_inc(s_const, 16)
            n_setup = 0
            for dst, src in ((wuqT_st, w_uqT), (wukT_st, w_ukT), (wq_sb[:, :, KVC:KVC + R], w_qr),
                             (wkvcT_sb, w_kvcT), (wkr_sb[:], w_kr), (wk_sb[:, :, 0:KVC], w_kvc),
                             (wuvT_st, w_uvT), (wo_lo, w_o[:, 0:NP_, :]), (wo_hi, w_o[:, NP_:H, :]),
                             (wdq_sb[:], w_dq), (win_sb[:], w_in), (wout_sb[:], w_out), (wg_sb[:], wg)):
                sp.dma_start(dst, src).then_inc(s_wsetup, 16)
                n_setup += 16

            def load(t):
                reuse(sp, ln_out[0], t)
                sp.dma_start(x_in[:], xt[bass.ts(t, P), :]).then_inc(s_x, 16)
                reuse(sp, kv_done, t)
                sp.dma_start(ctx_sb[:].rearrange("p b c k -> p (b c k)"), ctxT[bass.ts(t, P), :]).then_inc(s_ctx, 16)
                reuse(sp, x1_ready, t)
                sp.dma_start(x_res[:], xt[bass.ts(t, P), :]).then_inc(s_xres, 16)

            def store(t):
                sp.wait_ge(x3_ready, t + 1)
                sp.dma_start(out[bass.ts(t, P), :], x3[:]).then_inc(s_store, 16)

            load(0)
            for dst, src in ((w1_sb, w1), (v1_sb, v1), (w2_sb, w2)):
                sp.dma_start(dst[:].rearrange("p c n -> p (c n)"), src).then_inc(s_wmoe, 16)
            load(1)
            load(2)
            with sp.Fori(2, T - 1) as n:
                load(n + 1)
                store(n - 2)
            store(T - 3)
            store(T - 2)
            store(T - 1)
            sp.wait_ge(s_store, 16 * T)

        @block.tensor
        def _(pe):
            mm = nc.tensor.matmul
            pe.wait_ge(s_const, 48)
            pe.wait_ge(s_wsetup, 16 * 13)
            for hh in range(H):
                ins = mm(ps[0:QC, hh // 8, (hh % 8) * KVC:(hh % 8 + 1) * KVC], wuqT_st[:, hh, :], wukT_st[:, hh, :],
                         start=True, stop=True)
                if hh % 8 == 7:
                    ins.then_inc(s_setup, 1)
            for c in range(DC):
                ins = mm(ps[:, 2, c * R:(c + 1) * R], wkvcT_sb[:, c * P:(c + 1) * P], wkr_sb[:], start=True, stop=True)
            ins.then_inc(s_setup, 1)
            for j in range(NP_):
                if j >= 2:
                    pe.wait_ge(s_setup_ev, 3 + j - 1)
                for e in range(2):
                    hh = 2 * j + e
                    wo = wo_lo if hh < NP_ else wo_hi
                    ins = mm((ps_g if j % 2 else ps_u)[e * KVC:(e + 1) * KVC, 0:D],
                             wuvT_st[:, hh, :], wo[:, hh % NP_, :], start=True, stop=True)
                ins.then_inc(s_setup, 1)
            pe.wait_ge(s_setup_ev, 3 + NP_)
            pe.wait_ge(s_setup_misc, 3)

            def transpose_in(k, t, bank):
                pe.wait_ge(ln_out[k], t + 1)
                for c in range(DC):
                    ins = nc.tensor.transpose(bank[:, c * P:(c + 1) * P], xn[:, k, c * P:(c + 1) * P], ident)
                ins.then_inc(ln_tr[k], 1)

            def kv(t):
                reuse(pe, x1_ready, t)
                pe.wait_ge(s_ctx, (t + 1) * 16)
                for b in range(NB):
                    for c in range(DC):
                        ins = mm(ps[:, 0, b * P:(b + 1) * P], ctx_sb[:, b, c, :], wk_sb[:, c, :],
                                 start=(c == 0), stop=(c == DC - 1))
                ins.then_inc(kv_done, 1)
                transpose_in(0, t, ps[:, 0, D:])

            def qc(t):
                pe.wait_ge(ln_T[0], t + 1)
                for c in range(DC):
                    ins = mm(ps[0:QC, 1, 0:P], wdq_sb[:, c, :], xnT[:, 0, c, :], start=(c == 0), stop=(c == DC - 1))
                ins.then_inc(qc_done, 1)

            def kt(t):
                pe.wait_ge(k_rot, t + 1)
                for b in range(NB):
                    ins = nc.tensor.transpose(ps[:, 0, b * P:(b + 1) * P], k_sb[:, b, :], ident)
                ins.then_inc(kt_done, 1)

            def q_up(pair):
                def run(t):
                    for n in (2 * pair, 2 * pair + 1):
                        if n == 0:
                            pe.wait_ge(qc_copied, t + 1)
                        elif n == 1:
                            pe.wait_ge(kt_copied, t + 1)
                        else:
                            pe.wait_ge(q_parts, t * 12 + 3 * (n - 1))
                        mm(ps[:, 1 - n % 2, :], qcT[:], wq_sb[:, EG * n:EG * n + EG, :], start=True, stop=True)\
                            .then_inc(qup_done, 1)
                return run

            def q_transpose(pair):
                def run(t):
                    for n in (2 * pair, 2 * pair + 1):
                        if pair == 0:
                            pe.wait_ge(q_parts, t * 12 + 3 * (n + 3))
                            pe.wait_ge(q_rot, t * 4 + n + 1)
                        else:
                            pe.wait_ge(qt_copied, t * 4 + n - 1)
                            pe.wait_ge(q_rot, t * 4 + n + 1)
                        for hh in range(4):
                            ins = nc.tensor.transpose(ps[:, 1 - n % 2, hh * P:(hh + 1) * P], q_sb[:, 4 * n + hh, :],
                                                      ident)
                        ins.then_inc(qt_done, 1)
                return run

            def score(b):
                def run(t):
                    if b == 0:
                        pe.wait_ge(mask_done, t + 1)
                        pe.wait_ge(qt_copied, t * 4 + 4)
                    else:
                        pe.wait_ge(exp_done, t * 16 + 8)
                    own = slice(b * L, (b + 1) * L)
                    for half in range(2):
                        bank = ps[:, half, :]
                        mm(bank, same_l[own, :], mask[own, :].unsqueeze(1).to_broadcast([L, 4, KEYS]),
                           start=True, stop=False)
                        for j in range(4):
                            jj = 4 * half + j
                            ins = mm(bank[:, j * KEYS:(j + 1) * KEYS], qT[:, b, 2 * jj:2 * jj + 2, :], kT[:, b, :],
                                     start=False, stop=(j == 3))
                    ins.then_inc(score_done, 1)
                return run

            def p_transpose(b):
                def run(t):
                    if b == 0:
                        pe.wait_ge(exp_done, t * 16 + 16)
                    else:
                        pe.wait_ge(pt_copied, t * 4 + 2)
                    pe.wait_ge(prob_done, t * NB + b + 1)
                    for half in range(2):
                        for j in range(4):
                            ins = nc.tensor.transpose(ps[:, half, j * P:(j + 1) * P], probs[:, b, 4 * half + j, :],
                                                      ident)
                        ins.then_inc(pt_done, 1)
                return run

            def pv(t):
                pe.wait_ge(pt_copied, t * 4 + 4)
                for b in range(NB):
                    for e in range(2):
                        ins = mm(ps[e * KVC:(e + 1) * KVC, b, :], k_sb[:, b, 0:KVC], pT[:, b, e, :, :],
                                 start=True, stop=True)
                    ins.then_inc(pv_done, 1)

            def attn_out(t):
                pe.wait_ge(o_copied, t * NB + NB)
                for j in range(NP_):
                    ins = mm(ps[:, 0, 0:D], oT[:, j, :, :], wvo_sb[:, j, :], start=(j == 0), stop=(j == NP_ - 1))
                ins.then_inc(ao_done, 1)

            def trb(t):
                reuse(pe, yt_copied, t)
                transpose_in(1, t, ps[:, 2, :])

            def bc(t):
                pe.wait_ge(ln_T[1], t + 1)
                reuse(pe, x2_ready, t)
                for c in range(DC):
                    mm(ps[:, 3, 0:NH], xnT[:, 1, c, :], win_sb[:, c, 2 * DI + 2 * NS:2 * DI + 2 * NS + NH],
                       start=(c == 0), stop=(c == DC - 1))
                for m in range(2):
                    at = 2 * DI + m * NS
                    for c in range(DC):
                        ins = mm(ps[0:NS, 3, (m + 1) * P:(m + 2) * P], win_sb[:, c, at:at + NS], xnT[:, 1, c, :],
                                 start=(c == 0), stop=(c == DC - 1))
                ins.then_inc(bc_done, 1)

            def xp(t):
                for m in range(XC):
                    for c in range(DC):
                        ins = mm(ps[:, 2, m * P:(m + 1) * P], win_sb[:, c, DI + m * P:DI + (m + 1) * P],
                                 xnT[:, 1, c, :], start=(c == 0), stop=(c == DC - 1))
                ins.then_inc(xpart_done, 1)

            def z(t):
                pe.wait_ge(dt_raw, t + 1)
                for c in range(DC):
                    ins = mm(ps[:, 3, :], xnT[:, 1, c, :], win_sb[:, c, 0:DI], start=(c == 0), stop=(c == DC - 1))
                ins.then_inc(z_done, 1)

            def decay_(t):
                pe.wait_ge(pad_copied, t * 2 + 2)
                pe.wait_ge(decay_in_done, t + 1)
                mm(ps[:, 2, :], const("later"), decay_in[:], start=True, stop=True).then_inc(decay_sum, 1)

            def xh_(t):
                pe.wait_ge(zsilu_done, t + 1)
                pe.wait_ge(xbc_done, t * 2 + 2)
                for c in range(XC):
                    ins = nc.tensor.transpose(ps[:, 3, c * P:(c + 1) * P], xbc[:, c, :], ident)
                ins.then_inc(xh_tr, 1)
                pe.wait_ge(decay_exp, t + 1)
                for b in range(NB):
                    own = slice(b * L, (b + 1) * L)
                    if b == 0:
                        stand_alone(pe)
                    ins = mm(ps[own, 2, 0:L], xbc[0:NS, XC, own], xbc[0:NS, XC + 1, own], start=True, stop=True)
                ins.then_inc(gram_done, 1)

            def scan_(t):
                pe.wait_ge(scanw_done, t + 1)
                pe.wait_ge(xhdt_done, t + 1)
                stand_alone(pe)
                for b in range(NB):
                    own = slice(b * L, (b + 1) * L)
                    for hh in range(NH):
                        ins = mm(ps[own, 3, hh * PH:(hh + 1) * PH], scan_w[own, hh, :], xh_dt[own, hh, :],
                                 start=True, stop=True)
                ins.then_inc(y_done, 1)

            def scanT(t):
                pe.wait_ge(yg_done, t + 1)
                for c in range(XC):
                    ins = nc.tensor.transpose(ps[:, 2, c * P:(c + 1) * P], y_gated[:, c * P:(c + 1) * P], ident)
                ins.then_inc(yt_done, 1)

            def scan_out(t):
                pe.wait_ge(yt_copied, t + 1)
                for c in range(XC):
                    ins = mm(ps[:, 3, 0:D], yT[:, c, :], wout_sb[:, c, :], start=(c == 0), stop=(c == XC - 1))
                ins.then_inc(so_done, 1)

            def trm(t):
                if isinstance(t, int) and t == 0:
                    pe.wait_ge(s_wmoe, 48)
                reuse(pe, ht_copied, t * G)
                transpose_in(2, t, ps_t)

            def lg(t):
                pe.wait_ge(ln_T[2], t + 1)
                reuse(pe, gu_prod, t * G)
                for c in range(DC):
                    ins = mm(ps_g[:, 0:E], xnT[:, 2, c, :], wg_sb[:, c, :], start=(c == 0), stop=(c == DC - 1))
                ins.then_inc(lg_done, 1)

            def gate_up(g):
                def run(t):
                    if g == 0:
                        pe.wait_ge(lg_copied, t + 1)
                    else:
                        pe.wait_ge(gu_prod, t * G + g)
                    for w, bank in ((w1_sb, ps_g), (v1_sb, ps_u)):
                        for c in range(DC):
                            ins = mm(bank[:, 0:GW], xnT[:, 2, c, :], w[:, c, g * GW:(g + 1) * GW],
                                     start=(c == 0), stop=(c == DC - 1))
                    ins.then_inc(gu_done, 1)
                return run

            def h_transpose(g):
                def run(t):
                    if g == 0:
                        pe.wait_ge(ln_T[2], t + 1)
                    else:
                        pe.wait_ge(ht_copied, t * G + g)
                    pe.wait_ge(h_done, t * G + g + 1)
                    for c in range(GC):
                        ins = nc.tensor.transpose(ps_t[:, c * P:(c + 1) * P], h[:, g % 2, c * P:(c + 1) * P], ident)
                    ins.then_inc(ht_done, 1)
                return run

            def down(g):
                def run(t):
                    if g == 0:
                        reuse(pe, x3_ready, t)
                    pe.wait_ge(ht_copied, t * G + g + 1)
                    for c in range(GC):
                        ins = mm(ps_y[:, 0:D], hT[:, g % 2, c, :], w2_sb[:, g * GC + c, :],
                                 start=(g == 0 and c == 0), stop=(g == G - 1 and c == GC - 1))
                    ins.then_inc(down_done, 1)
                return run

            steps = {"kv": ("a", kv), "qc": ("a", qc), "kt": ("a", kt), "pv": ("a", pv), "ao": ("a", attn_out),
                     "trb": ("s", trb), "bc": ("s", bc), "xp": ("s", xp), "z": ("s", z), "decay": ("s", decay_),
                     "xh": ("s", xh_), "scan": ("s", scan_), "scanT": ("s", scanT), "so": ("s", scan_out),
                     "trm": ("m", trm), "lg": ("m", lg)}
            for i in range(2):
                steps |= {f"qup{i}": ("a", q_up(i)), f"qt{i}": ("a", q_transpose(i)), f"sc{i}": ("a", score(i)),
                          f"pt{i}": ("a", p_transpose(i))}
            for g in range(G):
                steps |= {f"gu{g}": ("m", gate_up(g)), f"tr{g}": ("m", h_transpose(g)), f"dn{g}": ("m", down(g))}
            turns(pe, lambda n, a, s, m: run_order(steps, n, a, s, m))

        @block.scalar
        def _(act):
            fn = nc.scalar.activation
            act.wait_ge(s_const, 48)
            fn(a_neg[:], param("a_log"), ACT.Exp).then_inc(s_aexp, 1)

            def copy_T(k, t, bank):
                act.wait_ge(ln_tr[k], t + 1)
                fn(xnT[:, k, :, :], bank[:, 0:D], ACT.Copy).then_inc(ln_T[k], 1)

            def kv(t):
                act.wait_ge(kv_done, t + 1)
                act.wait_ge(ln_tr[0], t + 1)
                fn(k_sb[:, :, 0:KVC], ps[:, 0, 0:NB * P].rearrange("p (b c) -> p b c", b=NB)[:, :, 0:KVC],
                   ACT.Copy).then_inc(k_lat, 1)
                copy_T(0, t, ps[:, 0, D:])

            def qc(t):
                act.wait_ge(qc_done, t + 1)
                fn(qcT[:], ps[0:QC, 1, 0:P], ACT.Copy).then_inc(qc_copied, 1)

            def kt(t):
                act.wait_ge(kt_done, t + 1)
                fn(kT[:], ps[:, 0, 0:NB * P].rearrange("p (b k) -> p b k", b=NB), ACT.Copy).then_inc(kt_copied, 1)

            def q_up(pair):
                def run(t):
                    for n in (2 * pair, 2 * pair + 1):
                        act.wait_ge(qup_done, t * 4 + n + 1)
                        fn(q_sb[:, EG * n:EG * n + EG, 0:KVC],
                           ps[:, 1 - n % 2, :].rearrange("p (h c) -> p h c", h=EG)[:, :, 0:KVC], ACT.Copy)\
                            .then_inc(q_lat, 1)
                return run

            def q_transpose(pair):
                def run(t):
                    for n in (2 * pair, 2 * pair + 1):
                        act.wait_ge(qt_done, t * 4 + n + 1)
                        fn(qT[:, :, 4 * n:4 * n + 4, :].rearrange("p b h l -> p h b l"),
                           ps[:, 1 - n % 2, :].rearrange("p (h b l) -> p h b l", h=4, b=NB), ACT.Copy, scale=SCALE)\
                            .then_inc(qt_copied, 1)
                return run

            def score(b):
                def run(t):
                    act.wait_ge(max_done, t * NB + b + 1)
                    for j in range(NP_):
                        fn(probs[:, b, j, :], ps[:, j // 4, (j % 4) * KEYS:(j % 4 + 1) * KEYS], ACT.Exp,
                           bias=neg_max[:, b, j:j + 1], accum_out=row_sum[:, b, j:j + 1]).then_inc(exp_done, 1)
                return run

            def p_transpose(b):
                def run(t):
                    for half in range(2):
                        act.wait_ge(pt_done, t * 4 + 2 * b + half + 1)
                        fn(pT[:, b, :, 4 * half:4 * half + 4, :].rearrange("p e j l -> p j e l"),
                           ps[:, half, :].rearrange("p (j e l) -> p j e l", j=4, e=2), ACT.Copy)\
                            .then_inc(pt_copied, 1)
                return run

            def trb(t):
                copy_T(1, t, ps[:, 2, :])

            def bc(t):
                act.wait_ge(bc_done, t + 1)
                reuse(act, conv_step, t * TAPS * CH)
                fn(xpad[0:NS, XC:CH, :, TAPS - 1:],
                   ps[0:NS, 3, P:3 * P].rearrange("p (c b l) -> p c b l", c=2, b=NB), ACT.Copy).then_inc(pad_copied, 1)

            def xp(t):
                act.wait_ge(xpart_done, t + 1)
                fn(xpad[:, 0:XC, :, TAPS - 1:], ps[:, 2, :].rearrange("p (c b l) -> p c b l", c=XC, b=NB),
                   ACT.Copy).then_inc(pad_copied, 1)
                act.wait_ge(dt_abs, t + 1)
                fn(dt8[:, 2, :], dt8[:, 1, :], ACT.Exp, scale=-1.0).then_inc(dt_exp, 1)

            def z(t):
                act.wait_ge(z_done, t + 1)
                reuse(act, yg_done, t)
                fn(z_th[:], ps[:, 3, :], ACT.Tanh, scale=0.5).then_inc(zth_done, 1)

            def decay_(t):
                act.wait_ge(decay_sum, t + 1)
                reuse(act, y_done, t)
                fn(decay[:].rearrange("p h l -> p (h l)"), ps[:, 2, :], ACT.Exp).then_inc(decay_exp, 1)

            def cth(t):
                act.wait_ge(conv_step, t * TAPS * CH + TAPS * CH)
                reuse(act, xh_tr, t)
                reuse(act, gram_done, t)
                fn(conv_th[:, 0:XC], conv[:, 0:XC], ACT.Tanh, scale=0.5).then_inc(cth_done, 1)
                fn(conv_th[0:NS, XC:CH], conv[0:NS, XC:CH], ACT.Tanh, scale=0.5).then_inc(cth_done, 1)

            def xh_(t):
                act.wait_ge(xh_tr, t + 1)
                reuse(act, xhd_done, t)
                fn(xh[:], ps[:, 3, :], ACT.Copy).then_inc(xh_copied, 1)

            def scanT(t):
                act.wait_ge(yt_done, t + 1)
                fn(yT[:].rearrange("p c t -> p (c t)"), ps[:, 2, :], ACT.Copy).then_inc(yt_copied, 1)
                reuse(act, yve_done, t)
                fn(xh_d[:], y_gated[:], ACT.Square, scale=0.5, accum_out=y_ms[:]).then_inc(ysq_done, 1)

            def trm(t):
                copy_T(2, t, ps_t)

            def lg(t):
                act.wait_ge(e_neg, t + 1)
                fn(e_exp[:], logits[:], ACT.Exp, bias=neg_top[:]).then_inc(e_exp_done, 1)

            def gate_up(g):
                def run(t):
                    act.wait_ge(gu_done, t * G + g + 1)
                    reuse(act, gsilu_done, t * G + g - 1)
                    fn(g_th[:, g % 2, :], ps_g[:, 0:GW], ACT.Tanh, scale=0.5).then_inc(gth_done, 1)
                return run

            def h_transpose(g):
                def run(t):
                    act.wait_ge(ht_done, t * G + g + 1)
                    reuse(act, down_done, t * G + g - 1)
                    fn(hT[:, g % 2, :, :], ps_t[:, 0:GW], ACT.Copy).then_inc(ht_copied, 1)
                return run

            steps = {"kv": ("a", kv), "qc": ("a", qc), "kt": ("a", kt), "trb": ("s", trb), "bc": ("s", bc),
                     "xp": ("s", xp), "z": ("s", z), "decay": ("s", decay_), "cth": ("s", cth), "xh": ("s", xh_),
                     "scanT": ("s", scanT), "trm": ("m", trm), "lg": ("m", lg)}
            for i in range(2):
                steps |= {f"qup{i}": ("a", q_up(i)), f"qt{i}": ("a", q_transpose(i)), f"sc{i}": ("a", score(i)),
                          f"pt{i}": ("a", p_transpose(i))}
            for g in range(G):
                steps |= {f"gu{g}": ("m", gate_up(g)), f"tr{g}": ("m", h_transpose(g))}
            turns(act, lambda n, a, s, m: run_order(steps, n, a, s, m))

        @block.gpsimd
        def _(pool):
            gp = nc.gpsimd
            gp.memset(xpad[:], 0.0).then_inc(s_pad, 1)
            pool.wait_ge(s_const, 48)

            def rsqrt(k, t, ready, done):
                pool.wait_ge(ready, t + 1)
                gp.tensor_tensor(rstd[:, k:k + 1], var_eps[:, k:k + 1], const("half"), ALU.pow).then_inc(done, 1)

            def ln1(t):
                rsqrt(0, t, ln_ve[0], ln_rstd[0])

            def ln2(t):
                rsqrt(1, t, ln_ve[1], ln_rstd[1])

            def ln3(t):
                rsqrt(2, t, ln_ve[2], ln_rstd[2])

            def keep(t):
                pool.wait_ge(x2_ready, t + 1)
                reuse(pool, x3_ready, t)
                stand_alone(pool)
                gp.tensor_copy(x2_res[:], x2[:]).then_inc(x2_kept, 1)

            def q_up(pair):
                def run(t):
                    for n in (2 * pair, 2 * pair + 1):
                        pool.wait_ge(q_parts, t * 12 + 3 * n + 3)
                        gp.tensor_tensor(q_sb[:, EG * n:EG * n + EG, KVC:KVC + R], q_cos[:, n % 2], q_sin[:, n % 2],
                                         ALU.add).then_inc(q_rot, 1)
                return run

            def normalise(b):
                def run(t):
                    pool.wait_ge(inv_done, t * NB + b + 1)
                    gp.tensor_tensor(probs[:, b], probs[:, b],
                                     row_inv[:, b, :].unsqueeze(2).to_broadcast([P, NP_, KEYS]), ALU.mult)\
                        .then_inc(prob_done, 1)
                return run

            def z(t):
                pool.wait_ge(a_done, t + 1)
                reuse(pool, decay_sum, t)
                gp.tensor_tensor(decay_in[:], dt8[:, 9, :].unsqueeze(2).to_broadcast([P, NH, L]),
                                 const("upto").unsqueeze(1).to_broadcast([P, NH, L]), ALU.mult)\
                    .then_inc(decay_in_done, 1)

            def xh_(t):
                pool.wait_ge(xh_copied, t + 1)
                reuse(pool, ysq_done, t)
                gp.tensor_tensor(xh_d[:], xh[:], param("d_skip"), ALU.mult).then_inc(xhd_done, 1)

            def scanT(t):
                rsqrt(3, t, yve_done, yr_done)

            def weigh(g):
                def run(t):
                    if g == 0:
                        pool.wait_ge(ew_done, t + 1)
                    pool.wait_ge(gu_prod, t * G + g + 1)
                    reuse(pool, ht_done, t * G + g - 1)
                    gp.tensor_tensor(h[:, g % 2, :].rearrange("p (e f) -> p e f", e=EG),
                                     gu[:, g % 2, :].rearrange("p (e f) -> p e f", e=EG),
                                     e_w[:, g * EG:(g + 1) * EG].unsqueeze(2).to_broadcast([P, EG, F]), ALU.mult)\
                        .then_inc(h_done, 1)
                return run

            steps = {"kv": ("m", keep), "ln1": ("next", ln1), "ln2": ("a", ln2), "ln3": ("s", ln3), "z": ("s", z),
                     "xh": ("s", xh_), "scanT": ("s", scanT)}
            for i in range(2):
                steps |= {f"qup{i}": ("a", q_up(i)), f"rc{i}": ("a", normalise(i))}
            for g in range(G):
                steps[f"gu{g}"] = ("m", weigh(g))
            ln1(0)
            turns(pool, lambda n, a, s, m: run_order(steps, n, a, s, m))

        @block.vector
        def _(dve):
            v = nc.vector
            dve.wait_ge(s_const, 48)
            v.tensor_copy(same_l[:], const("same_l")).then_inc(s_setup_misc, 1)
            v.tensor_copy(seg_f[:], seg_i[:]).then_inc(s_setup_misc, 1)
            v.tensor_scalar(param("d_skip"), param("d_skip"), 0.5, None, ALU.mult).then_inc(s_setup_misc, 1)
            dve.wait_ge(s_aexp, 1)
            v.tensor_scalar(a_neg[:], a_neg[:], 1e30, -1.0, ALU.min, ALU.mult).then_inc(s_setup_misc, 1)
            dve.wait_ge(s_wsetup, 16 * 13)
            for c in range(XC):
                v.tensor_scalar(wout_sb[:, c, :], wout_sb[:, c, :], param("norm_w")[:, c:c + 1], 0.5,
                                ALU.mult, ALU.mult).then_inc(s_setup_misc, 1)
            for n in range(2):
                dve.wait_ge(s_setup, n + 1)
                v.tensor_copy(wq_sb[:, 8 * n:8 * n + 8, 0:KVC],
                              ps[0:QC, n, :].rearrange("p (h c) -> p h c", h=8)).then_inc(s_setup_ev, 1)
            dve.wait_ge(s_setup, 3)
            v.tensor_copy(wk_sb[:, :, KVC:KVC + R], ps[:, 2, 0:DC * R].rearrange("p (c r) -> p c r", c=DC))\
                .then_inc(s_setup_ev, 1)
            for j in range(NP_):
                dve.wait_ge(s_setup, 4 + j)
                v.tensor_copy(wvo_sb[:, j, :], (ps_g if j % 2 else ps_u)[:, 0:D]).then_inc(s_setup_ev, 1)
            dve.wait_ge(s_setup_ev, 3 + NP_)
            dve.wait_ge(s_setup_misc, 4 + XC)
            dve.wait_ge(s_pad, 1)

            def norm(k, src, t):
                v.bn_stats(stats[:, k, :], src[:]).then_inc(ln_stat[k], 1)
                dve.wait_ge(ln_stat[k], t + 1)
                stand_alone(dve)
                v.bn_aggr(mean_var[:, k, :], stats[:, k, :]).then_inc(ln_mv[k], 1)
                dve.wait_ge(ln_mv[k], t + 1)
                v.tensor_scalar(var_eps[:, k:k + 1], mean_var[:, k, 1:2], LN_EPS, None, ALU.add).then_inc(ln_ve[k], 1)
                dve.wait_ge(ln_rstd[k], t + 1)
                reuse(dve, ln_tr[k], t)
                v.tensor_scalar(xn[:, k, :], src[:], mean_var[:, k, 0:1], rstd[:, k:k + 1], ALU.subtract, ALU.mult)\
                    .then_inc(ln_out[k], 1)

            def kv(t):
                v.tensor_scalar(mask_d[:], const("key_no"), seg_f[:, bass.ds(t, 1)], None, ALU.subtract)\
                    .then_inc(mask_step, 1)
                dve.wait_ge(mask_step, t * 2 + 1)
                v.scalar_tensor_tensor(mask_d[:], mask_d[:], -1.0, mask_d[:], ALU.mult, ALU.max)\
                    .then_inc(mask_step, 1)
                dve.wait_ge(mask_step, t * 2 + 2)
                reuse(dve, score_done, t * NB)
                v.tensor_scalar(mask[:], mask_d[:], LOOKBACK / 2.0, NEG, ALU.is_gt, ALU.mult).then_inc(mask_done, 1)

            def rotate_keys(t):
                dve.wait_ge(ln_T[0], t + 1)
                src = ps[:, 0, 0:NB * P].rearrange("p (b c) -> p b c", b=NB)
                half = R // 2
                v.tensor_tensor(k_cos[:], src[:, :, KVC:KVC + R], const("cos_k").unsqueeze(1).to_broadcast([P, NB, R]),
                                ALU.mult).then_inc(k_rot_parts, 1)
                for i, j in ((0, 1), (1, 0)):
                    v.tensor_tensor(k_sin[:, :, i * half:(i + 1) * half],
                                    src[:, :, KVC + j * half:KVC + (j + 1) * half],
                                    const("sin_k")[:, i * half:(i + 1) * half].unsqueeze(1)
                                    .to_broadcast([P, NB, half]), ALU.mult).then_inc(k_rot_parts, 1)
                dve.wait_ge(k_rot_parts, t * 3 + 3)
                v.tensor_tensor(k_sb[:, :, KVC:KVC + R], k_cos[:], k_sin[:], ALU.add).then_inc(k_rot, 1)

            def ln1(t):
                dve.wait_ge(s_x, (t + 1) * 16)
                norm(0, x_in, t)

            def ln2(t):
                dve.wait_ge(x1_ready, t + 1)
                norm(1, x1, t)

            def ln3(t):
                dve.wait_ge(x2_ready, t + 1)
                norm(2, x2, t)

            def q_up(pair):
                def run(t):
                    half = R // 2
                    for n in (2 * pair, 2 * pair + 1):
                        dve.wait_ge(q_lat, t * 4 + n + 1)
                        reuse(dve, q_rot, t * 4 + n - 1)
                        src = ps[:, 1 - n % 2, :].rearrange("p (h c) -> p h c", h=EG)
                        v.tensor_tensor(q_cos[:, n % 2], src[:, :, KVC:KVC + R],
                                        const("cos_q").unsqueeze(1).to_broadcast([P, EG, R]), ALU.mult)\
                            .then_inc(q_parts, 1)
                        for i, j in ((0, 1), (1, 0)):
                            v.tensor_tensor(q_sin[:, n % 2, :, i * half:(i + 1) * half],
                                            src[:, :, KVC + j * half:KVC + (j + 1) * half],
                                            const("sin_q")[:, i * half:(i + 1) * half].unsqueeze(1)
                                            .to_broadcast([P, EG, half]), ALU.mult).then_inc(q_parts, 1)
                return run

            def score(b):
                def run(t):
                    dve.wait_ge(score_done, t * NB + b + 1)
                    v.tensor_reduce(neg_max[:, b, :], ps[:, 0:2, :].rearrange("p n (j k) -> p (n j) k", j=4),
                                    AX_X, ALU.max, negate=True).then_inc(max_done, 1)
                return run

            def invert(b):
                def run(t):
                    dve.wait_ge(exp_done, t * 16 + 8 * b + 8)
                    reuse(dve, prob_done, t * NB + b - 1)
                    v.reciprocal(row_inv[:, b, :], row_sum[:, b, :]).then_inc(inv_done, 1)
                return run

            def pv(t):
                for b in range(NB):
                    dve.wait_ge(pv_done, t * NB + b + 1)
                    v.tensor_copy(oT[:, :, b, :], ps[:, b, :].rearrange("p (j l) -> p j l", j=NP_)).then_inc(o_copied, 1)

            def attn_out(t):
                dve.wait_ge(ao_done, t + 1)
                dve.wait_ge(s_xres, (t + 1) * 16)
                v.tensor_tensor(x1[:], ps[:, 0, 0:D], x_res[:], ALU.add).then_inc(x1_ready, 1)

            def softplus(t):
                raw, absv, u, den, s, q, poly, pos, dt, a = [dt8[:, i, :] for i in range(10)]
                dve.wait_ge(pad_copied, t * 2 + 1)
                reuse(dve, a_done, t)
                v.tensor_tensor(raw, ps[:, 3, 0:NH], param("dt_bias"), ALU.add).then_inc(dt_raw, 1)
                dve.wait_ge(dt_raw, t + 1)
                v.scalar_tensor_tensor(absv, raw, -1.0, raw, ALU.mult, ALU.max).then_inc(dt_abs, 1)

            def softplus_rest(t):
                raw, absv, u, den, s, q, poly, pos, dt, a = [dt8[:, i, :] for i in range(10)]
                chain = Steps(dve, dt_step, t, SOFT)
                chain.link(v.tensor_scalar(pos, raw, 0.0, None, ALU.max))
                dve.wait_ge(dt_exp, t + 1)
                chain.link(v.tensor_scalar(den, u, 2.0, None, ALU.add))
                chain.link(v.reciprocal(den, den))
                chain.link(v.tensor_tensor(s, u, den, ALU.mult))
                chain.link(v.tensor_tensor(q, s, s, ALU.mult))
                chain.link(v.tensor_scalar(poly, q, 1.0 / 15, None, ALU.mult))
                for k in (13, 11, 9, 7, 5):
                    chain.link(v.scalar_tensor_tensor(poly, poly, 1.0 / k, q, ALU.add, ALU.mult))
                chain.link(v.scalar_tensor_tensor(poly, poly, 1.0 / 3, q, ALU.add, ALU.mult))
                assert chain.k == SOFT

            def softplus_end(t):
                raw, absv, u, den, s, q, poly, pos, dt, a = [dt8[:, i, :] for i in range(10)]
                chain = Steps(dve, soft_end, t, 2)
                chain.link(v.scalar_tensor_tensor(poly, poly, 1.0, s, ALU.add, ALU.mult))
                chain.link(v.scalar_tensor_tensor(poly, poly, 2.0, pos, ALU.mult, ALU.add))
                reuse(dve, decay_in_done, t)
                v.tensor_tensor(a, poly, a_neg[:], ALU.mult).then_inc(a_done, 1)
                v.tensor_scalar(dt, poly, 0.5, None, ALU.mult).then_inc(dt_done, 1)

            def z(t):
                softplus_rest(t)
                softplus_end(t)
                dve.wait_ge(zth_done, t + 1)
                v.scalar_tensor_tensor(z_th[:], z_th[:], 1.0, ps[:, 3, :], ALU.add, ALU.mult).then_inc(zsilu_done, 1)

            def tap(k):
                def run(t):
                    cw = param("conv_w").rearrange("p (c k) -> p c k", c=CH)
                    if k == 0:
                        dve.wait_ge(pad_copied, t * 2 + 2)
                        reuse(dve, cth_done, t * 2)
                    for c in range(CH):
                        rows = slice(0, P if c < XC else NS)
                        src = xpad[rows, c, :, k:k + L]
                        if k == 0:
                            ins = v.tensor_scalar(conv[rows, c], src, cw[rows, c, 0:1],
                                                  param("conv_b")[rows, c:c + 1], ALU.mult, ALU.add)
                        else:
                            dve.wait_ge(conv_step, t * TAPS * CH + (k - 1) * CH + c + 1)
                            ins = v.scalar_tensor_tensor(conv[rows, c], src, cw[rows, c, k:k + 1], conv[rows, c],
                                                         ALU.mult, ALU.add)
                        ins.then_inc(conv_step, 1)
                return run

            def cth(t):
                for i, (rows, cs) in enumerate(((slice(0, P), slice(0, XC)), (slice(0, NS), slice(XC, CH)))):
                    dve.wait_ge(cth_done, t * 2 + i + 1)
                    v.scalar_tensor_tensor(xbc[rows, cs, :].rearrange("p c t -> p (c t)"),
                                           conv_th[rows, cs].rearrange("p c b l -> p (c b l)"), 1.0,
                                           conv[rows, cs].rearrange("p c b l -> p (c b l)"), ALU.add, ALU.mult)\
                        .then_inc(xbc_done, 1)

            def xh_(t):
                dve.wait_ge(xh_copied, t + 1)
                dve.wait_ge(dt_done, t + 1)
                reuse(dve, y_done, t)
                v.tensor_tensor(xh_dt[:], ps[:, 3, :].rearrange("p (h c) -> p h c", h=NH),
                                dt8[:, 8, :].unsqueeze(2).to_broadcast([P, NH, PH]), ALU.mult).then_inc(xhdt_done, 1)
                dve.wait_ge(gram_done, t + 1)
                v.tensor_tensor(gram[:], ps[:, 2, 0:L], const("upto4"), ALU.mult).then_inc(gram_masked, 1)
                dve.wait_ge(gram_masked, t + 1)
                dve.wait_ge(decay_exp, t + 1)
                v.tensor_tensor(scan_w[:], decay[:], gram[:].unsqueeze(1).to_broadcast([P, NH, L]), ALU.mult)\
                    .then_inc(scanw_done, 1)

            def scan_(t):
                dve.wait_ge(y_done, t + 1)
                dve.wait_ge(xhd_done, t + 1)
                reuse(dve, yt_done, t)
                reuse(dve, ysq_done, t)
                v.tensor_tensor(y_sb[:], ps[:, 3, :], xh_d[:], ALU.add).then_inc(y_skip, 1)
                dve.wait_ge(y_skip, t + 1)
                dve.wait_ge(zsilu_done, t + 1)
                v.tensor_tensor(y_gated[:], y_sb[:], z_th[:], ALU.mult).then_inc(yg_done, 1)

            def scanT(t):
                dve.wait_ge(ysq_done, t + 1)
                v.tensor_scalar(var_eps[:, 3:4], y_ms[:], 1.0 / DI, LN_EPS, ALU.mult, ALU.add).then_inc(yve_done, 1)

            def scan_out(t):
                dve.wait_ge(yr_done, t + 1)
                dve.wait_ge(so_done, t + 1)
                reuse(dve, x2_kept, t)
                v.scalar_tensor_tensor(x2[:], ps[:, 3, 0:D], rstd[:, 3:4], x1[:], ALU.mult, ALU.add)\
                    .then_inc(x2_ready, 1)

            def lg(t):
                dve.wait_ge(lg_done, t + 1)
                v.tensor_copy(logits[:], ps_g[:, 0:E]).then_inc(lg_copied, 1)
                dve.wait_ge(lg_copied, t + 1)
                chain = Steps(dve, gate_step, t, GATE)
                stand_alone(dve)
                chain.link(v.max(top8[:], logits[:]))
                v.tensor_scalar(neg_top[:], top8[:, 0:1], -1.0, None, ALU.mult).then_inc(e_neg, 1)
                chain.link(v.match_replace(struck[:], top8[:], logits[:], -3e38))
                chain.link(v.tensor_tensor(chosen[:], struck[:], logits[:], ALU.not_equal))
                dve.wait_ge(e_exp_done, t + 1)
                chain.link(v.tensor_tensor(e_exp[:], e_exp[:], chosen[:], ALU.mult))
                chain.link(v.tensor_reduce(e_sum[:, 0:1], e_exp[:], AX_X, ALU.add))
                chain.link(v.reciprocal(e_sum[:, 1:2], e_sum[:, 0:1]))
                reuse(dve, h_done, t * G)
                chain.link(v.tensor_scalar(e_w[:], e_exp[:], e_sum[:, 1:2], 0.5, ALU.mult, ALU.mult))
                assert chain.k == GATE
                v.tensor_copy(e_w[:, 0:1], e_w[:, 0:1]).then_inc(ew_done, 1)

            def gate_up(g):
                def run(t):
                    dve.wait_ge(gth_done, t * G + g + 1)
                    reuse(dve, h_done, t * G + g - 1)
                    v.scalar_tensor_tensor(gu[:, g % 2, :], g_th[:, g % 2, :], 1.0, ps_g[:, 0:GW], ALU.add, ALU.mult)\
                        .then_inc(gsilu_done, 1)
                    dve.wait_ge(gsilu_done, t * G + g + 1)
                    v.tensor_tensor(gu[:, g % 2, :], gu[:, g % 2, :], ps_u[:, 0:GW], ALU.mult).then_inc(gu_prod, 1)
                return run

            def moe_out(t):
                dve.wait_ge(down_done, t * G + G)
                dve.wait_ge(x2_kept, t + 1)
                reuse(dve, s_store, t * 16)
                v.tensor_tensor(x3[:], ps_y[:, 0:D], x2_res[:], ALU.add).then_inc(x3_ready, 1)

            def kv_all(t):
                kv(t)
                rotate_keys(t)

            steps = {"kv": ("a", kv_all), "ln1": ("next", ln1), "ln2": ("a", ln2), "ln3": ("s", ln3), "pv": ("a", pv),
                     "ao": ("a", attn_out), "bc": ("s", softplus), "z": ("s", z), "cth": ("s", cth), "xh": ("s", xh_),
                     "scan": ("s", scan_), "scanT": ("s", scanT), "so": ("s", scan_out), "lg": ("m", lg),
                     "moe_out": ("m", moe_out)}
            for i in range(2):
                steps |= {f"qup{i}": ("a", q_up(i)), f"sc{i}": ("a", score(i)), f"rc{i}": ("a", invert(i))}
            for k in range(TAPS):
                steps[f"conv{k}"] = ("s", tap(k))
            for g in range(G):
                steps[f"gu{g}"] = ("m", gate_up(g))
            ln1(0)
            turns(dve, lambda n, a, s, m: run_order(steps, n, a, s, m))


def kernel(x, ctx_2048, itok_BxS_0_1023, L0_xattn_W_kvc, L0_xattn_W_dq, L0_xattn_W_uq, L0_xattn_W_qr, L0_xattn_W_uk,
           L0_xattn_W_kr, L0_xattn_W_uv, L0_xattn_W_o, L0_attn_W_in, L0_attn_conv_w, L0_attn_conv_b, L0_attn_dt_bias,
           L0_attn_A_log, L0_attn_D, L0_attn_norm_w, L0_attn_W_out, L0_ffn_wg, L0_ffn_w1, L0_ffn_v1, L0_ffn_w2):
    import concourse.bacc as bacc
    from concourse.bass_utils import run_bass_kernel_spmd

    def a(v):
        return np.asarray(v)

    def chunks(w):
        w = a(w)
        return w.reshape(-1, P, w.shape[1]).transpose(1, 0, 2)

    pc, pwidth = columns(PARAMS)
    par = np.zeros((P, pwidth), np.float32)
    par[:, slice(*pc["dt_bias"])] = a(L0_attn_dt_bias)[None]
    par[:, slice(*pc["a_log"])] = a(L0_attn_A_log)[None]
    par[:, slice(*pc["d_skip"])] = np.repeat(a(L0_attn_D), PH)[None]
    par[:, slice(*pc["norm_w"])] = a(L0_attn_norm_w).reshape(XC, P).T
    cw = np.zeros((P, CH, TAPS), np.float32)
    cb = np.zeros((P, CH), np.float32)
    for c in range(CH):
        lo, n = (c * P, P) if c < XC else (DI + (c - XC) * NS, NS)
        cw[:n, c] = a(L0_attn_conv_w)[lo:lo + n]
        cb[:n, c] = a(L0_attn_conv_b)[lo:lo + n]
    par[:, slice(*pc["conv_w"])] = cw.reshape(P, -1)
    par[:, slice(*pc["conv_b"])] = cb
    ctxT = a(ctx_2048)[:, :KEYS].reshape(T, NB, KEYS, DC, P).transpose(0, 4, 1, 3, 2).reshape(T * P, NB * DC * KEYS)
    arrays = {
        "xt": a(x).reshape(B * L, D), "ctxT": ctxT, "seg": a(itok_BxS_0_1023).reshape(T, P).T,
        "consts": constants(), "params": par, "w_dq": chunks(L0_xattn_W_dq),
        "w_qr": a(L0_xattn_W_qr).reshape(QC, H, R), "w_uqT": a(L0_xattn_W_uq).reshape(QC, H, HD).transpose(2, 1, 0),
        "w_ukT": a(L0_xattn_W_uk).reshape(KVC, H, HD).transpose(2, 1, 0), "w_kvc": chunks(L0_xattn_W_kvc),
        "w_kvcT": a(L0_xattn_W_kvc).T, "w_kr": a(L0_xattn_W_kr),
        "w_uvT": a(L0_xattn_W_uv).reshape(KVC, H, HD).transpose(2, 1, 0),
        "w_o": a(L0_xattn_W_o).reshape(H, HD, D).transpose(1, 0, 2), "w_in": chunks(a(L0_attn_W_in).T),
        "w_out": chunks(a(L0_attn_W_out).T), "wg": chunks(a(L0_ffn_wg).T),
        "w1": chunks(a(L0_ffn_w1).transpose(1, 0, 2).reshape(D, E * F)).reshape(P, -1),
        "v1": chunks(a(L0_ffn_v1).transpose(1, 0, 2).reshape(D, E * F)).reshape(P, -1),
        "w2": chunks(a(L0_ffn_w2).reshape(E * F, D)).reshape(P, -1),
    }
    arrays = {k: np.ascontiguousarray(w) for k, w in arrays.items()}
    nc = bacc.Bacc("TRN2", target_bir_lowering=False, num_devices=1)
    args = {k: nc.dram_tensor(k, w.shape, mybir.dt.from_np(w.dtype), kind="ExternalInput").ap()
            for k, w in arrays.items()}
    out = nc.dram_tensor("out", (B * L, D), F32, kind="ExternalOutput").ap()
    build(nc, out=out, **args)
    r = run_bass_kernel_spmd(nc, [arrays], core_ids=[0])
    return np.asarray(r.results[0]["out"]).reshape(B, L, D)
```

```python
from contextlib import ExitStack

import numpy as np

import concourse.bass as bass
from concourse import mybir

ALU = mybir.AluOpType
ACT = mybir.ActivationFunctionType
F32 = mybir.dt.float32
BF16 = mybir.dt.bfloat16
I32 = mybir.dt.int32
AX_X = mybir.AxisListType.X

P = 128
B, L, D = 32, 64, 256
NB = P // L
T = B * L // P
DC = D // P
KEYS = 128
ALL_KEYS = 1601
NKC = -(-ALL_KEYS // KEYS)
LAST = ALL_KEYS - (NKC - 1) * KEYS
LOOKBACK = 8
H, HD = 16, 128
KVC, QC, R = 64, 96, 64
HG = 4
NP_ = H // 2
DI, NH, PH, NS, TAPS = 512, 8, 64, 64, 4
XC = DI // P
CH = XC + 2
E, K8, F = 32, 8, 96
EG = 4
GW = EG * F
G = E // EG
GC = GW // P
NEG = -1e30
SCALE = float(1.0 / np.sqrt(np.float32(HD + R)))
LN_EPS = 1e-5

CONSTS = [("ident", P), ("later", P), ("upto", L), ("upto4", L), ("key_no", KEYS),
          ("cos_qT", L), ("sin_qT", L), ("cos_k", R), ("sin_k", R), ("half", 1),
          ("one", 1)]
PARAMS = [("dt_bias", NH), ("a_log", NH), ("d_skip", DI), ("norm_w", XC), ("conv_w", CH * TAPS), ("conv_b", CH)]


def columns(fields):
    at, out = 0, {}
    for name, width in fields:
        out[name] = (at, at + width)
        at += width
    return out, at


def constants():
    c, width = columns(CONSTS)
    out = np.zeros((P, width), np.float32)
    p = np.arange(P)

    def put(name, values):
        out[:, c[name][0]:c[name][1]] = values

    def rope(pos):
        half = R // 2
        inv = (1.0 / np.float32(10000.0) ** (np.arange(half, dtype=np.float32) / half)).astype(np.float32)
        ang = pos.astype(np.float32)[:, None] * inv
        cos, sin = np.cos(ang), np.sin(ang)
        return np.concatenate([cos, cos], 1), np.concatenate([-sin, sin], 1)

    put("ident", np.eye(P))
    put("later", (p[:, None] > p[None, :]) & (p[:, None] // L == p[None, :] // L))
    put("upto", (p[:, None] % L) <= np.arange(L)[None, :])
    put("upto4", 0.25 * ((p[:, None] % L) <= np.arange(L)[None, :]))
    put("key_no", np.arange(KEYS)[None, :] + 4.0)
    cq, sq = rope(np.arange(L))
    ck, sk = rope(p)
    half = R // 2
    put("cos_qT", np.concatenate([np.zeros((KVC, L)), SCALE * cq.T]))
    put("sin_qT", np.concatenate([np.zeros((KVC, L)), SCALE * sq.T[half:], SCALE * sq.T[:half]]))
    put("cos_k", ck)
    put("sin_k", sk)
    put("half", -0.5)
    put("one", 1.0)
    key_tables = np.concatenate(rope(np.arange(NKC * KEYS)), 1).astype(np.float32)
    key_row = np.ascontiguousarray(np.broadcast_to(np.arange(NKC * KEYS, dtype=np.float32) + 4.0, (P, NKC * KEYS)))
    return out, key_tables, key_row


ORDER = ["kv", "trm", "lg", "trb", "qc", "gu0", "kt", "qup0", "bc", "gu1", "tr0", "qup1", "xp", "gu2", "dn0",
         "tr1", "z", "gu3", "tr2", "conv0", "sc0", "dn1", "tr3", "sc1", "rc0", "conv1", "conv2", "gu4", "rc1", "dn2",
         "decay", "pt0", "conv3", "cth", "dn3", "gu5", "tr4", "pt1", "xh", "dn4", "gu6", "pv", "tr5", "scan", "ln1",
         "gu7", "tr6", "scanT", "dn5", "so", "ln3", "tr7", "wide", "ao", "dn6", "ln2", "dn7", "moe_out"]
FIRST_ORDER = ["kv", "trb", "qc", "bc", "kt", "qup0", "qup1", "xp", "conv0", "conv1", "conv2", "sc0", "conv3",
               "sc1", "rc0", "z", "rc1", "cth", "pt0", "decay", "xh", "pt1", "scan", "pv", "scanT", "ln1", "so", "ln3",
               "wide", "ao", "ln2"]
CLOSING_ORDER = ["trm", "trb", "lg", "kv", "gu0", "bc", "xp", "gu1", "tr0", "z", "gu2", "conv0",
                 "conv1", "conv2", "dn0", "tr1", "decay", "gu3", "tr2", "dn1", "conv3", "cth", "gu4", "tr3", "dn2",
                 "xh", "gu5", "scan", "tr4", "dn3", "gu6", "dn4", "tr5", "scanT", "gu7", "dn5", "tr6", "so", "ln3",
                 "tr7", "dn6", "dn7", "moe_out"]
LAST_ORDER = ["kv", "trm", "lg", "gu0", "gu1", "tr0"]
LAST_ORDER += [f"{step}{g - back}" for g in range(2, G) for step, back in (("gu", 0), ("tr", 1), ("dn", 2))]
LAST_ORDER += [f"dn{G - 2}", f"tr{G - 1}", f"dn{G - 1}", "moe_out"]


def build(nc, xt, ctxT, seg, consts, key_tables, key_row, params, w_dq, w_qr, w_uqT, w_ukT, w_kvc, w_kvcT, w_kr,
          w_uvT, w_o, w_in, w_out, wg, w1, v1, w2, out):
    cc, cwidth = columns(CONSTS)
    pc, pwidth = columns(PARAMS)
    with ExitStack() as ctx:
        def sb(name, shape, dt=F32):
            return ctx.enter_context(nc.sbuf_tensor(name, shape, dt))

        def sem(name):
            return ctx.enter_context(nc.semaphore(name))

        w1_sb = sb("w1_sb", [P, DC, E * F])
        v1_sb = sb("v1_sb", [P, DC, E * F])
        w2_sb = sb("w2_sb", [P, E * F // P, D])
        wg_sb = sb("wg_sb", [P, DC, E])
        wdq_sb = sb("wdq_sb", [P, DC, QC])
        wq_sb = sb("wq_sb", [QC, H, KVC + R])
        wk_sb = sb("wk_sb", [P, DC, KVC + R])
        wvo_sb = sb("wvo_sb", [P, NP_, D])
        win_sb = sb("win_sb", [P, DC, 2 * DI + 2 * NS + NH])
        wout_sb = sb("wout_sb", [P, XC, D])
        wkr_sb = sb("wkr_sb", [KVC, R])
        c_sb = sb("c_sb", [P, cwidth])
        p_sb = sb("p_sb", [P, pwidth])
        a_neg = sb("a_neg", [P, NH])
        seg_i = sb("seg_i", [P, T * NB], I32)
        seg_f = sb("seg_f", [P, T * NB])

        def const(name):
            return c_sb[:, cc[name][0]:cc[name][1]]

        def param(name):
            return p_sb[:, pc[name][0]:pc[name][1]]

        ident = const("ident")

        x_in = sb("x_in", [P, D])
        ctx_sb = sb("ctx_sb", [P, NB, DC, KEYS])
        x_res = sb("x_res", [P, D])
        x1 = sb("x1", [P, D])
        x2 = sb("x2", [P, D])
        x2_res = sb("x2_res", [P, D])
        x3 = sb("x3", [P, D])
        stats = sb("stats", [P, 3, 6])
        mean_var = sb("mean_var", [P, 3, 2])
        var_eps = sb("var_eps", [P, 4])
        rstd = sb("rstd", [P, 4])
        xn = sb("xn", [P, 3, D])
        xnT = sb("xnT", [P, 3, DC, P])
        qcT = sb("qcT", [QC, P])
        k_sb = sb("k_sb", [KEYS, NB, KVC + R])
        k_cos = sb("k_cos", [KEYS, NB, R])
        k_sin = sb("k_sin", [KEYS, NB, R])
        kT = sb("kT", [KVC + R, NB, KEYS])
        q_rotary = sb("q_rotary", [P, 4, HG * P])
        q_cos, q_sin = q_rotary[:, 0:2, :], q_rotary[:, 2:4, :]
        qT = sb("qT", [KVC + R, NB, H, L])
        mask = sb("mask", [P, NB, KEYS])
        neg_max = sb("neg_max", [P, NB, NP_])
        row_sum = sb("row_sum", [P, NB, NP_])
        row_inv = sb("row_inv", [P, NB, NP_])
        probs = sb("probs", [P, NB, NP_, KEYS])
        pT = sb("pT", [KEYS, NB, 2, NP_, L])
        oT = sb("oT", [P, NP_, NB, L])
        scan_a = sb("scan_a", [P, 4, DI])
        scan_b = sb("scan_b", [P, 4, DI])
        z_th = scan_b[:, 0, :]
        xpad = sb("xpad", [P, CH, NB, TAPS - 1 + L])
        conv = sb("conv", [P, CH, NB, L])
        conv_th = sb("conv_th", [P, CH, NB, L])
        xbc = conv_th[:].rearrange("p c b l -> p c (b l)")
        dt8 = sb("dt8", [P, 10, NH])
        decay_in = scan_a[:, 0, :].rearrange("p (h l) -> p h l", h=NH)
        decay = scan_a[:, 1, :].rearrange("p (h l) -> p h l", h=NH)
        gram = sb("gram", [P, L])
        scan_w = decay
        xh = scan_a[:, 2, :]
        xh_d = scan_a[:, 3, :]
        xh_dt = scan_b[:, 1, :].rearrange("p (h c) -> p h c", h=NH)
        y_sb = scan_b[:, 2, :]
        y_gated = y_sb
        y_ms = sb("y_ms", [P, 1])
        yT = scan_b[:, 3, :].rearrange("p (c t) -> p c t", c=XC)
        logits = sb("logits", [P, E])
        top8 = sb("top8", [P, 8])
        struck = sb("struck", [P, E])
        chosen = sb("chosen", [P, E])
        neg_top = sb("neg_top", [P, 1])
        e_exp = sb("e_exp", [P, E])
        e_sum = sb("e_sum", [P, 2])
        e_w = sb("e_w", [P, E])
        g_th = sb("g_th", [P, 2, GW])
        gu = sb("gu", [P, 2, GW])
        h = sb("h", [P, 2, GW])
        hT = sb("hT", [P, 2, GC, P])

        wide_kT = scan_a[:].rearrange("p a n -> p (a n)")
        wide_mask = scan_b[:].rearrange("p a n -> p (a n)")
        wide_k = q_rotary[:].rearrange("p a n -> p (a n)").rearrange("p (c n) -> p c n", n=KVC + R)
        wide_p = probs[:].rearrange("p b j k -> p (b j k)")
        wide_pT = pT[:].rearrange("p b e j l -> p (b e j l)").rearrange("p (c q) -> p c q", q=P)
        conv_flat = conv[:].rearrange("p c b l -> p (c b l)")
        wide_ctx = conv_flat[:, 0:DC * KEYS].rearrange("p (c k) -> p c k", c=DC)
        wide_table = conv_flat[:, DC * KEYS:DC * KEYS + 2 * R]
        wide_stage = conv_flat[:, 4 * P:5 * P]
        wide_q = conv_flat[:, 5 * P:6 * P]
        wide_cos = conv_th[:].rearrange("p c b l -> p (c b l)")[:, 0:R]
        wide_sin = conv_th[:].rearrange("p c b l -> p (c b l)")[:, R:2 * R]
        wide_col = sb("wide_col", [P, 3])
        seg_out = sb("seg_out", [P, 2])
        wide_flag = sb("wide_flag", [1, 1], I32)

        wkvcT_sb = oT[:].rearrange("p j b l -> p (j b l)")[0:KVC, 0:D]
        wuqT_st = q_rotary[:].rearrange("p h c -> p (h c)")[:, 0:H * QC].rearrange("p (h c) -> p h c", h=H)
        wukT_st = qT[:].rearrange("p b h l -> p (b h l)")[:, 0:H * KVC].rearrange("p (h c) -> p h c", h=H)
        w1_flat = w1_sb[:].rearrange("p c n -> p (c n)")
        wuvT_st = w1_flat[:, 0:H * KVC].rearrange("p (h c) -> p h c", h=H)
        wo_st = w1_flat[:, H * KVC:H * (KVC + D)].rearrange("p (h n) -> p h n", n=D)

        ps = ctx.enter_context(nc.psum_tensor("ps", [P, 4, 512], F32))
        ps_g = ctx.enter_context(nc.psum_tensor("ps_g", [P, 512], F32))
        ps_u = ctx.enter_context(nc.psum_tensor("ps_u", [P, 512], F32))
        ps_t = ctx.enter_context(nc.psum_tensor("ps_t", [P, 512], F32))
        ps_y = ctx.enter_context(nc.psum_tensor("ps_y", [P, 512], F32))

        (s_const, s_wquery, s_wsetup, s_wvalue, s_wscan, s_wmoe, s_x, s_ctx, s_xres, s_store) = [sem(n) for n in (
            "consts_loaded", "query_weights_loaded", "attention_weights_loaded", "value_weights_loaded",
            "scan_weights_loaded", "expert_weights_loaded", "x_loaded", "ctx_loaded",
            "x_res_loaded", "out_stored")]
        s_setup = sem("setup_products")
        s_setup_ev = sem("setup_copied")
        s_setup_misc = sem("setup_misc")
        s_value = sem("value_products")
        s_value_ev = sem("value_copied")
        s_wout = sem("w_out_scaled")
        s_aexp = sem("a_exp_done")
        s_pad = sem("pads_zeroed")
        ln_stat = [sem(f"ln{k}_stats") for k in range(3)]
        ln_mv = [sem(f"ln{k}_mean_var") for k in range(3)]
        ln_ve = [sem(f"ln{k}_var_eps") for k in range(3)]
        ln_rstd = [sem(f"ln{k}_rstd") for k in range(3)]
        ln_out = [sem(f"ln{k}_normed") for k in range(3)]
        ln_tr = [sem(f"ln{k}_transposed") for k in range(3)]
        ln_T = [sem(f"ln{k}_T_copied") for k in range(3)]
        kv_done = sem("kv_done")
        k_lat = sem("k_latent_copied")
        k_rot_parts = sem("k_rot_parts")
        k_rot = sem("k_rotated")
        kt_done = sem("kT_done")
        kt_copied = sem("kT_copied")
        qc_done = sem("qc_done")
        qc_copied = sem("qc_copied")
        qup_done = sem("q_up_done")
        q_lat = sem("q_latent_copied")
        q_parts = sem("q_rot_parts")
        q_rot = sem("q_rotated")
        mask_step = sem("mask_distance")
        masked = sem("scores_masked")
        mask_done = sem("mask_done")
        score_done = sem("scores_done")
        max_done = sem("max_done")
        exp_done = sem("exp_done")
        inv_done = sem("row_inv_done")
        prob_done = sem("probs_done")
        pt_done = sem("pT_done")
        pt_copied = sem("pT_copied")
        pv_done = sem("pv_done")
        o_copied = sem("oT_copied")
        ao_done = sem("attn_out_done")
        x1_ready = sem("x1_ready")
        z_done = sem("z_done")
        zth_done = sem("z_tanh_done")
        zsilu_done = sem("z_silu_done")
        xpart_done = sem("x_part_done")
        bc_done = sem("dt_bc_done")
        pad_copied = sem("pad_copied")
        dt_raw = sem("dt_biased")
        dt_step = sem("softplus_steps")
        dt_abs = sem("dt_abs_done")
        soft_end = sem("softplus_end")
        dt_exp = sem("dt_exp_done")
        dt_done = sem("dt_done")
        a_done = sem("dt_a_done")
        decay_in_done = sem("decay_in_done")
        decay_sum = sem("decay_sums_done")
        decay_exp = sem("decay_exp_done")
        conv_first = sem("conv_first_tap")
        conv_step = sem("conv_steps")
        cth_done = sem("conv_tanh_done")
        xbc_done = sem("xbc_done")
        xh_tr = sem("xh_transposed")
        xh_copied = sem("xh_copied")
        xhdt_done = sem("xh_dt_done")
        xhd_done = sem("xh_d_done")
        gram_done = sem("gram_done")
        gram_masked = sem("gram_masked")
        scanw_done = sem("scan_w_done")
        y_done = sem("y_done")
        y_skip = sem("y_with_skip")
        yg_done = sem("y_gated_done")
        ysq_done = sem("y_mean_square")
        yve_done = sem("y_var_eps")
        yr_done = sem("y_rstd")
        yt_done = sem("yT_done")
        yt_copied = sem("yT_copied")
        so_done = sem("scan_out_done")
        x2_ready = sem("x2_ready")
        x2_kept = sem("x2_kept")
        lg_done = sem("logits_done")
        lg_copied = sem("logits_copied")
        gate_step = sem("gate_steps")
        e_neg = sem("neg_top_done")
        e_exp_done = sem("gate_exp_done")
        ew_done = sem("expert_weights_done")
        gu_done = sem("gate_up_done")
        gth_done = sem("gate_tanh_done")
        gsilu_done = sem("gate_silu_done")
        gu_prod = sem("gate_up_product")
        h_done = sem("h_done")
        ht_done = sem("hT_done")
        ht_copied = sem("hT_copied")
        down_done = sem("down_done")
        x3_ready = sem("x3_ready")
        passed = sem("waits_passed")
        seg_fold = sem("seg_distance")
        seg_step = sem("seg_range_steps")
        flag_sum = sem("wide_flag_summed")
        flag_ready = sem("wide_flag_ready")
        w_row = sem("wide_key_row_loaded")
        w_mask = sem("wide_mask_steps")
        w_masked = sem("wide_scores_masked")
        w_loaded = sem("wide_ctx_loaded")
        w_kdone = sem("wide_keys_done")
        w_klat = sem("wide_latent_copied")
        w_kpart = sem("wide_rot_parts")
        w_krot = sem("wide_keys_rotated")
        w_kturn = sem("wide_keys_transposed")
        w_kT = sem("wide_kT_copied")
        w_q = sem("wide_q_copied")
        w_score = sem("wide_scores_done")
        w_max = sem("wide_max_done")
        w_exp = sem("wide_exp_done")
        w_inv = sem("wide_inv_done")
        w_prob = sem("wide_probs_done")
        w_pturn = sem("wide_probs_transposed")
        w_pT = sem("wide_pT_copied")
        w_pv = sem("wide_pv_done")
        w_attn = sem("wide_o_copied")
        SOFT, GATE = 12, 7

        def reuse(eng, s, value):
            if not (isinstance(value, int) and value <= 0):
                eng.wait_ge(s, value)

        def stand_alone(eng):
            eng.sem_inc(passed, 1)

        class Steps:
            def __init__(self, eng, s, tile, per):
                self.eng, self.s, self.base, self.per, self.k = eng, s, tile * per, per, 0

            def link(self, ins):
                self.k += 1
                assert self.k <= self.per
                ins.then_inc(self.s, 1)
                self.eng.wait_ge(self.s, self.base + self.k)

        def turns(eng, run):
            run(0, True, False, False)
            run(1, True, True, False)
            run(2, True, True, True)
            with eng.Fori(3, T - 1) as n:
                run(n, True, True, True)
            run(T - 1, True, True, True)
            run(T, False, True, True)
            run(T + 1, False, False, True)

        def run_order(steps, n, attn, scan, moe):
            order = (FIRST_ORDER if not moe else ORDER if attn else CLOSING_ORDER if scan else LAST_ORDER)
            for name in order:
                chain, fn = steps.get(name, (None, None))
                if fn is None:
                    continue
                if chain == "a" and attn:
                    fn(n)
                if chain == "s" and scan:
                    fn(n - 1)
                if chain == "m" and moe:
                    fn(n - 2)
                if chain == "next" and not (isinstance(n, int) and n + 1 >= T):
                    fn(n + 1)

        def read_flag(eng):
            eng.wait_ge(flag_ready, 1)
            return eng.value_load(wide_flag[0:1, 0:1], min_val=0, max_val=P)

        def attention_over(t):
            return isinstance(t, int) and t >= T - 2

        def gate_up_banks(t, g):
            return (ps[:, 0, :], ps[:, 1, :]) if attention_over(t) and g % 2 else (ps_g, ps_u)

        value_banks = (ps_g, ps_u, ps_t, ps_y)
        VB = len(value_banks)
        assert NP_ == 2 * VB

        block = ctx.enter_context(nc.Block())

        @block.sync
        def _(sp):
            for dst, src in ((wuqT_st, w_uqT), (wukT_st, w_ukT)):
                sp.dma_start(dst, src).then_inc(s_wquery, 16)
            sp.dma_start(c_sb[:], consts).then_inc(s_const, 16)
            sp.dma_start(p_sb[:], params).then_inc(s_const, 16)
            sp.dma_start(seg_i[:], seg).then_inc(s_const, 16)
            for dst, src in ((wq_sb[:, :, KVC:KVC + R], w_qr), (wkvcT_sb, w_kvcT), (wkr_sb[:], w_kr),
                             (wk_sb[:, :, 0:KVC], w_kvc),
                             (wdq_sb[:], w_dq)):
                sp.dma_start(dst, src).then_inc(s_wsetup, 16)

            def load(t):
                reuse(sp, ln_out[0], t)
                sp.dma_start(x_in[:], xt[bass.ts(t, P), :]).then_inc(s_x, 16)
                reuse(sp, kv_done, t)
                sp.dma_start(ctx_sb[:].rearrange("p b c k -> p (b c k)"), ctxT[bass.ds(t * NKC * P, P), :])\
                    .then_inc(s_ctx, 16)
                reuse(sp, x1_ready, t)
                sp.dma_start(x_res[:], xt[bass.ts(t, P), :]).then_inc(s_xres, 16)

            def store(t):
                sp.wait_ge(x3_ready, t + 1)
                sp.dma_start(out[bass.ts(t, P), :], x3[:]).then_inc(s_store, 16)

            load(0)
            sp.dma_start(wuvT_st, w_uvT).then_inc(s_wvalue, 16)
            sp.dma_start(wo_st, w_o).then_inc(s_wvalue, 16)
            for dst, src in ((win_sb, w_in), (wout_sb, w_out), (wg_sb, wg)):
                sp.dma_start(dst[:], src).then_inc(s_wscan, 16)
            for dst, src in ((v1_sb, v1), (w2_sb, w2)):
                sp.dma_start(dst[:].rearrange("p c n -> p (c n)"), src).then_inc(s_wmoe, 16)
            load(1)
            sp.wait_ge(s_value_ev, NP_)
            sp.dma_start(w1_flat, w1).then_inc(s_wmoe, 16)
            load(2)
            with sp.Fori(2, T - 1) as n:
                load(n + 1)
                store(n - 2)
            store(T - 3)
            store(T - 2)
            store(T - 1)
            sp.wait_ge(s_store, 16 * T)

        @block.tensor
        def _(pe):
            mm = nc.tensor.matmul
            pe.wait_ge(s_wquery, 32)
            for hh in range(H):
                ins = mm(ps[0:QC, hh // 8, (hh % 8) * KVC:(hh % 8 + 1) * KVC], wuqT_st[:, hh, :], wukT_st[:, hh, :],
                         start=True, stop=True)
                if hh % 8 == 7:
                    ins.then_inc(s_setup, 1)
            pe.wait_ge(s_wsetup, 16 * 5)
            for c in range(DC):
                ins = mm(ps[:, 2, c * R:(c + 1) * R], wkvcT_sb[:, c * P:(c + 1) * P], wkr_sb[:], start=True, stop=True)
            ins.then_inc(s_setup, 1)
            pe.wait_ge(s_setup_ev, 3)
            pe.wait_ge(s_setup_misc, 2)
            pe.wait_ge(s_const, 48)
            pe.wait_ge(seg_step, 2)
            mm(ps_t[0:1, 0:1], seg_out[:, 1:2], const("one"), start=True, stop=True).then_inc(flag_sum, 1)
            flag = read_flag(pe)

            def wide(t):
                with pe.If(flag > 0):
                    reuse(pe, x2_ready, t)
                    pe.wait_ge(o_copied, t * NB + NB)
                    stand_alone(pe)
                    for b in range(NB):
                        u = t * NB + b
                        with pe.Fori(0, NKC) as c:
                            pe.wait_ge(w_loaded, u * NKC * 32 + c * 32 + 32)
                            for d in range(DC):
                                ins = mm(ps[:, 0, 0:P], wide_ctx[:, d, :], wk_sb[:, d, :], start=(d == 0),
                                         stop=(d == DC - 1))
                            ins.then_inc(w_kdone, 1)
                            pe.wait_ge(w_krot, u * NKC + c + 1)
                            nc.tensor.transpose(ps[:, 1, 0:P], wide_stage, ident).then_inc(w_kturn, 1)
                        pe.wait_ge(w_kT, u * NKC * 2 + NKC * 2)
                        stand_alone(pe)
                        with pe.Fori(0, NP_) as j:
                            pe.wait_ge(w_q, u * NP_ + j + 1)
                            for q in range(-(-ALL_KEYS // 512)):
                                n = min(512, ALL_KEYS - q * 512)
                                ins = mm(ps[:, q, 0:n], wide_q, wide_kT[:, q * 512:q * 512 + n],
                                         start=True, stop=True)
                            ins.then_inc(w_score, 1)
                            pe.wait_ge(w_prob, u * NP_ + j + 1)
                            for c in range(NKC):
                                n = KEYS if c < NKC - 1 else LAST
                                ins = nc.tensor.transpose(ps[0:n, c // 4, c % 4 * P:(c % 4 + 1) * P],
                                                          wide_p[:, c * KEYS:c * KEYS + n], ident)
                            ins.then_inc(w_pturn, 1)
                            pe.wait_ge(w_pT, u * NP_ * 2 + j * 2 + 2)
                            stand_alone(pe)
                            for e in range(2):
                                for c in range(NKC):
                                    n = KEYS if c < NKC - 1 else LAST
                                    ins = mm(ps[e * KVC:(e + 1) * KVC, 0, 0:L], wide_k[0:n, c, 0:KVC],
                                             wide_pT[0:n, c, e * L:(e + 1) * L], start=(c == 0), stop=(c == NKC - 1))
                            ins.then_inc(w_pv, 1)
                            pe.wait_ge(w_attn, u * NP_ + j + 1)
                            stand_alone(pe)

            def transpose_in(k, t, bank):
                pe.wait_ge(ln_out[k], t + 1)
                for c in range(DC):
                    ins = nc.tensor.transpose(bank[:, c * P:(c + 1) * P], xn[:, k, c * P:(c + 1) * P], ident)
                ins.then_inc(ln_tr[k], 1)

            def kv(t):
                reuse(pe, x1_ready, t)
                pe.wait_ge(s_ctx, (t + 1) * 16)
                for b in range(NB):
                    for c in range(DC):
                        ins = mm(ps[:, 0, b * P:(b + 1) * P], ctx_sb[:, b, c, :], wk_sb[:, c, :],
                                 start=(c == 0), stop=(c == DC - 1))
                ins.then_inc(kv_done, 1)
                transpose_in(0, t, ps[:, 0, D:])

            def qc(t):
                pe.wait_ge(ln_T[0], t + 1)
                for c in range(DC):
                    ins = mm(ps[0:QC, 1, 0:P], wdq_sb[:, c, :], xnT[:, 0, c, :], start=(c == 0), stop=(c == DC - 1))
                ins.then_inc(qc_done, 1)

            def kt(t):
                pe.wait_ge(k_rot, t + 1)
                for b in range(NB):
                    ins = nc.tensor.transpose(ps[:, 0, b * P:(b + 1) * P], k_sb[:, b, :], ident)
                ins.then_inc(kt_done, 1)

            def q_up(pair):
                def run(t):
                    for n in (2 * pair, 2 * pair + 1):
                        if n == 0:
                            pe.wait_ge(qc_copied, t + 1)
                        elif n == 1:
                            pe.wait_ge(kt_copied, t + 1)
                        else:
                            pe.wait_ge(q_parts, t * 12 + 3 * (n - 1))
                        for hh in range(HG):
                            ins = mm(ps[:, 1 - n % 2, hh * P:(hh + 1) * P], wq_sb[:, HG * n + hh, :], qcT[:],
                                     start=True, stop=True)
                        ins.then_inc(qup_done, 1)
                return run

            def value_products(half):
                pe.wait_ge(s_wvalue, 32)
                for j in range(half * VB, (half + 1) * VB):
                    if half:
                        pe.wait_ge(s_value_ev, j - VB + 1)
                    for e in range(2):
                        ins = mm(value_banks[j % VB][e * KVC:(e + 1) * KVC, 0:D], wuvT_st[:, 2 * j + e, :],
                                 wo_st[:, 2 * j + e, :], start=True, stop=True)
                    ins.then_inc(s_value, 1)

            def score(b):
                def run(t):
                    if b == 0:
                        pe.wait_ge(q_parts, t * 12 + 12)
                        pe.wait_ge(q_rot, t * 4 + 4)
                    else:
                        pe.wait_ge(masked, t * NB + 1)
                    for j in range(NP_):
                        ins = mm(ps[:, j // 4, (j % 4) * KEYS:(j % 4 + 1) * KEYS], qT[:, b, 2 * j:2 * j + 2, :],
                                 kT[:, b, :], start=True, stop=True)
                    ins.then_inc(score_done, 1)
                    if isinstance(t, int) and t == 0:
                        value_products(b)
                return run

            def p_transpose(b):
                def run(t):
                    if b == 0:
                        pe.wait_ge(masked, t * NB + 2)
                    else:
                        pe.wait_ge(pt_copied, t * 4 + 2)
                    pe.wait_ge(prob_done, t * NB + b + 1)
                    for half in range(2):
                        for j in range(4):
                            ins = nc.tensor.transpose(ps[:, half, j * P:(j + 1) * P], probs[:, b, 4 * half + j, :],
                                                      ident)
                        ins.then_inc(pt_done, 1)
                return run

            def pv(t):
                pe.wait_ge(pt_copied, t * 4 + 4)
                for b in range(NB):
                    for e in range(2):
                        ins = mm(ps[e * KVC:(e + 1) * KVC, b, :], k_sb[:, b, 0:KVC], pT[:, b, e, :, :],
                                 start=True, stop=True)
                    ins.then_inc(pv_done, 1)

            def attn_out(t):
                if isinstance(t, int) and t == 0:
                    pe.wait_ge(s_value_ev, NP_)
                pe.wait_ge(o_copied, t * NB + NB)
                for j in range(NP_):
                    ins = mm(ps[:, 0, 0:D], oT[:, j, :, :], wvo_sb[:, j, :], start=(j == 0), stop=(j == NP_ - 1))
                ins.then_inc(ao_done, 1)

            def trb(t):
                reuse(pe, yt_copied, t)
                transpose_in(1, t, ps[:, 2, :])

            def bc(t):
                if isinstance(t, int) and t == 0:
                    pe.wait_ge(s_wscan, 48)
                pe.wait_ge(ln_T[1], t + 1)
                reuse(pe, x2_ready, t)
                for c in range(DC):
                    mm(ps[:, 3, 0:NH], xnT[:, 1, c, :], win_sb[:, c, 2 * DI + 2 * NS:2 * DI + 2 * NS + NH],
                       start=(c == 0), stop=(c == DC - 1))
                for m in range(2):
                    at = 2 * DI + m * NS
                    for c in range(DC):
                        ins = mm(ps[0:NS, 3, (m + 1) * P:(m + 2) * P], win_sb[:, c, at:at + NS], xnT[:, 1, c, :],
                                 start=(c == 0), stop=(c == DC - 1))
                ins.then_inc(bc_done, 1)

            def xp(t):
                for m in range(XC):
                    for c in range(DC):
                        ins = mm(ps[:, 2, m * P:(m + 1) * P], win_sb[:, c, DI + m * P:DI + (m + 1) * P],
                                 xnT[:, 1, c, :], start=(c == 0), stop=(c == DC - 1))
                ins.then_inc(xpart_done, 1)

            def z(t):
                pe.wait_ge(dt_raw, t + 1)
                for c in range(DC):
                    ins = mm(ps[:, 3, :], xnT[:, 1, c, :], win_sb[:, c, 0:DI], start=(c == 0), stop=(c == DC - 1))
                ins.then_inc(z_done, 1)

            def decay_(t):
                pe.wait_ge(pad_copied, t * 2 + 2)
                pe.wait_ge(decay_in_done, t + 1)
                mm(ps[:, 2, :], const("later"), decay_in[:], start=True, stop=True).then_inc(decay_sum, 1)

            def xh_(t):
                pe.wait_ge(zsilu_done, t + 1)
                pe.wait_ge(xbc_done, t * 2 + 2)
                for c in range(XC):
                    ins = nc.tensor.transpose(ps[:, 3, c * P:(c + 1) * P], xbc[:, c, :], ident)
                ins.then_inc(xh_tr, 1)
                pe.wait_ge(decay_exp, t + 1)
                for b in range(NB):
                    own = slice(b * L, (b + 1) * L)
                    if b == 0:
                        stand_alone(pe)
                    ins = mm(ps[own, 2, 0:L], xbc[0:NS, XC, own], xbc[0:NS, XC + 1, own], start=True, stop=True)
                ins.then_inc(gram_done, 1)

            def scan_(t):
                pe.wait_ge(scanw_done, t + 1)
                pe.wait_ge(xhdt_done, t + 1)
                stand_alone(pe)
                for b in range(NB):
                    own = slice(b * L, (b + 1) * L)
                    for hh in range(NH):
                        ins = mm(ps[own, 3, hh * PH:(hh + 1) * PH], scan_w[own, hh, :], xh_dt[own, hh, :],
                                 start=True, stop=True)
                ins.then_inc(y_done, 1)

            def scanT(t):
                pe.wait_ge(yg_done, t + 1)
                for c in range(XC):
                    ins = nc.tensor.transpose(ps[:, 2, c * P:(c + 1) * P], y_gated[:, c * P:(c + 1) * P], ident)
                ins.then_inc(yt_done, 1)

            def scan_out(t):
                if isinstance(t, int) and t == 0:
                    pe.wait_ge(s_wout, XC)
                pe.wait_ge(yt_copied, t + 1)
                for c in range(XC):
                    ins = mm(ps[:, 3, 0:D], yT[:, c, :], wout_sb[:, c, :], start=(c == 0), stop=(c == XC - 1))
                ins.then_inc(so_done, 1)

            def trm(t):
                if isinstance(t, int) and t == 0:
                    pe.wait_ge(s_wmoe, 48)
                reuse(pe, ht_copied, t * G)
                transpose_in(2, t, ps_t)

            def lg(t):
                pe.wait_ge(ln_T[2], t + 1)
                reuse(pe, gu_prod, t * G)
                for c in range(DC):
                    ins = mm(ps_g[:, 0:E], xnT[:, 2, c, :], wg_sb[:, c, :], start=(c == 0), stop=(c == DC - 1))
                ins.then_inc(lg_done, 1)

            def gate_up(g):
                def run(t):
                    if g == 0:
                        pe.wait_ge(lg_copied, t + 1)
                    elif not attention_over(t):
                        pe.wait_ge(gu_prod, t * G + g)
                    elif g == 1:
                        pe.wait_ge(x1_ready, T)
                        pe.wait_ge(gu_prod, t * G)
                    else:
                        pe.wait_ge(gu_prod, t * G + g - 1)
                    for w, bank in zip((w1_sb, v1_sb), gate_up_banks(t, g)):
                        for c in range(DC):
                            ins = mm(bank[:, 0:GW], xnT[:, 2, c, :], w[:, c, g * GW:(g + 1) * GW],
                                     start=(c == 0), stop=(c == DC - 1))
                    ins.then_inc(gu_done, 1)
                return run

            def h_transpose(g):
                def run(t):
                    if g == 0:
                        pe.wait_ge(ln_T[2], t + 1)
                    else:
                        pe.wait_ge(ht_copied, t * G + g)
                    pe.wait_ge(h_done, t * G + g + 1)
                    for c in range(GC):
                        ins = nc.tensor.transpose(ps_t[:, c * P:(c + 1) * P], h[:, g % 2, c * P:(c + 1) * P], ident)
                    ins.then_inc(ht_done, 1)
                return run

            def down(g):
                def run(t):
                    if g == 0:
                        reuse(pe, x3_ready, t)
                    pe.wait_ge(ht_copied, t * G + g + 1)
                    for c in range(GC):
                        ins = mm(ps_y[:, 0:D], hT[:, g % 2, c, :], w2_sb[:, g * GC + c, :],
                                 start=(g == 0 and c == 0), stop=(g == G - 1 and c == GC - 1))
                    ins.then_inc(down_done, 1)
                return run

            steps = {"wide": ("a", wide), "kv": ("a", kv), "qc": ("a", qc), "kt": ("a", kt), "pv": ("a", pv),
                     "ao": ("a", attn_out),
                     "trb": ("s", trb), "bc": ("s", bc), "xp": ("s", xp), "z": ("s", z), "decay": ("s", decay_),
                     "xh": ("s", xh_), "scan": ("s", scan_), "scanT": ("s", scanT), "so": ("s", scan_out),
                     "trm": ("m", trm), "lg": ("m", lg)}
            for i in range(2):
                steps |= {f"qup{i}": ("a", q_up(i)), f"sc{i}": ("a", score(i)),
                          f"pt{i}": ("a", p_transpose(i))}
            for g in range(G):
                steps |= {f"gu{g}": ("m", gate_up(g)), f"tr{g}": ("m", h_transpose(g)), f"dn{g}": ("m", down(g))}
            turns(pe, lambda n, a, s, m: run_order(steps, n, a, s, m))

        @block.scalar
        def _(act):
            fn = nc.scalar.activation
            act.wait_ge(s_const, 48)
            fn(a_neg[:], param("a_log"), ACT.Exp).then_inc(s_aexp, 1)
            flag = read_flag(act)

            def wide(t):
                with act.If(flag > 0):
                    reuse(act, x2_ready, t)
                    reuse(act, ysq_done, t)
                    act.wait_ge(o_copied, t * NB + NB)
                    act.wait_ge(pt_copied, t * 4 + 4)
                    for b in range(NB):
                        u = t * NB + b
                        if b > 0:
                            act.wait_ge(w_attn, u * NP_)
                        act.dma_start(wide_mask[:, 0:NKC * KEYS], key_row).then_inc(w_row, 16)
                        with act.Fori(0, NKC) as c:
                            act.dma_start(wide_ctx.rearrange("p c k -> p (c k)"),
                                          ctxT[bass.ds((t * NKC + c) * P, P), b * DC * KEYS:(b + 1) * DC * KEYS])\
                                .then_inc(w_loaded, 16)
                            act.dma_start(wide_table, key_tables[bass.ts(c, KEYS), :]).then_inc(w_loaded, 16)
                            act.wait_ge(w_kdone, u * NKC + c + 1)
                            fn(wide_stage[:, 0:KVC], ps[:, 0, 0:KVC], ACT.Copy).then_inc(w_klat, 1)
                            act.wait_ge(w_kturn, u * NKC + c + 1)
                            fn(wide_k[:, bass.ds(c, 1), 0:KVC], wide_stage[:, 0:KVC].unsqueeze(1), ACT.Copy)\
                                .then_inc(w_kT, 1)
                            fn(wide_kT[:, bass.ts(c, KEYS)], ps[:, 1, 0:P], ACT.Copy).then_inc(w_kT, 1)
                            act.wait_ge(w_kT, u * NKC * 2 + c * 2 + 2)
                            stand_alone(act)
                        with act.Fori(0, NP_) as j:
                            fn(wide_q.rearrange("p (e l) -> p e l", e=2), qT[:, b, bass.ds(2 * j, 2), :], ACT.Copy)\
                                .then_inc(w_q, 1)
                            act.wait_ge(w_max, u * NP_ + j + 1)
                            fn(wide_p[:, 0:ALL_KEYS], wide_p[:, 0:ALL_KEYS], ACT.Exp,
                               bias=wide_col[:, 0:1], accum_out=wide_col[:, 1:2]).then_inc(w_exp, 1)
                            act.wait_ge(w_pturn, u * NP_ + j + 1)
                            fn(wide_pT[:, 0:NKC - 1, :],
                               ps[:, 0:3, :].rearrange("p a (c q) -> p (a c) q", q=P), ACT.Copy).then_inc(w_pT, 1)
                            fn(wide_pT[0:LAST, NKC - 1, :], ps[0:LAST, 3, 0:P], ACT.Copy).then_inc(w_pT, 1)
                    act.wait_ge(w_attn, t * NB * NP_ + NB * NP_)
                    stand_alone(act)

            def copy_T(k, t, bank):
                act.wait_ge(ln_tr[k], t + 1)
                fn(xnT[:, k, :, :], bank[:, 0:D], ACT.Copy).then_inc(ln_T[k], 1)

            def kv(t):
                act.wait_ge(kv_done, t + 1)
                act.wait_ge(ln_tr[0], t + 1)
                fn(k_sb[:, :, 0:KVC], ps[:, 0, 0:NB * P].rearrange("p (b c) -> p b c", b=NB)[:, :, 0:KVC],
                   ACT.Copy).then_inc(k_lat, 1)
                copy_T(0, t, ps[:, 0, D:])

            def qc(t):
                act.wait_ge(qc_done, t + 1)
                fn(qcT[:], ps[0:QC, 1, 0:P], ACT.Copy).then_inc(qc_copied, 1)

            def kt(t):
                act.wait_ge(kt_done, t + 1)
                fn(kT[:], ps[:, 0, 0:NB * P].rearrange("p (b k) -> p b k", b=NB), ACT.Copy).then_inc(kt_copied, 1)

            def q_up(pair):
                def run(t):
                    for n in (2 * pair, 2 * pair + 1):
                        act.wait_ge(qup_done, t * 4 + n + 1)
                        reuse(act, score_done, t * NB)
                        fn(qT[0:KVC, :, HG * n:HG * n + HG, :].rearrange("p b h l -> p h b l"),
                           ps[0:KVC, 1 - n % 2, :].rearrange("p (h b l) -> p h b l", h=HG, b=NB), ACT.Copy,
                           scale=SCALE).then_inc(q_lat, 1)
                return run

            def score(b):
                def run(t):
                    act.wait_ge(max_done, t * NB + b + 1)
                    for j in range(NP_):
                        fn(probs[:, b, j, :], probs[:, b, j, :], ACT.Exp,
                           bias=neg_max[:, b, j:j + 1], accum_out=row_sum[:, b, j:j + 1]).then_inc(exp_done, 1)
                return run

            def p_transpose(b):
                def run(t):
                    for half in range(2):
                        act.wait_ge(pt_done, t * 4 + 2 * b + half + 1)
                        fn(pT[:, b, :, 4 * half:4 * half + 4, :].rearrange("p e j l -> p j e l"),
                           ps[:, half, :].rearrange("p (j e l) -> p j e l", j=4, e=2), ACT.Copy)\
                            .then_inc(pt_copied, 1)
                return run

            def trb(t):
                copy_T(1, t, ps[:, 2, :])

            def bc(t):
                act.wait_ge(bc_done, t + 1)
                reuse(act, conv_step, t * (TAPS - 1) * CH)
                fn(xpad[0:NS, XC:CH, :, TAPS - 1:],
                   ps[0:NS, 3, P:3 * P].rearrange("p (c b l) -> p c b l", c=2, b=NB), ACT.Copy).then_inc(pad_copied, 1)

            def xp(t):
                act.wait_ge(xpart_done, t + 1)
                fn(xpad[:, 0:XC, :, TAPS - 1:], ps[:, 2, :].rearrange("p (c b l) -> p c b l", c=XC, b=NB),
                   ACT.Copy).then_inc(pad_copied, 1)
                act.wait_ge(dt_abs, t + 1)
                fn(dt8[:, 2, :], dt8[:, 1, :], ACT.Exp, scale=-1.0).then_inc(dt_exp, 1)

            def first_tap(t):
                cw = param("conv_w").rearrange("p (c k) -> p c k", c=CH)
                act.wait_ge(pad_copied, t * 2 + 2)
                reuse(act, xbc_done, t * 2)
                for c in range(CH):
                    rows = slice(0, P if c < XC else NS)
                    fn(conv[rows, c], xpad[rows, c, :, 0:L], ACT.Identity, bias=param("conv_b")[rows, c:c + 1],
                       scale=cw[rows, c, 0:1]).then_inc(conv_first, 1)

            def z(t):
                act.wait_ge(z_done, t + 1)
                reuse(act, yg_done, t)
                fn(z_th[:], ps[:, 3, :], ACT.Tanh, scale=0.5).then_inc(zth_done, 1)

            def decay_(t):
                act.wait_ge(decay_sum, t + 1)
                reuse(act, y_done, t)
                fn(decay[:].rearrange("p h l -> p (h l)"), ps[:, 2, :], ACT.Exp).then_inc(decay_exp, 1)

            def cth(t):
                act.wait_ge(conv_step, t * (TAPS - 1) * CH + (TAPS - 1) * CH)
                reuse(act, xh_tr, t)
                reuse(act, gram_done, t)
                fn(conv_th[:, 0:XC], conv[:, 0:XC], ACT.Tanh, scale=0.5).then_inc(cth_done, 1)
                fn(conv_th[0:NS, XC:CH], conv[0:NS, XC:CH], ACT.Tanh, scale=0.5).then_inc(cth_done, 1)

            def xh_(t):
                act.wait_ge(xh_tr, t + 1)
                reuse(act, xhd_done, t)
                fn(xh[:], ps[:, 3, :], ACT.Copy).then_inc(xh_copied, 1)

            def scanT(t):
                act.wait_ge(yt_done, t + 1)
                fn(yT[:].rearrange("p c t -> p (c t)"), ps[:, 2, :], ACT.Copy).then_inc(yt_copied, 1)
                reuse(act, yve_done, t)
                fn(xh_d[:], y_gated[:], ACT.Square, scale=0.5, accum_out=y_ms[:]).then_inc(ysq_done, 1)

            def trm(t):
                copy_T(2, t, ps_t)

            def lg(t):
                act.wait_ge(e_neg, t + 1)
                fn(e_exp[:], logits[:], ACT.Exp, bias=neg_top[:]).then_inc(e_exp_done, 1)

            def gate_up(g):
                def run(t):
                    act.wait_ge(gu_done, t * G + g + 1)
                    reuse(act, gsilu_done, t * G + g - 1)
                    fn(g_th[:, g % 2, :], gate_up_banks(t, g)[0][:, 0:GW], ACT.Tanh, scale=0.5).then_inc(gth_done, 1)
                return run

            def h_transpose(g):
                def run(t):
                    act.wait_ge(ht_done, t * G + g + 1)
                    reuse(act, down_done, t * G + g - 1)
                    fn(hT[:, g % 2, :, :], ps_t[:, 0:GW], ACT.Copy).then_inc(ht_copied, 1)
                return run

            steps = {"wide": ("a", wide), "kv": ("a", kv), "qc": ("a", qc), "kt": ("a", kt),
                     "trb": ("s", trb), "conv0": ("s", first_tap), "bc": ("s", bc),
                     "xp": ("s", xp), "z": ("s", z), "decay": ("s", decay_), "cth": ("s", cth), "xh": ("s", xh_),
                     "scanT": ("s", scanT), "trm": ("m", trm), "lg": ("m", lg)}
            for i in range(2):
                steps |= {f"qup{i}": ("a", q_up(i)), f"sc{i}": ("a", score(i)),
                          f"pt{i}": ("a", p_transpose(i))}
            for g in range(G):
                steps |= {f"gu{g}": ("m", gate_up(g)), f"tr{g}": ("m", h_transpose(g))}
            turns(act, lambda n, a, s, m: run_order(steps, n, a, s, m))

        @block.gpsimd
        def _(pool):
            gp = nc.gpsimd
            gp.memset(xpad[:], 0.0).then_inc(s_pad, 1)
            pool.wait_ge(s_const, 48)

            def rsqrt(k, t, ready, done):
                pool.wait_ge(ready, t + 1)
                gp.tensor_tensor(rstd[:, k:k + 1], var_eps[:, k:k + 1], const("half"), ALU.pow).then_inc(done, 1)

            def ln1(t):
                rsqrt(0, t, ln_ve[0], ln_rstd[0])

            def ln2(t):
                rsqrt(1, t, ln_ve[1], ln_rstd[1])

            def ln3(t):
                rsqrt(2, t, ln_ve[2], ln_rstd[2])

            def keep(t):
                pool.wait_ge(x2_ready, t + 1)
                reuse(pool, x3_ready, t)
                stand_alone(pool)
                gp.tensor_copy(x2_res[:], x2[:]).then_inc(x2_kept, 1)

            def normalise(b):
                def run(t):
                    pool.wait_ge(inv_done, t * NB + b + 1)
                    gp.tensor_tensor(probs[:, b], probs[:, b],
                                     row_inv[:, b, :].unsqueeze(2).to_broadcast([P, NP_, KEYS]), ALU.mult)\
                        .then_inc(prob_done, 1)
                return run

            def z(t):
                pool.wait_ge(a_done, t + 1)
                reuse(pool, decay_sum, t)
                gp.tensor_tensor(decay_in[:], dt8[:, 9, :].unsqueeze(2).to_broadcast([P, NH, L]),
                                 const("upto").unsqueeze(1).to_broadcast([P, NH, L]), ALU.mult)\
                    .then_inc(decay_in_done, 1)

            def xh_(t):
                pool.wait_ge(xh_copied, t + 1)
                pool.wait_ge(dt_done, t + 1)
                reuse(pool, y_done, t)
                gp.tensor_tensor(xh_dt[:], xh[:].rearrange("p (h c) -> p h c", h=NH),
                                 dt8[:, 8, :].unsqueeze(2).to_broadcast([P, NH, PH]), ALU.mult).then_inc(xhdt_done, 1)
                reuse(pool, ysq_done, t)
                gp.tensor_tensor(xh_d[:], xh[:], param("d_skip"), ALU.mult).then_inc(xhd_done, 1)

            def scanT(t):
                rsqrt(3, t, yve_done, yr_done)

            def weigh(g):
                def run(t):
                    if g == 0:
                        pool.wait_ge(ew_done, t + 1)
                    pool.wait_ge(gu_prod, t * G + g + 1)
                    reuse(pool, ht_done, t * G + g - 1)
                    gp.tensor_tensor(h[:, g % 2, :].rearrange("p (e f) -> p e f", e=EG),
                                     gu[:, g % 2, :].rearrange("p (e f) -> p e f", e=EG),
                                     e_w[:, g * EG:(g + 1) * EG].unsqueeze(2).to_broadcast([P, EG, F]), ALU.mult)\
                        .then_inc(h_done, 1)
                return run

            steps = {"kv": ("m", keep), "ln1": ("next", ln1), "ln2": ("a", ln2), "ln3": ("s", ln3), "z": ("s", z),
                     "xh": ("s", xh_), "scanT": ("s", scanT)}
            for i in range(2):
                steps[f"rc{i}"] = ("a", normalise(i))
            for g in range(G):
                steps[f"gu{g}"] = ("m", weigh(g))
            ln1(0)
            turns(pool, lambda n, a, s, m: run_order(steps, n, a, s, m))

        @block.vector
        def _(dve):
            v = nc.vector
            dve.wait_ge(s_const, 48)
            v.tensor_copy(seg_f[:], seg_i[:]).then_inc(s_setup_misc, 1)
            seg_abs = mask[:, 0, 0:T * NB]
            dve.wait_ge(s_setup_misc, 1)
            v.tensor_scalar(seg_abs, seg_f[:], -(KEYS - 1) / 2.0, None, ALU.add).then_inc(seg_fold, 1)
            dve.wait_ge(seg_fold, 1)
            v.scalar_tensor_tensor(seg_abs, seg_abs, -1.0, seg_abs, ALU.mult, ALU.max).then_inc(seg_fold, 1)
            dve.wait_ge(seg_fold, 2)
            v.tensor_reduce(seg_out[:, 0:1], seg_abs, AX_X, ALU.max).then_inc(seg_step, 1)
            dve.wait_ge(seg_step, 1)
            v.tensor_scalar(seg_out[:, 1:2], seg_out[:, 0:1], KEYS / 2.0, None, ALU.is_gt).then_inc(seg_step, 1)
            v.tensor_scalar(param("d_skip"), param("d_skip"), 0.5, None, ALU.mult).then_inc(s_setup_misc, 1)
            dve.wait_ge(s_aexp, 1)
            v.tensor_scalar(a_neg[:], a_neg[:], 1e30, -1.0, ALU.min, ALU.mult).then_inc(s_setup_misc, 1)
            for n in range(2):
                dve.wait_ge(s_setup, n + 1)
                v.tensor_copy(wq_sb[:, 8 * n:8 * n + 8, 0:KVC],
                              ps[0:QC, n, :].rearrange("p (h c) -> p h c", h=8)).then_inc(s_setup_ev, 1)
            dve.wait_ge(s_setup, 3)
            v.tensor_copy(wk_sb[:, :, KVC:KVC + R], ps[:, 2, 0:DC * R].rearrange("p (c r) -> p c r", c=DC))\
                .then_inc(s_setup_ev, 1)
            dve.wait_ge(s_setup_ev, 3)
            dve.wait_ge(s_setup_misc, 3)
            dve.wait_ge(s_pad, 1)
            dve.wait_ge(flag_sum, 1)
            v.tensor_copy(wide_flag[:], ps_t[0:1, 0:1]).then_inc(flag_ready, 1)
            flag = read_flag(dve)

            def wide(t):
                with dve.If(flag > 0):
                    half = R // 2
                    for b in range(NB):
                        u = t * NB + b
                        own_mask = wide_mask[:, 0:ALL_KEYS]
                        dve.wait_ge(w_row, u * 16 + 16)
                        v.tensor_scalar(own_mask, own_mask, seg_f[:, bass.ds(u, 1)], None, ALU.subtract)\
                            .then_inc(w_mask, 1)
                        dve.wait_ge(w_mask, u * 3 + 1)
                        v.scalar_tensor_tensor(own_mask, own_mask, -1.0, own_mask, ALU.mult, ALU.max)\
                            .then_inc(w_mask, 1)
                        dve.wait_ge(w_mask, u * 3 + 2)
                        v.tensor_scalar(own_mask, own_mask, LOOKBACK / 2.0, NEG, ALU.is_gt, ALU.mult)\
                            .then_inc(w_mask, 1)
                        with dve.Fori(0, NKC) as c:
                            dve.wait_ge(w_klat, u * NKC + c + 1)
                            v.tensor_tensor(wide_cos, ps[:, 0, KVC:KVC + R], wide_table[:, 0:R], ALU.mult)\
                                .then_inc(w_kpart, 1)
                            for i, k in ((0, 1), (1, 0)):
                                v.tensor_tensor(wide_sin[:, i * half:(i + 1) * half],
                                                ps[:, 0, KVC + k * half:KVC + (k + 1) * half],
                                                wide_table[:, R + i * half:R + (i + 1) * half], ALU.mult)\
                                    .then_inc(w_kpart, 1)
                            dve.wait_ge(w_kpart, u * NKC * 3 + c * 3 + 3)
                            v.tensor_tensor(wide_stage[:, KVC:KVC + R], wide_cos, wide_sin, ALU.add)\
                                .then_inc(w_krot, 1)
                        with dve.Fori(0, NP_) as j:
                            dve.wait_ge(w_score, u * NP_ + j + 1)
                            dve.wait_ge(w_mask, u * 3 + 3)
                            v.tensor_tensor(wide_p[:, 0:ALL_KEYS], ps[:].rearrange("p a n -> p (a n)")[:, 0:ALL_KEYS],
                                            own_mask, ALU.add).then_inc(w_masked, 1)
                            dve.wait_ge(w_masked, u * NP_ + j + 1)
                            v.tensor_reduce(wide_col[:, 0:1], wide_p[:, 0:ALL_KEYS], AX_X, ALU.max, negate=True)\
                                .then_inc(w_max, 1)
                            dve.wait_ge(w_exp, u * NP_ + j + 1)
                            v.reciprocal(wide_col[:, 2:3], wide_col[:, 1:2]).then_inc(w_inv, 1)
                            dve.wait_ge(w_inv, u * NP_ + j + 1)
                            v.tensor_scalar(wide_p[:, 0:ALL_KEYS], wide_p[:, 0:ALL_KEYS], wide_col[:, 2:3], None,
                                            ALU.mult).then_inc(w_prob, 1)
                            dve.wait_ge(w_pv, u * NP_ + j + 1)
                            v.tensor_copy(oT[:, bass.ds(j, 1), b, :], ps[:, 0, 0:L].unsqueeze(1)).then_inc(w_attn, 1)

            def norm(k, src, t):
                v.bn_stats(stats[:, k, :], src[:]).then_inc(ln_stat[k], 1)
                dve.wait_ge(ln_stat[k], t + 1)
                stand_alone(dve)
                v.bn_aggr(mean_var[:, k, :], stats[:, k, :]).then_inc(ln_mv[k], 1)
                dve.wait_ge(ln_mv[k], t + 1)
                v.tensor_scalar(var_eps[:, k:k + 1], mean_var[:, k, 1:2], LN_EPS, None, ALU.add).then_inc(ln_ve[k], 1)
                dve.wait_ge(ln_rstd[k], t + 1)
                reuse(dve, ln_tr[k], t)
                v.tensor_scalar(xn[:, k, :], src[:], mean_var[:, k, 0:1], rstd[:, k:k + 1], ALU.subtract, ALU.mult)\
                    .then_inc(ln_out[k], 1)

            def kv(t):
                v.tensor_tensor(mask[:], const("key_no").unsqueeze(1).to_broadcast([P, NB, KEYS]),
                                seg_f[:, bass.ds(t * NB, NB)].unsqueeze(2).to_broadcast([P, NB, KEYS]),
                                ALU.subtract).then_inc(mask_step, 1)
                dve.wait_ge(mask_step, t * 2 + 1)
                v.scalar_tensor_tensor(mask[:], mask[:], -1.0, mask[:], ALU.mult, ALU.max).then_inc(mask_step, 1)
                dve.wait_ge(mask_step, t * 2 + 2)
                v.tensor_scalar(mask[:], mask[:], LOOKBACK / 2.0, NEG, ALU.is_gt, ALU.mult).then_inc(mask_done, 1)

            def rotate_keys(t):
                dve.wait_ge(ln_T[0], t + 1)
                src = ps[:, 0, 0:NB * P].rearrange("p (b c) -> p b c", b=NB)
                half = R // 2
                v.tensor_tensor(k_cos[:], src[:, :, KVC:KVC + R], const("cos_k").unsqueeze(1).to_broadcast([P, NB, R]),
                                ALU.mult).then_inc(k_rot_parts, 1)
                for i, j in ((0, 1), (1, 0)):
                    v.tensor_tensor(k_sin[:, :, i * half:(i + 1) * half],
                                    src[:, :, KVC + j * half:KVC + (j + 1) * half],
                                    const("sin_k")[:, i * half:(i + 1) * half].unsqueeze(1)
                                    .to_broadcast([P, NB, half]), ALU.mult).then_inc(k_rot_parts, 1)
                dve.wait_ge(k_rot_parts, t * 3 + 3)
                v.tensor_tensor(k_sb[:, :, KVC:KVC + R], k_cos[:], k_sin[:], ALU.add).then_inc(k_rot, 1)

            def ln1(t):
                dve.wait_ge(s_x, (t + 1) * 16)
                norm(0, x_in, t)

            def ln2(t):
                dve.wait_ge(x1_ready, t + 1)
                norm(1, x1, t)

            def ln3(t):
                dve.wait_ge(x2_ready, t + 1)
                norm(2, x2, t)

            def q_up(pair):
                def run(t):
                    half = R // 2
                    for n in (2 * pair, 2 * pair + 1):
                        dve.wait_ge(q_lat, t * 4 + n + 1)
                        reuse(dve, q_rot, t * 4 + n - 1)
                        bank = ps[:, 1 - n % 2, :].rearrange("p (g l) -> p g l", l=L)
                        for dst, to, at, rows, table in ((q_cos, KVC, KVC, R, "cos_qT"),
                                                         (q_sin, KVC, KVC + half, half, "sin_qT"),
                                                         (q_sin, KVC + half, KVC, half, "sin_qT")):
                            v.tensor_tensor(dst[to:to + rows, n % 2].rearrange("p (g l) -> p g l", l=L),
                                            bank[at:at + rows],
                                            const(table)[at:at + rows].unsqueeze(1).to_broadcast([rows, HG * NB, L]),
                                            ALU.mult).then_inc(q_parts, 1)
                        dve.wait_ge(q_parts, t * 12 + 3 * n + 3)
                        v.tensor_tensor(qT[KVC:, :, HG * n:HG * n + HG, :].rearrange("p b h l -> p h b l"),
                                        q_cos[KVC:, n % 2].rearrange("p (h b l) -> p h b l", h=HG, b=NB),
                                        q_sin[KVC:, n % 2].rearrange("p (h b l) -> p h b l", h=HG, b=NB),
                                        ALU.add).then_inc(q_rot, 1)
                return run

            def score(b):
                def run(t):
                    dve.wait_ge(score_done, t * NB + b + 1)
                    dve.wait_ge(mask_done, t + 1)
                    reuse(dve, pt_done, t * 4)
                    v.tensor_tensor(probs[:, b], ps[:, 0:2, :].rearrange("p n (j k) -> p (n j) k", j=4),
                                    mask[:, b, :].unsqueeze(1).to_broadcast([P, NP_, KEYS]), ALU.add)\
                        .then_inc(masked, 1)
                    dve.wait_ge(masked, t * NB + b + 1)
                    v.tensor_reduce(neg_max[:, b, :], probs[:, b], AX_X, ALU.max, negate=True).then_inc(max_done, 1)
                    if isinstance(t, int) and t == 0:
                        for j in range(b * VB, (b + 1) * VB):
                            dve.wait_ge(s_value, j + 1)
                            v.tensor_copy(wvo_sb[:, j, :], value_banks[j % VB][:, 0:D]).then_inc(s_value_ev, 1)
                return run

            def invert(b):
                def run(t):
                    dve.wait_ge(exp_done, t * 16 + 8 * b + 8)
                    reuse(dve, prob_done, t * NB + b - 1)
                    v.reciprocal(row_inv[:, b, :], row_sum[:, b, :]).then_inc(inv_done, 1)
                return run

            def pv(t):
                for b in range(NB):
                    dve.wait_ge(pv_done, t * NB + b + 1)
                    v.tensor_copy(oT[:, :, b, :], ps[:, b, :].rearrange("p (j l) -> p j l", j=NP_))\
                        .then_inc(o_copied, 1)

            def attn_out(t):
                dve.wait_ge(ao_done, t + 1)
                dve.wait_ge(s_xres, (t + 1) * 16)
                v.tensor_tensor(x1[:], ps[:, 0, 0:D], x_res[:], ALU.add).then_inc(x1_ready, 1)

            def softplus(t):
                if isinstance(t, int) and t == 0:
                    dve.wait_ge(s_wscan, 48)
                    for c in range(XC):
                        v.tensor_scalar(wout_sb[:, c, :], wout_sb[:, c, :], param("norm_w")[:, c:c + 1], 0.5,
                                        ALU.mult, ALU.mult).then_inc(s_wout, 1)
                raw, absv, u, den, s, q, poly, pos, dt, a = [dt8[:, i, :] for i in range(10)]
                dve.wait_ge(pad_copied, t * 2 + 1)
                reuse(dve, a_done, t)
                v.tensor_tensor(raw, ps[:, 3, 0:NH], param("dt_bias"), ALU.add).then_inc(dt_raw, 1)
                dve.wait_ge(dt_raw, t + 1)
                v.scalar_tensor_tensor(absv, raw, -1.0, raw, ALU.mult, ALU.max).then_inc(dt_abs, 1)

            def softplus_rest(t):
                raw, absv, u, den, s, q, poly, pos, dt, a = [dt8[:, i, :] for i in range(10)]
                chain = Steps(dve, dt_step, t, SOFT)
                chain.link(v.tensor_scalar(pos, raw, 0.0, None, ALU.max))
                dve.wait_ge(dt_exp, t + 1)
                chain.link(v.tensor_scalar(den, u, 2.0, None, ALU.add))
                chain.link(v.reciprocal(den, den))
                chain.link(v.tensor_tensor(s, u, den, ALU.mult))
                chain.link(v.tensor_tensor(q, s, s, ALU.mult))
                chain.link(v.tensor_scalar(poly, q, 1.0 / 15, None, ALU.mult))
                for k in (13, 11, 9, 7, 5):
                    chain.link(v.scalar_tensor_tensor(poly, poly, 1.0 / k, q, ALU.add, ALU.mult))
                chain.link(v.scalar_tensor_tensor(poly, poly, 1.0 / 3, q, ALU.add, ALU.mult))
                assert chain.k == SOFT

            def softplus_end(t):
                raw, absv, u, den, s, q, poly, pos, dt, a = [dt8[:, i, :] for i in range(10)]
                chain = Steps(dve, soft_end, t, 2)
                chain.link(v.scalar_tensor_tensor(poly, poly, 1.0, s, ALU.add, ALU.mult))
                chain.link(v.scalar_tensor_tensor(poly, poly, 2.0, pos, ALU.mult, ALU.add))
                reuse(dve, decay_in_done, t)
                v.tensor_tensor(a, poly, a_neg[:], ALU.mult).then_inc(a_done, 1)
                v.tensor_scalar(dt, poly, 0.5, None, ALU.mult).then_inc(dt_done, 1)

            def z(t):
                softplus_rest(t)
                softplus_end(t)
                dve.wait_ge(zth_done, t + 1)
                v.scalar_tensor_tensor(z_th[:], z_th[:], 1.0, ps[:, 3, :], ALU.add, ALU.mult).then_inc(zsilu_done, 1)

            def tap(k):
                def run(t):
                    cw = param("conv_w").rearrange("p (c k) -> p c k", c=CH)
                    for c in range(CH):
                        if k == 1:
                            dve.wait_ge(conv_first, t * CH + c + 1)
                        else:
                            dve.wait_ge(conv_step, t * (TAPS - 1) * CH + (k - 2) * CH + c + 1)
                        rows = slice(0, P if c < XC else NS)
                        v.scalar_tensor_tensor(conv[rows, c], xpad[rows, c, :, k:k + L], cw[rows, c, k:k + 1],
                                               conv[rows, c], ALU.mult, ALU.add).then_inc(conv_step, 1)
                return run

            def cth(t):
                for i, (rows, cs) in enumerate(((slice(0, P), slice(0, XC)), (slice(0, NS), slice(XC, CH)))):
                    dve.wait_ge(cth_done, t * 2 + i + 1)
                    v.scalar_tensor_tensor(xbc[rows, cs, :].rearrange("p c t -> p (c t)"),
                                           conv_th[rows, cs].rearrange("p c b l -> p (c b l)"), 1.0,
                                           conv[rows, cs].rearrange("p c b l -> p (c b l)"), ALU.add, ALU.mult)\
                        .then_inc(xbc_done, 1)

            def xh_(t):
                reuse(dve, y_done, t)
                dve.wait_ge(gram_done, t + 1)
                v.tensor_tensor(gram[:], ps[:, 2, 0:L], const("upto4"), ALU.mult).then_inc(gram_masked, 1)
                dve.wait_ge(gram_masked, t + 1)
                dve.wait_ge(decay_exp, t + 1)
                v.tensor_tensor(scan_w[:], decay[:], gram[:].unsqueeze(1).to_broadcast([P, NH, L]), ALU.mult)\
                    .then_inc(scanw_done, 1)

            def scan_(t):
                dve.wait_ge(y_done, t + 1)
                dve.wait_ge(xhd_done, t + 1)
                reuse(dve, yt_done, t)
                reuse(dve, ysq_done, t)
                v.tensor_tensor(y_sb[:], ps[:, 3, :], xh_d[:], ALU.add).then_inc(y_skip, 1)
                dve.wait_ge(y_skip, t + 1)
                dve.wait_ge(zsilu_done, t + 1)
                v.tensor_tensor(y_gated[:], y_sb[:], z_th[:], ALU.mult).then_inc(yg_done, 1)

            def scanT(t):
                dve.wait_ge(ysq_done, t + 1)
                v.tensor_scalar(var_eps[:, 3:4], y_ms[:], 1.0 / DI, LN_EPS, ALU.mult, ALU.add).then_inc(yve_done, 1)

            def scan_out(t):
                dve.wait_ge(yr_done, t + 1)
                dve.wait_ge(so_done, t + 1)
                reuse(dve, x2_kept, t)
                v.scalar_tensor_tensor(x2[:], ps[:, 3, 0:D], rstd[:, 3:4], x1[:], ALU.mult, ALU.add)\
                    .then_inc(x2_ready, 1)

            def lg(t):
                dve.wait_ge(lg_done, t + 1)
                v.tensor_copy(logits[:], ps_g[:, 0:E]).then_inc(lg_copied, 1)
                dve.wait_ge(lg_copied, t + 1)
                chain = Steps(dve, gate_step, t, GATE)
                stand_alone(dve)
                chain.link(v.max(top8[:], logits[:]))
                v.tensor_scalar(neg_top[:], top8[:, 0:1], -1.0, None, ALU.mult).then_inc(e_neg, 1)
                chain.link(v.match_replace(struck[:], top8[:], logits[:], -3e38))
                chain.link(v.tensor_tensor(chosen[:], struck[:], logits[:], ALU.not_equal))
                dve.wait_ge(e_exp_done, t + 1)
                chain.link(v.tensor_tensor(e_exp[:], e_exp[:], chosen[:], ALU.mult))
                chain.link(v.tensor_reduce(e_sum[:, 0:1], e_exp[:], AX_X, ALU.add))
                chain.link(v.reciprocal(e_sum[:, 1:2], e_sum[:, 0:1]))
                reuse(dve, h_done, t * G)
                chain.link(v.tensor_scalar(e_w[:], e_exp[:], e_sum[:, 1:2], 0.5, ALU.mult, ALU.mult))
                assert chain.k == GATE
                v.tensor_copy(e_w[:, 0:1], e_w[:, 0:1]).then_inc(ew_done, 1)

            def gate_up(g):
                def run(t):
                    dve.wait_ge(gth_done, t * G + g + 1)
                    reuse(dve, h_done, t * G + g - 1)
                    v.scalar_tensor_tensor(gu[:, g % 2, :], g_th[:, g % 2, :], 1.0, gate_up_banks(t, g)[0][:, 0:GW],
                                           ALU.add, ALU.mult)\
                        .then_inc(gsilu_done, 1)
                    dve.wait_ge(gsilu_done, t * G + g + 1)
                    v.tensor_tensor(gu[:, g % 2, :], gu[:, g % 2, :], gate_up_banks(t, g)[1][:, 0:GW], ALU.mult)\
                        .then_inc(gu_prod, 1)
                return run

            def moe_out(t):
                dve.wait_ge(down_done, t * G + G)
                dve.wait_ge(x2_kept, t + 1)
                reuse(dve, s_store, t * 16)
                v.tensor_tensor(x3[:], ps_y[:, 0:D], x2_res[:], ALU.add).then_inc(x3_ready, 1)

            def kv_all(t):
                kv(t)
                rotate_keys(t)

            steps = {"wide": ("a", wide), "kv": ("a", kv_all), "ln1": ("next", ln1), "ln2": ("a", ln2),
                     "ln3": ("s", ln3), "pv": ("a", pv),
                     "ao": ("a", attn_out), "bc": ("s", softplus), "z": ("s", z), "cth": ("s", cth), "xh": ("s", xh_),
                     "scan": ("s", scan_), "scanT": ("s", scanT), "so": ("s", scan_out), "lg": ("m", lg),
                     "moe_out": ("m", moe_out)}
            for i in range(2):
                steps |= {f"qup{i}": ("a", q_up(i)), f"sc{i}": ("a", score(i)), f"rc{i}": ("a", invert(i))}
            for k in range(1, TAPS):
                steps[f"conv{k}"] = ("s", tap(k))
            for g in range(G):
                steps[f"gu{g}"] = ("m", gate_up(g))
            ln1(0)
            turns(dve, lambda n, a, s, m: run_order(steps, n, a, s, m))


def kernel(x, ctx_2048, itok_BxS_0_1023, L0_xattn_W_kvc, L0_xattn_W_dq, L0_xattn_W_uq, L0_xattn_W_qr, L0_xattn_W_uk,
           L0_xattn_W_kr, L0_xattn_W_uv, L0_xattn_W_o, L0_attn_W_in, L0_attn_conv_w, L0_attn_conv_b, L0_attn_dt_bias,
           L0_attn_A_log, L0_attn_D, L0_attn_norm_w, L0_attn_W_out, L0_ffn_wg, L0_ffn_w1, L0_ffn_v1, L0_ffn_w2):
    import concourse.bacc as bacc
    from concourse.bass_utils import run_bass_kernel_spmd

    def a(v):
        return np.asarray(v)

    def chunks(w):
        w = a(w)
        return w.reshape(-1, P, w.shape[1]).transpose(1, 0, 2)

    pc, pwidth = columns(PARAMS)
    par = np.zeros((P, pwidth), np.float32)
    par[:, slice(*pc["dt_bias"])] = a(L0_attn_dt_bias)[None]
    par[:, slice(*pc["a_log"])] = a(L0_attn_A_log)[None]
    par[:, slice(*pc["d_skip"])] = np.repeat(a(L0_attn_D), PH)[None]
    par[:, slice(*pc["norm_w"])] = a(L0_attn_norm_w).reshape(XC, P).T
    cw = np.zeros((P, CH, TAPS), np.float32)
    cb = np.zeros((P, CH), np.float32)
    for c in range(CH):
        lo, n = (c * P, P) if c < XC else (DI + (c - XC) * NS, NS)
        cw[:n, c] = a(L0_attn_conv_w)[lo:lo + n]
        cb[:n, c] = a(L0_attn_conv_b)[lo:lo + n]
    par[:, slice(*pc["conv_w"])] = cw.reshape(P, -1)
    par[:, slice(*pc["conv_b"])] = cb
    ctxT = np.zeros((B, NKC * KEYS, D), np.float32)
    ctxT[:, :ALL_KEYS] = a(ctx_2048)
    ctxT = ctxT.reshape(T, NB, NKC, KEYS, DC, P).transpose(0, 2, 5, 1, 4, 3).reshape(T * NKC * P, NB * DC * KEYS)
    consts, key_tables, key_row = constants()
    arrays = {
        "xt": a(x).reshape(B * L, D), "ctxT": ctxT, "seg": np.tile(a(itok_BxS_0_1023).T, (2, 1)),
        "consts": consts, "key_tables": key_tables, "key_row": key_row,
        "params": par, "w_dq": chunks(L0_xattn_W_dq),
        "w_qr": a(L0_xattn_W_qr).reshape(QC, H, R), "w_uqT": a(L0_xattn_W_uq).reshape(QC, H, HD).transpose(2, 1, 0),
        "w_ukT": a(L0_xattn_W_uk).reshape(KVC, H, HD).transpose(2, 1, 0), "w_kvc": chunks(L0_xattn_W_kvc),
        "w_kvcT": a(L0_xattn_W_kvc).T, "w_kr": a(L0_xattn_W_kr),
        "w_uvT": a(L0_xattn_W_uv).reshape(KVC, H, HD).transpose(2, 1, 0),
        "w_o": a(L0_xattn_W_o).reshape(H, HD, D).transpose(1, 0, 2), "w_in": chunks(a(L0_attn_W_in).T),
        "w_out": chunks(a(L0_attn_W_out).T), "wg": chunks(a(L0_ffn_wg).T),
        "w1": chunks(a(L0_ffn_w1).transpose(1, 0, 2).reshape(D, E * F)).reshape(P, -1),
        "v1": chunks(a(L0_ffn_v1).transpose(1, 0, 2).reshape(D, E * F)).reshape(P, -1),
        "w2": chunks(a(L0_ffn_w2).reshape(E * F, D)).reshape(P, -1),
    }
    arrays = {k: np.ascontiguousarray(w) for k, w in arrays.items()}
    nc = bacc.Bacc("TRN2", target_bir_lowering=False, num_devices=1)
    args = {k: nc.dram_tensor(k, w.shape, mybir.dt.from_np(w.dtype), kind="ExternalInput").ap()
            for k, w in arrays.items()}
    out = nc.dram_tensor("out", (B * L, D), F32, kind="ExternalOutput").ap()
    build(nc, out=out, **args)
    r = run_bass_kernel_spmd(nc, [arrays], core_ids=[0])
    return np.asarray(r.results[0]["out"]).reshape(B, L, D)
```
